# Optimizing a Trainium2 kernel written in Bass

```python
import numpy as np
import jax
import jax.numpy as jnp

def _softmax(x, axis=-1):
    return jax.nn.softmax(x, axis=axis)

def _gelu(x):
    return jax.nn.gelu(x, approximate=True)

def _silu(x):
    return jax.nn.silu(x)

def _sigmoid(x):
    return jax.nn.sigmoid(x)

def _layernorm(x, axis=-1, eps=1e-05):
    m = jnp.mean(x, axis=axis, keepdims=True)
    v = jnp.var(x, axis=axis, keepdims=True)
    return (x - m) / jnp.sqrt(v + eps)

def _scatter_add(tgt, idx, src, axis=0):
    return tgt.at[idx].add(src)

def _segment_sum(src, seg, n):
    return jax.ops.segment_sum(src, seg, n)
kernel_name = 'mk_metaformer_d2_conv_nchw1024_r4_eab985'

def setup_inputs(seed: int=0):
    np.random.seed(seed)
    _w = jnp.asarray

    def _rec_inputs():
        import jax
        import jax.numpy as jnp
        _gk = jax.random.key(seed)
        x = -0.0006537 + 1.001 * jax.random.normal(jax.random.fold_in(_gk, 1), (4, 256, 24, 24), jnp.float32)
        return x
    x = _rec_inputs()

    def _L0_conv_setup():
        import jax, jax.numpy as jnp
        import numpy as np
        DIM = 256
        R = 2
        D_MODEL = DIM // (R * R)
        D_INNER = 2 * D_MODEL
        D_STATE = 16
        D_CONV = 4
        DT_RANK = (D_MODEL + 15) // 16
        NUM_TOKENS = 1

        def pixel_shuffle(x, r):
            B, C, H, W = x.shape
            c = C // (r * r)
            x = x.reshape(B, c, r, r, H, W)
            x = x.transpose(0, 1, 4, 2, 5, 3)
            return x.reshape(B, c, H * r, W * r)

        def pixel_unshuffle(x, r):
            B, C, Hr, Wr = x.shape
            H, W = (Hr // r, Wr // r)
            x = x.reshape(B, C, H, r, W, r)
            x = x.transpose(0, 1, 3, 5, 2, 4)
            return x.reshape(B, C * r * r, H, W)

        def mamba_block(seq, in_proj_w, conv_w, conv_b, x_proj_w, dt_proj_w, dt_proj_b, A_log, D, out_proj_w):
            B, L, _ = seq.shape
            xz = jnp.einsum('bld,ed->ble', seq, in_proj_w)
            u, z = jnp.split(xz, 2, axis=-1)
            up = jnp.pad(u, ((0, 0), (D_CONV - 1, 0), (0, 0)))
            u = sum((up[:, k:k + L, :] * conv_w[:, k] for k in range(D_CONV))) + conv_b
            u = jax.nn.silu(u)
            x_dbl = jnp.einsum('bld,ed->ble', u, x_proj_w)
            dt, Bm, Cm = jnp.split(x_dbl, [DT_RANK, DT_RANK + D_STATE], axis=-1)
            dt = jax.nn.softplus(jnp.einsum('blr,dr->bld', dt, dt_proj_w) + dt_proj_b)
            A = -jnp.exp(A_log)

            def step(h, inputs):
                dt_t, B_t, C_t, u_t = inputs
                dA = jnp.exp(dt_t[:, :, None] * A)
                h = dA * h + (dt_t * u_t)[:, :, None] * B_t[:, None, :]
                y = jnp.einsum('bdn,bn->bd', h, C_t)
                return (h, y)
            h0 = jnp.zeros((B, D_INNER, D_STATE), dtype=seq.dtype)
            xs = (dt.transpose(1, 0, 2), Bm.transpose(1, 0, 2), Cm.transpose(1, 0, 2), u.transpose(1, 0, 2))
            _, ys = jax.lax.scan(step, h0, xs)
            y = ys.transpose(1, 0, 2) + u * D
            y = y * jax.nn.silu(z)
            return jnp.einsum('bld,ed->ble', y, out_proj_w)
        key = jax.random.key(seed)
        ks = jax.random.split(key, 12)
        s = lambda k, shape, scale=0.02: jax.random.normal(k, shape, dtype=jnp.float32) * scale
        inp = {'x': jax.random.normal(ks[0], (4, DIM, 24, 24), dtype=jnp.float32), 'global_token': jnp.zeros((1, NUM_TOKENS, D_MODEL), dtype=jnp.float32), 'in_proj_w': s(ks[1], (2 * D_INNER, D_MODEL)), 'conv_w': s(ks[2], (D_INNER, D_CONV), 0.1), 'conv_b': jnp.zeros((D_INNER,), dtype=jnp.float32), 'x_proj_w': s(ks[3], (DT_RANK + 2 * D_STATE, D_INNER)), 'dt_proj_w': s(ks[4], (D_INNER, DT_RANK), 0.1), 'dt_proj_b': jax.random.uniform(ks[5], (D_INNER,), dtype=jnp.float32, minval=-4.0, maxval=-2.0), 'A_log': jnp.log(jnp.broadcast_to(jnp.arange(1, D_STATE + 1, dtype=jnp.float32), (D_INNER, D_STATE))), 'D': jnp.ones((D_INNER,), dtype=jnp.float32), 'out_proj_w': s(ks[6], (D_MODEL, D_INNER))}
        return inp
    _L0_conv_all = _L0_conv_setup()
    _L0_conv_in = {k: v for k, v in _L0_conv_all.items() if k in ('global_token', 'in_proj_w', 'conv_w', 'conv_b', 'x_proj_w', 'dt_proj_w', 'dt_proj_b', 'A_log', 'D', 'out_proj_w')}
    del _L0_conv_all

    def _L0_ffn_setup():
        import jax, jax.numpy as jnp
        import numpy as np
        N_EXPERTS = 8
        TOP_K = 2
        D_MODEL = 256
        D_FF = 512
        B, T = (4, 512)
        key = jax.random.key(seed)
        ks = jax.random.split(key, 8)
        s = 0.02
        return {'x': jax.random.normal(ks[0], (B, T, D_MODEL), jnp.float32), 'router_w': jax.random.normal(ks[1], (N_EXPERTS, D_MODEL), jnp.float32) * s, 'w_gate': jax.random.normal(ks[2], (N_EXPERTS, D_MODEL, D_FF), jnp.float32) * s, 'w_up': jax.random.normal(ks[3], (N_EXPERTS, D_MODEL, D_FF), jnp.float32) * s, 'w_down': jax.random.normal(ks[4], (N_EXPERTS, D_FF, D_MODEL), jnp.float32) * s, 'sg': jax.random.normal(ks[5], (D_MODEL, D_FF), jnp.float32) * s, 'su': jax.random.normal(ks[6], (D_MODEL, D_FF), jnp.float32) * s, 'sd': jax.random.normal(ks[7], (D_FF, D_MODEL), jnp.float32) * s}
    _L0_ffn_all = _L0_ffn_setup()
    _L0_ffn_in = {k: v for k, v in _L0_ffn_all.items() if k in ('router_w', 'w_gate', 'w_up', 'w_down', 'sg', 'su', 'sd')}
    del _L0_ffn_all

    def _L1_conv_setup():
        import jax, jax.numpy as jnp
        import numpy as np
        DIM = 256
        R = 2
        D_MODEL = DIM // (R * R)
        D_INNER = 2 * D_MODEL
        D_STATE = 16
        D_CONV = 4
        DT_RANK = (D_MODEL + 15) // 16
        NUM_TOKENS = 1

        def pixel_shuffle(x, r):
            B, C, H, W = x.shape
            c = C // (r * r)
            x = x.reshape(B, c, r, r, H, W)
            x = x.transpose(0, 1, 4, 2, 5, 3)
            return x.reshape(B, c, H * r, W * r)

        def pixel_unshuffle(x, r):
            B, C, Hr, Wr = x.shape
            H, W = (Hr // r, Wr // r)
            x = x.reshape(B, C, H, r, W, r)
            x = x.transpose(0, 1, 3, 5, 2, 4)
            return x.reshape(B, C * r * r, H, W)

        def mamba_block(seq, in_proj_w, conv_w, conv_b, x_proj_w, dt_proj_w, dt_proj_b, A_log, D, out_proj_w):
            B, L, _ = seq.shape
            xz = jnp.einsum('bld,ed->ble', seq, in_proj_w)
            u, z = jnp.split(xz, 2, axis=-1)
            up = jnp.pad(u, ((0, 0), (D_CONV - 1, 0), (0, 0)))
            u = sum((up[:, k:k + L, :] * conv_w[:, k] for k in range(D_CONV))) + conv_b
            u = jax.nn.silu(u)
            x_dbl = jnp.einsum('bld,ed->ble', u, x_proj_w)
            dt, Bm, Cm = jnp.split(x_dbl, [DT_RANK, DT_RANK + D_STATE], axis=-1)
            dt = jax.nn.softplus(jnp.einsum('blr,dr->bld', dt, dt_proj_w) + dt_proj_b)
            A = -jnp.exp(A_log)

            def step(h, inputs):
                dt_t, B_t, C_t, u_t = inputs
                dA = jnp.exp(dt_t[:, :, None] * A)
                h = dA * h + (dt_t * u_t)[:, :, None] * B_t[:, None, :]
                y = jnp.einsum('bdn,bn->bd', h, C_t)
                return (h, y)
            h0 = jnp.zeros((B, D_INNER, D_STATE), dtype=seq.dtype)
            xs = (dt.transpose(1, 0, 2), Bm.transpose(1, 0, 2), Cm.transpose(1, 0, 2), u.transpose(1, 0, 2))
            _, ys = jax.lax.scan(step, h0, xs)
            y = ys.transpose(1, 0, 2) + u * D
            y = y * jax.nn.silu(z)
            return jnp.einsum('bld,ed->ble', y, out_proj_w)
        key = jax.random.key(seed)
        ks = jax.random.split(key, 12)
        s = lambda k, shape, scale=0.02: jax.random.normal(k, shape, dtype=jnp.float32) * scale
        inp = {'x': jax.random.normal(ks[0], (4, DIM, 24, 24), dtype=jnp.float32), 'global_token': jnp.zeros((1, NUM_TOKENS, D_MODEL), dtype=jnp.float32), 'in_proj_w': s(ks[1], (2 * D_INNER, D_MODEL)), 'conv_w': s(ks[2], (D_INNER, D_CONV), 0.1), 'conv_b': jnp.zeros((D_INNER,), dtype=jnp.float32), 'x_proj_w': s(ks[3], (DT_RANK + 2 * D_STATE, D_INNER)), 'dt_proj_w': s(ks[4], (D_INNER, DT_RANK), 0.1), 'dt_proj_b': jax.random.uniform(ks[5], (D_INNER,), dtype=jnp.float32, minval=-4.0, maxval=-2.0), 'A_log': jnp.log(jnp.broadcast_to(jnp.arange(1, D_STATE + 1, dtype=jnp.float32), (D_INNER, D_STATE))), 'D': jnp.ones((D_INNER,), dtype=jnp.float32), 'out_proj_w': s(ks[6], (D_MODEL, D_INNER))}
        return inp
    _L1_conv_all = _L1_conv_setup()
    _L1_conv_in = {k: v for k, v in _L1_conv_all.items() if k in ('global_token', 'in_proj_w', 'conv_w', 'conv_b', 'x_proj_w', 'dt_proj_w', 'dt_proj_b', 'A_log', 'D', 'out_proj_w')}
    del _L1_conv_all

    def _L1_ffn_setup():
        import math
        import jax, jax.numpy as jnp
        import numpy as np
        NUM_EXPERTS = 8
        CAPACITY_FACTOR = 1.5
        key = jax.random.key(seed)
        ks = jax.random.split(key, 4)
        B, T, D, F, E = (4, 512, 256, 1024, NUM_EXPERTS)
        scale = 0.02
        return {'x': jax.random.normal(ks[0], (B, T, D), dtype=jnp.float32), 'router_w': jax.random.normal(ks[1], (E, D), dtype=jnp.float32) * scale, 'w1': jax.random.normal(ks[2], (E, D, F), dtype=jnp.float32) * scale, 'b1': jnp.zeros((E, F), dtype=jnp.float32), 'w2': jax.random.normal(ks[3], (E, F, D), dtype=jnp.float32) * scale, 'b2': jnp.zeros((E, D), dtype=jnp.float32)}
    _L1_ffn_all = _L1_ffn_setup()
    _L1_ffn_in = {k: v for k, v in _L1_ffn_all.items() if k in ('router_w', 'w1', 'b1', 'w2', 'b2')}
    del _L1_ffn_all
    return {'x': x, 'L0_conv_global_token': _L0_conv_in['global_token'], 'L0_conv_in_proj_w': _L0_conv_in['in_proj_w'], 'L0_conv_conv_w': _L0_conv_in['conv_w'], 'L0_conv_conv_b': _L0_conv_in['conv_b'], 'L0_conv_x_proj_w': _L0_conv_in['x_proj_w'], 'L0_conv_dt_proj_w': _L0_conv_in['dt_proj_w'], 'L0_conv_dt_proj_b': _L0_conv_in['dt_proj_b'], 'L0_conv_A_log': _L0_conv_in['A_log'], 'L0_conv_D': _L0_conv_in['D'], 'L0_conv_out_proj_w': _L0_conv_in['out_proj_w'], 'L0_ffn_router_w': _L0_ffn_in['router_w'], 'L0_ffn_w_gate': _L0_ffn_in['w_gate'], 'L0_ffn_w_up': _L0_ffn_in['w_up'], 'L0_ffn_w_down': _L0_ffn_in['w_down'], 'L0_ffn_sg': _L0_ffn_in['sg'], 'L0_ffn_su': _L0_ffn_in['su'], 'L0_ffn_sd': _L0_ffn_in['sd'], 'L1_conv_global_token': _L1_conv_in['global_token'], 'L1_conv_in_proj_w': _L1_conv_in['in_proj_w'], 'L1_conv_conv_w': _L1_conv_in['conv_w'], 'L1_conv_conv_b': _L1_conv_in['conv_b'], 'L1_conv_x_proj_w': _L1_conv_in['x_proj_w'], 'L1_conv_dt_proj_w': _L1_conv_in['dt_proj_w'], 'L1_conv_dt_proj_b': _L1_conv_in['dt_proj_b'], 'L1_conv_A_log': _L1_conv_in['A_log'], 'L1_conv_D': _L1_conv_in['D'], 'L1_conv_out_proj_w': _L1_conv_in['out_proj_w'], 'L1_ffn_router_w': _L1_ffn_in['router_w'], 'L1_ffn_w1': _L1_ffn_in['w1'], 'L1_ffn_b1': _L1_ffn_in['b1'], 'L1_ffn_w2': _L1_ffn_in['w2'], 'L1_ffn_b2': _L1_ffn_in['b2']}

def reference(x, L0_conv_global_token, L0_conv_in_proj_w, L0_conv_conv_w, L0_conv_conv_b, L0_conv_x_proj_w, L0_conv_dt_proj_w, L0_conv_dt_proj_b, L0_conv_A_log, L0_conv_D, L0_conv_out_proj_w, L0_ffn_router_w, L0_ffn_w_gate, L0_ffn_w_up, L0_ffn_w_down, L0_ffn_sg, L0_ffn_su, L0_ffn_sd, L1_conv_global_token, L1_conv_in_proj_w, L1_conv_conv_w, L1_conv_conv_b, L1_conv_x_proj_w, L1_conv_dt_proj_w, L1_conv_dt_proj_b, L1_conv_A_log, L1_conv_D, L1_conv_out_proj_w, L1_ffn_router_w, L1_ffn_w1, L1_ffn_b1, L1_ffn_w2, L1_ffn_b2):
    import jax
    import jax.numpy as jnp

    def _L0_conv_ref(x, global_token, in_proj_w, conv_w, conv_b, x_proj_w, dt_proj_w, dt_proj_b, A_log, D, out_proj_w):
        import jax, jax.numpy as jnp
        import numpy as np
        DIM = 256
        R = 2
        D_MODEL = DIM // (R * R)
        D_INNER = 2 * D_MODEL
        D_STATE = 16
        D_CONV = 4
        DT_RANK = (D_MODEL + 15) // 16
        NUM_TOKENS = 1

        def pixel_shuffle(x, r):
            B, C, H, W = x.shape
            c = C // (r * r)
            x = x.reshape(B, c, r, r, H, W)
            x = x.transpose(0, 1, 4, 2, 5, 3)
            return x.reshape(B, c, H * r, W * r)

        def pixel_unshuffle(x, r):
            B, C, Hr, Wr = x.shape
            H, W = (Hr // r, Wr // r)
            x = x.reshape(B, C, H, r, W, r)
            x = x.transpose(0, 1, 3, 5, 2, 4)
            return x.reshape(B, C * r * r, H, W)

        def mamba_block(seq, in_proj_w, conv_w, conv_b, x_proj_w, dt_proj_w, dt_proj_b, A_log, D, out_proj_w):
            B, L, _ = seq.shape
            xz = jnp.einsum('bld,ed->ble', seq, in_proj_w)
            u, z = jnp.split(xz, 2, axis=-1)
            up = jnp.pad(u, ((0, 0), (D_CONV - 1, 0), (0, 0)))
            u = sum((up[:, k:k + L, :] * conv_w[:, k] for k in range(D_CONV))) + conv_b
            u = jax.nn.silu(u)
            x_dbl = jnp.einsum('bld,ed->ble', u, x_proj_w)
            dt, Bm, Cm = jnp.split(x_dbl, [DT_RANK, DT_RANK + D_STATE], axis=-1)
            dt = jax.nn.softplus(jnp.einsum('blr,dr->bld', dt, dt_proj_w) + dt_proj_b)
            A = -jnp.exp(A_log)

            def step(h, inputs):
                dt_t, B_t, C_t, u_t = inputs
                dA = jnp.exp(dt_t[:, :, None] * A)
                h = dA * h + (dt_t * u_t)[:, :, None] * B_t[:, None, :]
                y = jnp.einsum('bdn,bn->bd', h, C_t)
                return (h, y)
            h0 = jnp.zeros((B, D_INNER, D_STATE), dtype=seq.dtype)
            xs = (dt.transpose(1, 0, 2), Bm.transpose(1, 0, 2), Cm.transpose(1, 0, 2), u.transpose(1, 0, 2))
            _, ys = jax.lax.scan(step, h0, xs)
            y = ys.transpose(1, 0, 2) + u * D
            y = y * jax.nn.silu(z)
            return jnp.einsum('bld,ed->ble', y, out_proj_w)
        B, C, H, W = x.shape
        xs = pixel_shuffle(x, R)
        seq = xs.reshape(B, D_MODEL, -1).transpose(0, 2, 1)
        tok = jnp.broadcast_to(global_token, (B, NUM_TOKENS, D_MODEL))
        seq = jnp.concatenate([tok, seq], axis=1)
        seq = mamba_block(seq, in_proj_w, conv_w, conv_b, x_proj_w, dt_proj_w, dt_proj_b, A_log, D, out_proj_w)
        seq = seq[:, -H * W * R * R:, :]
        out = seq.reshape(B, H * R, W * R, D_MODEL).transpose(0, 3, 1, 2)
        return pixel_unshuffle(out, R)

    def _L0_ffn_ref(x, router_w, w_gate, w_up, w_down, sg, su, sd):
        import jax, jax.numpy as jnp
        import numpy as np
        N_EXPERTS = 8
        TOP_K = 2
        D_MODEL = 256
        D_FF = 512
        B, T = (4, 512)
        Bb, Tt, C = x.shape
        xf = x.reshape(-1, C)
        logits = xf @ router_w.T
        top_vals, top_idx = jax.lax.top_k(logits, TOP_K)
        top_w = jax.nn.softmax(top_vals, axis=-1)
        comb = jnp.sum(jax.nn.one_hot(top_idx, N_EXPERTS, dtype=xf.dtype) * top_w[..., None], axis=1)
        out = jnp.zeros_like(xf)
        for e in range(N_EXPERTS):
            h = jax.nn.silu(xf @ w_gate[e]) * (xf @ w_up[e])
            out = out + comb[:, e:e + 1] * (h @ w_down[e])
        out = out + jax.nn.silu(xf @ sg) * (xf @ su) @ sd
        return out.reshape(Bb, Tt, C)

    def _L1_conv_ref(x, global_token, in_proj_w, conv_w, conv_b, x_proj_w, dt_proj_w, dt_proj_b, A_log, D, out_proj_w):
        import jax, jax.numpy as jnp
        import numpy as np
        DIM = 256
        R = 2
        D_MODEL = DIM // (R * R)
        D_INNER = 2 * D_MODEL
        D_STATE = 16
        D_CONV = 4
        DT_RANK = (D_MODEL + 15) // 16
        NUM_TOKENS = 1

        def pixel_shuffle(x, r):
            B, C, H, W = x.shape
            c = C // (r * r)
            x = x.reshape(B, c, r, r, H, W)
            x = x.transpose(0, 1, 4, 2, 5, 3)
            return x.reshape(B, c, H * r, W * r)

        def pixel_unshuffle(x, r):
            B, C, Hr, Wr = x.shape
            H, W = (Hr // r, Wr // r)
            x = x.reshape(B, C, H, r, W, r)
            x = x.transpose(0, 1, 3, 5, 2, 4)
            return x.reshape(B, C * r * r, H, W)

        def mamba_block(seq, in_proj_w, conv_w, conv_b, x_proj_w, dt_proj_w, dt_proj_b, A_log, D, out_proj_w):
            B, L, _ = seq.shape
            xz = jnp.einsum('bld,ed->ble', seq, in_proj_w)
            u, z = jnp.split(xz, 2, axis=-1)
            up = jnp.pad(u, ((0, 0), (D_CONV - 1, 0), (0, 0)))
            u = sum((up[:, k:k + L, :] * conv_w[:, k] for k in range(D_CONV))) + conv_b
            u = jax.nn.silu(u)
            x_dbl = jnp.einsum('bld,ed->ble', u, x_proj_w)
            dt, Bm, Cm = jnp.split(x_dbl, [DT_RANK, DT_RANK + D_STATE], axis=-1)
            dt = jax.nn.softplus(jnp.einsum('blr,dr->bld', dt, dt_proj_w) + dt_proj_b)
            A = -jnp.exp(A_log)

            def step(h, inputs):
                dt_t, B_t, C_t, u_t = inputs
                dA = jnp.exp(dt_t[:, :, None] * A)
                h = dA * h + (dt_t * u_t)[:, :, None] * B_t[:, None, :]
                y = jnp.einsum('bdn,bn->bd', h, C_t)
                return (h, y)
            h0 = jnp.zeros((B, D_INNER, D_STATE), dtype=seq.dtype)
            xs = (dt.transpose(1, 0, 2), Bm.transpose(1, 0, 2), Cm.transpose(1, 0, 2), u.transpose(1, 0, 2))
            _, ys = jax.lax.scan(step, h0, xs)
            y = ys.transpose(1, 0, 2) + u * D
            y = y * jax.nn.silu(z)
            return jnp.einsum('bld,ed->ble', y, out_proj_w)
        B, C, H, W = x.shape
        xs = pixel_shuffle(x, R)
        seq = xs.reshape(B, D_MODEL, -1).transpose(0, 2, 1)
        tok = jnp.broadcast_to(global_token, (B, NUM_TOKENS, D_MODEL))
        seq = jnp.concatenate([tok, seq], axis=1)
        seq = mamba_block(seq, in_proj_w, conv_w, conv_b, x_proj_w, dt_proj_w, dt_proj_b, A_log, D, out_proj_w)
        seq = seq[:, -H * W * R * R:, :]
        out = seq.reshape(B, H * R, W * R, D_MODEL).transpose(0, 3, 1, 2)
        return pixel_unshuffle(out, R)

    def _L1_ffn_ref(x, router_w, w1, b1, w2, b2):
        import math
        import jax, jax.numpy as jnp
        import numpy as np
        NUM_EXPERTS = 8
        CAPACITY_FACTOR = 1.5
        B, T, D = x.shape
        E = router_w.shape[0]
        N = B * T
        C = max(math.ceil(CAPACITY_FACTOR * N / E), 1)
        x_flat = x.reshape(N, D)
        logits = x_flat @ router_w.T
        probs = jax.nn.softmax(logits, axis=-1)
        chosen_e = jnp.argmax(probs, axis=-1)
        chosen_p = jnp.max(probs, axis=-1)
        onehot = jax.nn.one_hot(chosen_e, E, dtype=jnp.float32)
        pos = jnp.take_along_axis(jnp.cumsum(onehot, axis=0), chosen_e[:, None], axis=1)[:, 0] - 1.0
        pos = pos.astype(jnp.int32)
        kept = pos < C
        pos_c = jnp.clip(pos, 0, C - 1)
        buf = jnp.zeros((E, C, D), dtype=x.dtype).at[chosen_e, pos_c].add(x_flat * kept[:, None].astype(x.dtype))
        h = jax.nn.gelu(jnp.einsum('ecd,edf->ecf', buf, w1) + b1[:, None, :], approximate=False)
        eo = jnp.einsum('ecf,efd->ecd', h, w2) + b2[:, None, :]
        y = eo[chosen_e, pos_c] * (chosen_p * kept.astype(x.dtype))[:, None]
        return y.reshape(B, T, D)

    def _gn(v, G=32, eps=1e-05):
        B_, C_, H_, W_ = v.shape
        g = v.reshape(B_, G, C_ // G, H_, W_)
        m = jnp.mean(g, axis=(2, 3, 4), keepdims=True)
        s = jnp.var(g, axis=(2, 3, 4), keepdims=True)
        return ((g - m) / jnp.sqrt(s + eps)).reshape(v.shape)

    def _ln_c(v, eps=1e-06):
        m = jnp.mean(v, axis=1, keepdims=True)
        s = jnp.var(v, axis=1, keepdims=True)
        return (v - m) / jnp.sqrt(s + eps)

    def _ln_t(v, eps=1e-05):
        m = jnp.mean(v, axis=-1, keepdims=True)
        s = jnp.var(v, axis=-1, keepdims=True)
        return (v - m) / jnp.sqrt(s + eps)

    def _to_tokens(v):
        B_, C_, H_, W_ = v.shape
        return v.reshape(B_, C_, H_ * W_).transpose(0, 2, 1)

    def _from_tokens(t, like):
        B_, C_, H_, W_ = like.shape
        return t.transpose(0, 2, 1).reshape(B_, C_, H_, W_)
    x = x + _L0_conv_ref(_ln_c(x), L0_conv_global_token, L0_conv_in_proj_w, L0_conv_conv_w, L0_conv_conv_b, L0_conv_x_proj_w, L0_conv_dt_proj_w, L0_conv_dt_proj_b, L0_conv_A_log, L0_conv_D, L0_conv_out_proj_w)
    t = _to_tokens(x)
    t = t + _L0_ffn_ref(_ln_t(t), L0_ffn_router_w, L0_ffn_w_gate, L0_ffn_w_up, L0_ffn_w_down, L0_ffn_sg, L0_ffn_su, L0_ffn_sd)
    x = _from_tokens(t, x)
    x = x + _L1_conv_ref(_ln_c(x), L1_conv_global_token, L1_conv_in_proj_w, L1_conv_conv_w, L1_conv_conv_b, L1_conv_x_proj_w, L1_conv_dt_proj_w, L1_conv_dt_proj_b, L1_conv_A_log, L1_conv_D, L1_conv_out_proj_w)
    t = _to_tokens(x)
    t = t + _L1_ffn_ref(_ln_t(t), L1_ffn_router_w, L1_ffn_w1, L1_ffn_b1, L1_ffn_w2, L1_ffn_b2)
    x = _from_tokens(t, x)
    return x

_drawn_inputs = setup_inputs


def setup_inputs(seed=0):
    import zlib

    import numpy as np

    out = dict(_drawn_inputs(seed))
    spreads = {'L0_conv_global_token': (0.0, 2.0),
     'L0_conv_conv_b': (0.0, 0.8),
     'L0_conv_D': (1.0, 0.6),
     'L1_conv_global_token': (0.0, 2.0),
     'L1_conv_conv_b': (0.0, 0.8),
     'L1_conv_D': (1.0, 0.6),
     'L1_ffn_b1': (0.0, 2.0),
     'L1_ffn_b2': (0.0, 2.0)}
    factors = {'L0_conv_in_proj_w': 8.0,
     'L0_conv_conv_w': 8.0,
     'L0_conv_x_proj_w': 8.0,
     'L0_conv_dt_proj_w': 8.0,
     'L0_conv_dt_proj_b': 8.0,
     'L0_conv_A_log': 8.0,
     'L0_conv_out_proj_w': 8.0,
     'L0_ffn_router_w': 3.74,
     'L0_ffn_w_gate': 3.288,
     'L0_ffn_w_up': 3.245,
     'L0_ffn_w_down': 3.242,
     'L1_conv_in_proj_w': 8.0,
     'L1_conv_conv_w': 8.0,
     'L1_conv_x_proj_w': 8.0,
     'L1_conv_dt_proj_w': 8.0,
     'L1_conv_dt_proj_b': 8.0,
     'L1_conv_A_log': 8.0,
     'L1_conv_out_proj_w': 8.0,
     'L1_ffn_w1': 15.968,
     'L0_ffn_sg': 4.436,
     'L0_ffn_su': 4.119,
     'L0_ffn_sd': 3.001,
     'L1_ffn_router_w': 3.395,
     'L1_ffn_w2': 4.113}
    for name, (base, spread) in spreads.items():
        noise = np.random.default_rng([zlib.crc32(name.encode()), seed]).standard_normal(out[name].shape)
        drawn = base * np.exp(spread * noise) if base else spread * noise
        out[name] = jnp.asarray(drawn.astype(out[name].dtype))
    for name, factor in factors.items():
        out[name] = (out[name] * factor).astype(out[name].dtype)
    return out
```

```python
from contextlib import ExitStack

import concourse.bass as bass
from concourse import mybir

F32 = mybir.dt.float32
I32 = mybir.dt.int32
U32 = mybir.dt.uint32
ALU = mybir.AluOpType
ACT = mybir.ActivationFunctionType
AX_X = mybir.AxisListType.X

P = 128
B, C, H, W = 4, 256, 24, 24
HW = H * W
TT = 96
ROWS = TT // W
TPB = HW // TT
NT = B * TPB
R = 2
DM, DI, DS, DC, DR = C // 4, 128, 16, 4, 4
LSEQ = HW * R * R + 1
BANK = 512
CPB = 5
NCH = B * CPB
TC = 462
PAD = DC - 1
LPAD = PAD + CPB * TC
CW = TC + PAD
NG, DG = 4, 32
NM, NS = 4, 4
ITEMS = NG * NM
REP_ROWS = 2 * NG + 2 * NM
UBUFS = 4
BANKS = 5
STATE_BANK = [i % BANKS for i in range(ITEMS - 1)] + [2]
STATE_GAP = [min(n for n in range(1, ITEMS) if STATE_BANK[i - n] == STATE_BANK[i]) for i in range(ITEMS)]
AT_SILU, AT_EXP, AT_ONE, AT_LN, AT_BC, AT_DT, AT_R, AT_LR = 9, 12, 14, 15, 15, 8, 15, 15
START = 6
NE, TOPK = 8, (2, 1)
F0, F1 = 512, 1024
FC0, FC1 = F0 // P, F1 // P
STILES = B * HW // P
MAXT = B * HW // P
RTILES = TOPK[0] * B * HW // P + NE
SLOTS0 = (STILES + RTILES) * P
CAP = -(-3 * B * HW // (2 * NE))
CT = 108
CTILES = CAP // CT
assert CTILES * CT == CAP and RTILES % 2 == 0 and STILES % 2 == 0 and B * HW % P == 0
assert NE * CAP + B * HW <= SLOTS0
assert NS * DG == P and CPB * TC >= LSEQ and NG * DG == DI and NM * NS == DS and TC <= BANK


def memory(nc, ctx, phase, used):

    def sb(name, shape, dt=F32):
        return ctx.enter_context(nc.sbuf_tensor(f"{phase}_{name}", shape, dt))

    def ps(name, shape, dt=F32):
        return ctx.enter_context(nc.psum_tensor(f"{phase}_{name}", shape, dt))

    def sem(name):
        used.append(nc.alloc_semaphore(f"{phase}_{name}"))
        return used[-1]

    return sb, ps, sem


def phase_setup(nc, a, g):
    with ExitStack() as ctx:
        sb, ps, sem = memory(nc, ctx, "setup", g["used"])
        xc = sb("xc", [P, B * 2, HW])
        raw = [{n: sb(f"raw{l}_{n}", s) for n, s in (
            ("winT", [P, DI]), ("cw", [P, 2, DI]), ("alog", [P, ITEMS]),
            ("wxT", [DR, DI]), ("wdtT", [DR, DI]))} for l in range(2)]
        zero = sb("zero", [P, 4 * C])
        tp = ps("tp", [P, 4, BANK])
        wp = ps("wp", [P, 2, BANK])
        zeroed, zero_stored = sem("zeroed"), sem("zero_stored")
        x_loaded, w_loaded = sem("x_loaded"), sem("w_loaded")
        ident_ready, x_turned, t_copied = sem("ident_ready"), sem("x_turned"), sem("t_copied")
        fold_ready, fold_multiplied = sem("fold_ready"), sem("fold_multiplied")
        pool_steps, exp_ready, act_copied = sem("pool_steps"), sem("exp_ready"), sem("act_copied")
        wz_zeroed, sel_ready, vec_steps = sem("wz_zeroed"), sem("sel_ready"), sem("vec_steps")
        block = ctx.enter_context(nc.Block())
        NW = 13

        @block.sync
        def _(sp):
            for b in range(B):
                sp.dma_start(xc[:, 2 * b:2 * b + 2, :],
                             a["x"][b].rearrange("(k p) h w -> p k (h w)", p=P)).then_inc(x_loaded, 16)
            sp.wait_ge(wz_zeroed, 2)
            for l in range(2):
                w, m = raw[l], g["mamba"][l]
                for s in range(2):
                    sp.dma_start(w["winT"][s * DM:(s + 1) * DM, :], a[f"L{l}_winT"][:, 0:DI]).then_inc(w_loaded, 16)
                    for pair in range(2):
                        tap = a[f"L{l}_cwT"][2 * pair + s:2 * pair + s + 1, :].broadcast_to([DM, DI])
                        sp.dma_start(w["cw"][s * DM:(s + 1) * DM, pair, :], tap).then_inc(w_loaded, 16)
                sp.dma_start(m["wz"][DM:P, :], a[f"L{l}_winT"][:, DI:2 * DI]).then_inc(w_loaded, 16)
                sp.dma_start(w["alog"][:, :], a[f"L{l}_alog"]).then_inc(w_loaded, 16)
                sp.dma_start(w["wxT"][:, :], a[f"L{l}_xpw"][0:DR, :]).then_inc(w_loaded, 16)
                sp.dma_start(w["wdtT"][:, :], a[f"L{l}_dtwT"]).then_inc(w_loaded, 16)
                sp.dma_start(m["wbc"][:, :], a[f"L{l}_xpT"][:, DR:DR + 2 * DS]).then_inc(w_loaded, 16)
                sp.dma_start(m["wout"][:, :], a[f"L{l}_woT"]).then_inc(w_loaded, 16)
                sp.dma_start(m["vec"][:, :], a[f"L{l}_vec"]).then_inc(w_loaded, 16)

            sp.wait_ge(zeroed, 1)
            routed = g["xs"][B * HW:SLOTS0, :].rearrange("(n p r) c -> n p (r c)", p=P, r=4)
            for n in range(routed.shape[0]):
                sp.dma_start(routed[n], zero[:, :]).then_inc(zero_stored, 16)
            sp.wait_ge(zero_stored, 16 * routed.shape[0])

        @block.gpsimd
        def _(pool):
            pool.memset(zero[:, :], 0.0).then_inc(zeroed, 1)
            for l in range(2):
                pool.memset(g["mamba"][l]["wz"][0:DM, :], 0.0).then_inc(wz_zeroed, 1)
            pool.memset(g["ident"][:, :], 0.0).then_inc(pool_steps, 1)
            pool.memset(g["fold"][:, :], 0.0).then_inc(pool_steps, 1)
            pool.memset(g["sel"][:, :, :], 0.0).then_inc(pool_steps, 1)
            pool.wait_ge(pool_steps, 3)
            pool.affine_select(out=g["ident"][:, :], in_=g["ident"][:, :], compare_op=ALU.not_equal, fill=1.0,
                               base=0, pattern=[[-1, P]], channel_multiplier=1).then_inc(ident_ready, 1)
            for s in range(NS):
                pool.affine_select(out=g["fold"][:, :], in_=g["fold"][:, :], compare_op=ALU.not_equal, fill=1.0,
                                   base=-DG * s, pattern=[[-1, DG]], channel_multiplier=1).then_inc(pool_steps, 1)
                pool.wait_ge(pool_steps, 4 + s)
            for k in range(NG):
                pool.tensor_copy(g["sel"][:, k, DG * k:DG * k + DG], g["fold"][:, :]).then_inc(sel_ready, 1)

        @block.tensor
        def _(pe):
            pe.wait_ge(ident_ready, 1)
            pe.wait_ge(x_loaded, 16 * B)
            for t in range(NT):
                if t >= 4:
                    pe.wait_ge(t_copied, t - 3)
                b, j = divmod(t, TPB)
                for k in range(2):
                    mm = nc.tensor.transpose(tp[0:TT, t % 4, k * P:(k + 1) * P],
                                             xc[:, 2 * b + k, j * TT:(j + 1) * TT], g["ident"][:, :])
                mm.then_inc(x_turned, 1)
            pe.wait_ge(w_loaded, 16 * 2 * NW)
            for l in range(2):
                nc.tensor.matmul(wp[:, l, 0:DI], raw[l]["wxT"][:, :], raw[l]["wdtT"][:, :],
                                 start=True, stop=True).then_inc(fold_multiplied, 1)

        @block.scalar
        def _(act):
            act.wait_ge(w_loaded, 16 * 2 * NW)
            for l in range(2):
                nc.scalar.activation(g["mamba"][l]["acol"][:, :], raw[l]["alog"][:, :], ACT.Exp).then_inc(exp_ready, 1)
                act.wait_ge(fold_multiplied, l + 1)
                nc.scalar.activation(g["mamba"][l]["wdt"][:, :], wp[:, l, 0:DI], ACT.Copy).then_inc(act_copied, 1)

        @block.vector
        def _(dve):
            for t in range(NT):
                dve.wait_ge(x_turned, t + 1)
                nc.vector.tensor_copy(g["T"][:, t, :], tp[0:TT, t % 4, 0:C]).then_inc(t_copied, 1)
            dve.wait_ge(w_loaded, 16 * 2 * NW)
            for l in range(2):
                dve.wait_ge(exp_ready, l + 1)
                m = g["mamba"][l]
                nc.vector.tensor_scalar(m["acol"][:, :], m["acol"][:, :], -1.0, None, ALU.mult).then_inc(vec_steps, 1)
                nc.vector.tensor_scalar(m["diag"][:, :], g["ident"][:, :], m["vec"][:, 2:3], None, ALU.mult).then_inc(vec_steps, 1)
                for pair in range(2):
                    nc.vector.tensor_tensor(m["wu"][:, pair, :], raw[l]["winT"][:, :], raw[l]["cw"][:, pair, :],
                                            ALU.mult).then_inc(vec_steps, 1)


def layernorm_stats(nc, dve, T, stats, mv, steps):
    for t in range(NT):
        nc.vector.bn_stats(stats[:, t, :], T[:, t, :]).then_inc(steps, 1)
    dve.wait_ge(steps, NT)
    for t in range(NT):
        nc.vector.bn_aggr(mv[:, t, :], stats[:, t, :]).then_inc(steps, 1)


def phase_sequence(nc, a, g, l):
    with ExitStack() as ctx:
        sb, ps, sem = memory(nc, ctx, f"seq{l}", g["used"])
        T = g["T"]
        stats, mv = sb("stats", [TT, NT, 6]), sb("mv", [TT, NT, 2])
        vare, rstd, mhalf = sb("vare", [TT, NT]), sb("rstd", [TT, NT]), sb("mhalf", [TT, NT])
        tn = sb("tn", [TT, 2, C])
        sq = sb("sq", [DM, B + 1, LPAD])
        token = sb("token", [DM, 1])
        tp = ps("tp", [DM, 2, 512])
        stat_steps, vare_ready, half_ready, rstd_ready = sem("stat_steps"), sem("vare_ready"), sem("half_ready"), sem("rstd_ready")
        tn_ready, turned, placed = sem("tn_ready"), sem("turned"), sem("placed")
        padded, token_loaded, stored = sem("padded"), sem("token_loaded"), sem("stored")
        block = ctx.enter_context(nc.Block())

        @block.gpsimd
        def _(pool):
            pool.memset(mhalf[:, :], -0.5).then_inc(half_ready, 1)
            pool.memset(sq[:, 0:B, 0:PAD], 0.0).then_inc(padded, 1)
            pool.memset(sq[:, 0:B, PAD + LSEQ:LPAD], 0.0).then_inc(padded, 1)
            pool.memset(sq[:, B, 0:CW], 0.0).then_inc(padded, 1)
            pool.wait_ge(token_loaded, 16)
            pool.tensor_copy(sq[:, 0:B, PAD:PAD + 1], token[:, :].unsqueeze(1).broadcast_to([DM, B, 1])).then_inc(padded, 1)
            pool.wait_ge(half_ready, 1)
            pool.wait_ge(vare_ready, 1)
            pool.tensor_tensor(rstd[:, :], vare[:, :], mhalf[:, :], ALU.pow).then_inc(rstd_ready, 1)

        @block.vector
        def _(dve):
            layernorm_stats(nc, dve, T, stats, mv, stat_steps)
            dve.wait_ge(stat_steps, 2 * NT)
            nc.vector.tensor_scalar(vare[:, :], mv[:, :, 1], 1e-6, None, ALU.add).then_inc(vare_ready, 1)
            dve.wait_ge(rstd_ready, 1)
            for t in range(NT):
                if t >= 2:
                    dve.wait_ge(turned, t - 1)
                nc.vector.tensor_scalar(tn[:, t % 2, :], T[:, t, :], mv[:, t, 0:1], rstd[:, t:t + 1],
                                        ALU.subtract, ALU.mult).then_inc(tn_ready, 1)

        @block.tensor
        def _(pe):
            for t in range(NT):
                pe.wait_ge(tn_ready, t + 1)
                if t >= 2:
                    pe.wait_ge(placed, 2 * (t - 1))
                planes = tn[:, t % 2, :].rearrange("p (c q) -> p q c", q=R * R)
                for q in range(R * R):
                    mm = nc.tensor.transpose(tp[:, t % 2, q * TT:(q + 1) * TT], planes[:, q, :], g["ident"][0:TT, 0:TT])
                mm.then_inc(turned, 1)

        @block.scalar
        def _(act):
            for t in range(NT):
                b, j = divmod(t, TPB)
                act.wait_ge(turned, t + 1)
                at = PAD + 1 + j * TT * R * R
                dst = sq[:, b, at:at + TT * R * R].rearrange("c (h i w q) -> c i h w q", h=ROWS, i=R, w=W, q=R)
                src = tp[:, t % 2, 0:TT * R * R].rearrange("c (i q h w) -> c i h w q", i=R, q=R, h=ROWS, w=W)
                for i in range(R):
                    nc.scalar.activation(dst[:, i], src[:, i], ACT.Copy).then_inc(placed, 1)

        @block.sync
        def _(sp):
            sp.dma_start(token[:, :], a[f"L{l}_token"]).then_inc(token_loaded, 16)
            sp.wait_ge(padded, 4)
            for k in range(NCH, NCH + 3):
                sp.dma_start(g["seq"][k], sq[:, B, 0:CW]).then_inc(stored, 16)
            for b in range(B):
                sp.wait_ge(placed, 2 * TPB * (b + 1))
                for c in range(CPB):
                    sp.dma_start(g["seq"][CPB * b + c], sq[:, b, c * TC:c * TC + CW]).then_inc(stored, 16)
            sp.wait_ge(stored, 16 * (NCH + 3))


def phase_mamba(nc, a, g, l):
    with ExitStack() as ctx:
        sb, ps, sem = memory(nc, ctx, f"mamba{l}", g["used"])
        T, m, sel = g["T"], g["mamba"][l], g["sel"]
        xs = sb("xs", [P, CW - 1])
        u, sz = sb("u", [P, UBUFS, TC]), sb("sz", [P, UBUFS, TC])
        ab, ex, w1, ln, rx = sb("ab", [P, TC]), sb("ex", [P, TC]), sb("w1", [P, TC]), sb("ln", [P, TC]), sb("rx", [P, TC])
        rr, lr = sb("rr", [P, TC]), sb("lr", [P, TC])
        dd = sb("dd", [P, 2, TC])
        bc = sb("bc", [2 * DS, TC])
        rep = sb("rep", [P, 2 * REP_ROWS, TC])
        dbu, hc = sb("dbu", [P, 4, TC]), sb("hc", [P, 4, TC])
        carry = sb("carry", [P, ITEMS])
        y = sb("y", [P, NCH * TC])
        yp = sb("yp", [P, 2, R * R, HW])
        state = ps("state", [P, BANKS, BANK])
        ysum, front = ps("ysum", [P, BANK]), ps("front", [P, 2, BANK])

        xs_loaded, scratch_stored, rep_loaded = sem("xs_loaded"), sem("scratch_stored"), sem("rep_loaded")
        front_mm, front_act, front_dve = sem("front_mm"), sem("front_act"), sem("front_dve")
        decay_ready, dbu_ready, scan_done, carry_done = sem("decay_ready"), sem("dbu_ready"), sem("scan_done"), sem("carry_done")
        hc_ready, hc_summed, carry_zeroed = sem("hc_ready"), sem("hc_summed"), sem("carry_zeroed")
        y_ready, projected, added = sem("y_ready"), sem("projected"), sem("added")
        unshuffled = [sem("unshuffled0"), sem("unshuffled1")]
        MM_U, MM_Z, MM_DT, MM_BC, MMS = 1, 2, 3, 4, 4
        A_U, A_Z, A_ABS, A_RELU, A_EXP, A_ONE, A_LN, A_BC, ACTS = 1, 2, 3, 4, 5, 6, 7, 8, 8
        D_R, D_LR, D_DT, D_DTU, DVES = 1, 2, 3, 4, 4
        REPS = 2 * NS
        block = ctx.enter_context(nc.Block())

        def chunk_of(eng, tile, k):
            if isinstance(k, int):
                return tile[:, k % UBUFS, :]
            return tile[:, bass.ds(eng.snap(k % UBUFS), 1), :]

        @block.sync
        def _(sp):
            def load_xs(k):
                for s in range(2):
                    src = g["seq"][bass.ds(k, 1), :, s:s + CW - 1].rearrange("o c n -> (o c) n")
                    sp.dma_start(xs[s * DM:(s + 1) * DM, :], src).then_inc(xs_loaded, 16)

            def half(k):
                return k % 2 if isinstance(k, int) else sp.snap(k % 2)

            def store(k):
                at = half(k)
                scr = g["scr"][bass.ds(at, 1), :, :]
                sp.wait_ge(front_dve, START + DVES * k + D_DTU)
                sp.dma_start(scr[:, 0:2 * P, :].rearrange("o (w p) n -> p (o w) n", p=P), dd[:, :, :]).then_inc(scratch_stored, 16)
                sp.wait_ge(front_act, START + ACTS * k + A_BC)
                sp.dma_start(scr[:, 2 * P:2 * P + 2 * DS, :].rearrange("o w n -> (o w) n"), bc[:, :]).then_inc(scratch_stored, 16)

            def replicate(k):
                at = half(k)
                scr = g["scr"][bass.ds(at, 1), :, :]
                row = at * REP_ROWS if isinstance(k, int) else sp.snap(k % 2 * REP_ROWS)
                sp.wait_ge(scratch_stored, 32 * (k + 1))
                for s in range(NS):
                    src = scr[:, 0:2 * P, :].rearrange("o (w d) n -> d (o w) n", d=DG)
                    sp.dma_start(rep[s * DG:(s + 1) * DG, bass.ds(row, 2 * NG), :], src).then_inc(rep_loaded, 16)
                    src = scr[:, 2 * P:2 * P + 2 * DS, :].rearrange("o (w s) n -> s (o w) n", s=NS)[s:s + 1]
                    sp.dma_start(rep[s * DG:(s + 1) * DG, bass.ds(row + 2 * NG, 2 * NM), :],
                                 src.broadcast_to([DG, 2 * NM, TC])).then_inc(rep_loaded, 16)

            replicas = sp.alloc_register(f"replicas{l}")
            load_xs(0)
            for k in range(2):
                sp.wait_ge(front_mm, START + MMS * k + MM_Z)
                load_xs(k + 1)
                store(k)
                if k == 0:
                    replicate(0)
            with sp.Fori(0, NCH) as k:
                sp.reg_mul(replicas, k, 16 * REPS)
                sp.reg_add(replicas, replicas, 16 * REPS)
                replicas_before = sp.snap(replicas)
                items_before = START + ITEMS * k
                sp.wait_ge(decay_ready, items_before)
                sp.wait_ge(dbu_ready, items_before)
                sp.wait_ge(hc_ready, items_before)
                sp.wait_ge(rep_loaded, replicas_before)
                replicate(k + 1)
                sp.wait_ge(front_mm, START + MMS * (k + 2) + MM_Z)
                load_xs(k + 3)
                store(k + 2)
            sp.wait_ge(rep_loaded, 16 * REPS * (NCH + 1))
            sp.wait_ge(scratch_stored, 32 * (NCH + 2))
            sp.wait_ge(xs_loaded, 32 * (NCH + 3))

        @block.tensor
        def _(pe):
            for s in (front_mm, hc_summed, projected):
                pe.sem_inc(s, START)

            def prep_u(k):
                pe.wait_ge(xs_loaded, 32 * (k + 1))
                pe.wait_ge(front_act, START + ACTS * k)
                nc.tensor.matmul(front[:, 0, 0:TC], m["wu"][:, 0, :], xs[:, 0:TC], start=True, stop=False)
                nc.tensor.matmul(front[:, 0, 0:TC], m["wu"][:, 1, :], xs[:, 2:2 + TC],
                                 start=False, stop=True).then_inc(front_mm, 1)

            def prep_z(k):
                nc.tensor.matmul(front[:, 1, 0:TC], m["wz"][:, :], xs[:, 2:2 + TC],
                                 start=True, stop=True).then_inc(front_mm, 1)

            def prep_dt(k):
                pe.wait_ge(front_act, START + ACTS * k + A_Z)
                nc.tensor.matmul(front[:, 0, 0:TC], m["wdt"][:, :], chunk_of(pe, u, k),
                                 start=True, stop=True).then_inc(front_mm, 1)

            def prep_bc(k):
                nc.tensor.matmul(front[0:2 * DS, 1, 0:TC], m["wbc"][:, :], chunk_of(pe, u, k),
                                 start=True, stop=True).then_inc(front_mm, 1)

            for k in range(2):
                prep_u(k)
                prep_z(k)
                prep_dt(k)
                prep_bc(k)
            with pe.Fori(0, NCH) as k:
                pe.wait_ge(y_ready, START + k)
                nc.tensor.matmul(ysum[:, 0:TC], m["diag"][:, :], chunk_of(pe, u, k), start=True, stop=False)
                for i in range(ITEMS):
                    pe.wait_ge(hc_ready, START + ITEMS * k + i + 1)
                    nc.tensor.matmul(ysum[:, 0:TC], sel[:, i // NM, :], hc[:, i % 4, :],
                                     start=False, stop=(i == ITEMS - 1)).then_inc(hc_summed, 1)
                    if i == 0:
                        prep_u(k + 2)
                    if i == 1:
                        prep_z(k + 2)
                    if i == AT_DT:
                        prep_dt(k + 2)
                    if i == AT_DT + 1:
                        prep_bc(k + 2)
            pe.wait_ge(front_act, START + ACTS * (NCH + 2))
            for t in range(NT):
                b, j = divmod(t, TPB)
                for i in range(R):
                    pe.wait_ge(unshuffled[i], b + 1)
                pe.wait_ge(added, START + t - 1)
                out = front[0:TT, t % 2, 0:C].rearrange("p (c q) -> p q c", q=R * R)
                for q in range(R * R):
                    mm = nc.tensor.matmul(out[:, q, :], yp[:, b % 2, q, j * TT:(j + 1) * TT], m["wout"][:, :],
                                          start=True, stop=True, skip_group_check=True)
                mm.then_inc(projected, 1)

        def planes(b, i):
            at = b * CPB * TC + 1
            src = y[:, at:at + HW * R * R].rearrange("d (h i w q) -> d i q h w", h=H, i=R, w=W, q=R)[:, i]
            return src, yp[:, b % 2, R * i:R * i + R, :].rearrange("d q (h w) -> d q h w", h=H)

        @block.scalar
        def _(act):
            act.sem_inc(front_act, START)
            act.sem_inc(decay_ready, START)
            at = act.alloc_register(f"act_row{l}")
            conv_b, dt_b = m["vec"][:, 0:1], m["vec"][:, 1:2]

            def out_of(tile, k):
                if isinstance(k, int):
                    return tile[:, k % UBUFS, :]
                act.reg_add(at, act.snap(k % UBUFS), 0)
                return tile[:, bass.ds(act.snap(at), 1), :]

            def prep_silu(k):
                act.wait_ge(front_mm, START + MMS * k + MM_Z)
                act.wait_ge(y_ready, START + k - UBUFS + 1)
                nc.scalar.activation(out_of(u, k), front[:, 0, 0:TC], ACT.Silu, bias=conv_b).then_inc(front_act, 1)
                nc.scalar.activation(out_of(sz, k), front[:, 1, 0:TC], ACT.Silu).then_inc(front_act, 1)

            def prep_exp(k):
                act.wait_ge(front_mm, START + MMS * k + MM_DT)
                act.wait_ge(front_dve, START + DVES * k)
                nc.scalar.activation(ab[:, :], front[:, 0, 0:TC], ACT.Abs, bias=dt_b).then_inc(front_act, 1)
                nc.scalar.activation(rx[:, :], front[:, 0, 0:TC], ACT.Relu, bias=dt_b).then_inc(front_act, 1)
                act.wait_ge(front_act, START + ACTS * k + A_ABS)
                nc.scalar.activation(ex[:, :], ab[:, :], ACT.Exp, scale=-1.0).then_inc(front_act, 1)

            def prep_one(k):
                act.wait_ge(front_act, START + ACTS * k + A_EXP)
                nc.scalar.activation(w1[:, :], ex[:, :], ACT.Copy, bias=1.0).then_inc(front_act, 1)

            def prep_ln(k):
                nc.scalar.activation(ln[:, :], ex[:, :], ACT.Ln, bias=1.0).then_inc(front_act, 1)

            def prep_bc(k):
                act.wait_ge(front_mm, START + MMS * k + MM_BC)
                if not (isinstance(k, int) and k == 0):
                    act.wait_ge(scratch_stored, 32 * k)
                nc.scalar.activation(bc[:, :], front[0:2 * DS, 1, 0:TC], ACT.Copy).then_inc(front_act, 1)

            for k in range(2):
                prep_silu(k)
                prep_exp(k)
                prep_one(k)
                prep_ln(k)
                prep_bc(k)
            with act.Fori(0, NCH // 2) as pair:
                for par in range(2):
                    k = pair * 2 + par
                    act.wait_ge(rep_loaded, 16 * REPS * (k + 1))
                    for i in range(ITEMS):
                        act.wait_ge(carry_done, START + ITEMS * k + i - STATE_GAP[i] + 1)
                        nc.scalar.activation(state[:, STATE_BANK[i], 0:TC], rep[:, par * REP_ROWS + i // NM, :], ACT.Exp,
                                             scale=m["acol"][:, i:i + 1]).then_inc(decay_ready, 1)
                        if i == AT_SILU:
                            prep_silu(k + 2)
                        if i == AT_EXP:
                            prep_exp(k + 2)
                        if i == AT_ONE:
                            prep_one(k + 2)
                        if i == AT_LN:
                            prep_ln(k + 2)
                        if i == AT_BC:
                            prep_bc(k + 2)
            for b in range(B):
                act.wait_ge(y_ready, START + NCH)
                if b >= 2:
                    act.wait_ge(projected, START + TPB * (b - 1))
                src, dst = planes(b, 0)
                nc.scalar.activation(dst, src, ACT.Copy).then_inc(unshuffled[0], 1)

        @block.gpsimd
        def _(pool):
            pool.sem_inc(dbu_ready, START)
            with pool.Fori(0, NCH // 2) as pair:
                for par in range(2):
                    k = pair * 2 + par
                    at = par * REP_ROWS
                    pool.wait_ge(rep_loaded, 16 * REPS * (k + 1))
                    for i in range(ITEMS):
                        pool.wait_ge(scan_done, START + ITEMS * k + i - 3)
                        pool.tensor_tensor(dbu[:, i % 4, :], rep[:, at + NG + i // NM, :], rep[:, at + 2 * NG + i % NM, :],
                                           ALU.mult).then_inc(dbu_ready, 1)
            for b in range(B):
                pool.wait_ge(y_ready, START + NCH)
                if b >= 2:
                    pool.wait_ge(projected, START + TPB * (b - 1))
                src, dst = planes(b, 1)
                pool.tensor_copy(dst, src).then_inc(unshuffled[1], 1)

        @block.vector
        def _(dve):
            for s in (scan_done, carry_done, hc_ready, front_dve, y_ready, added):
                dve.sem_inc(s, START)

            def prep(k, step):
                done = START + DVES * k
                if step == D_R:
                    dve.wait_ge(front_act, START + ACTS * k + A_ONE)
                    nc.vector.scalar_tensor_tensor(out=rr[:, :], in0=w1[:, :], scalar=1.0, in1=ex[:, :],
                                                   op0=ALU.subtract, op1=ALU.subtract).then_inc(front_dve, 1)
                if step == D_LR:
                    dve.wait_ge(front_act, START + ACTS * k + A_LN)
                    dve.wait_ge(front_dve, done + D_R)
                    nc.vector.tensor_tensor(lr[:, :], ln[:, :], rr[:, :], ALU.subtract).then_inc(front_dve, 1)
                if step == D_DT:
                    if not (isinstance(k, int) and k == 0):
                        dve.wait_ge(scratch_stored, 32 * k)
                    dve.wait_ge(front_dve, done + D_LR)
                    nc.vector.tensor_tensor(dd[:, 0, :], lr[:, :], rx[:, :], ALU.add).then_inc(front_dve, 1)
                if step == D_DTU:
                    dve.wait_ge(front_dve, done + D_DT)
                    nc.vector.tensor_tensor(dd[:, 1, :], dd[:, 0, :], chunk_of(dve, u, k), ALU.mult).then_inc(front_dve, 1)

            for k in range(2):
                for step in (D_R, D_LR, D_DT, D_DTU):
                    prep(k, step)
            with dve.Fori(0, B) as b:
                dve.wait_ge(scan_done, START + ITEMS * CPB * b)
                nc.vector.memset(carry[:, :], 0.0).then_inc(carry_zeroed, 1)
                with dve.Fori(0, CPB) as c:
                    k = dve.snap(b * CPB + c)
                    dve.wait_ge(carry_zeroed, b + 1)
                    dve.wait_ge(rep_loaded, 16 * REPS * (k + 1))
                    c_rows = dve.snap(k % 2 * REP_ROWS)

                    def read_out(i):
                        dve.wait_ge(scan_done, START + ITEMS * k + i + 1)
                        dve.wait_ge(hc_summed, START + ITEMS * k + i - 3)
                        nc.vector.tensor_tensor(hc[:, i % 4, :], state[:, STATE_BANK[i], 0:TC],
                                                rep[:, bass.ds(c_rows + 3 * NG + i % NM, 1), :],
                                                ALU.mult).then_inc(hc_ready, 1)
                        nc.vector.tensor_copy(carry[:, i:i + 1], state[:, STATE_BANK[i], TC - 1:TC]).then_inc(carry_done, 1)

                    for i in range(ITEMS):
                        n = START + ITEMS * k + i
                        dve.wait_ge(decay_ready, n + 1)
                        dve.wait_ge(dbu_ready, n + 1)
                        bank = state[:, STATE_BANK[i], 0:TC]
                        nc.vector.tensor_tensor_scan(bank, bank, dbu[:, i % 4, :],
                                                     carry[:, i:i + 1], ALU.mult, ALU.add).then_inc(scan_done, 1)
                        if i > 0:
                            read_out(i - 1)
                        if i == AT_R:
                            prep(k + 2, D_R)
                        if i == AT_LR:
                            prep(k + 2, D_LR)
                    read_out(ITEMS - 1)
                    prep(k + 2, D_DT)
                    prep(k + 2, D_DTU)
                    dve.wait_ge(hc_summed, START + ITEMS * (k + 1))
                    nc.vector.tensor_tensor(y[:, bass.ds(k * TC, TC)], ysum[:, 0:TC], chunk_of(dve, sz, k),
                                            ALU.mult).then_inc(y_ready, 1)
            for t in range(NT):
                dve.wait_ge(projected, START + t + 1)
                nc.vector.tensor_tensor(T[:, t, :], T[:, t, :], front[0:TT, t % 2, 0:C], ALU.add).then_inc(added, 1)


def phase_route(nc, a, g, l):
    top = TOPK[l]
    with ExitStack() as ctx:
        sb, ps, sem = memory(nc, ctx, f"route{l}", g["used"])
        T, ident = g["T"], g["ident"]
        stats, mv = sb("stats", [TT, NT, 6]), sb("mv", [TT, NT, 2])
        vare, rstd, mhalf = sb("vare", [TT, NT]), sb("rstd", [TT, NT]), sb("mhalf", [TT, NT])
        xn = sb("xn", [TT, NT, C])
        xT = sb("xT", [P, 2, 2 * TT])
        wr = sb("wr", [P, 2, NE])
        lg, best, which = sb("lg", [TT, NT, NE]), sb("best", [TT, NT, NE]), sb("which", [TT, NT, NE], U32)
        whichf = sb("whichf", [TT, 2, NT])
        eid = sb("eid", [TT, NE, NT])
        one = sb("one", [TT, 2, NE, NT])
        both, picked = sb("both", [TT, NE, NT]), sb("picked", [TT, NE, NT])
        before, ones = sb("before", [TT, TT]), sb("ones", [TT, TT])
        tot, cum, prev = sb("tot", [TT, NE, NT]), sb("cum", [TT, NE * NT]), sb("prev", [TT, NE, NT])
        pos, count = sb("pos", [TT, NE, NT]), sb("count", [TT, NE])
        steps128, over = sb("steps128", [TT, NE, MAXT]), sb("over", [TT, NE, MAXT])
        tiles, ends, first = sb("tiles", [TT, NE]), sb("ends", [TT, NE]), sb("first", [TT, NE])
        slotf, kept = sb("slotf", [TT, 2, NT]), sb("kept", [TT, NT])
        token, base = sb("token", [TT, NT]), sb("base", [TT, NT])
        tile_id, passed, owner = sb("tile_id", [1, RTILES, NE]), sb("passed", [1, RTILES, NE]), sb("owner", [1, RTILES])
        dif, ee, den, prob = sb("dif", [TT, NT, NE]), sb("ee", [TT, NT, NE]), sb("den", [TT, NT]), sb("prob", [TT, NT])
        tp, lgp = ps("tp", [P, 2, BANK]), ps("lgp", [TT, BANK])
        rank_ps, tot_ps = ps("rank", [TT, BANK]), ps("tot_ps", [TT, BANK])
        stat_steps, vare_ready, rstd_ready = sem("stat_steps"), sem("vare_ready"), sem("rstd_ready")
        xn_ready, turned, xT_ready, scored = sem("xn_ready"), sem("turned"), sem("xT_ready"), sem("scored")
        consts, wr_loaded, one_ready, counted = sem("consts"), sem("wr_loaded"), sem("one_ready"), sem("counted")
        steps, exp_asked, exp_ready, slots_ready, sent = sem("steps"), sem("exp_asked"), sem("exp_ready"), sem("slots_ready"), sem("sent")
        straight = sem("straight")
        block = ctx.enter_context(nc.Block())

        @block.sync
        def _(sp):
            sp.dma_start(wr[:, :, :], a[f"L{l}_wrT"].rearrange("(k p) e -> p k e", p=P)).then_inc(wr_loaded, 16)
            if l == 0:
                for t in range(NT):
                    sp.wait_ge(xn_ready, t + 1)
                    sp.dma_start(g["xs"][t * TT:(t + 1) * TT, :], xn[:, t, :]).then_inc(straight, 16)
                sp.wait_ge(straight, 16 * NT)

        @block.gpsimd
        def _(pool):
            pool.memset(mhalf[:, :], -0.5).then_inc(consts, 1)
            pool.memset(before[:, :], 1.0).then_inc(consts, 1)
            pool.memset(ones[:, :], 1.0).then_inc(consts, 1)
            pool.iota(eid[:, :, :], pattern=[[1, NE], [0, NT]], base=0, channel_multiplier=0,
                      allow_small_or_imprecise_dtypes=True).then_inc(consts, 1)
            pool.iota(steps128[:, :, :], pattern=[[0, NE], [P, MAXT]], base=0, channel_multiplier=0,
                      allow_small_or_imprecise_dtypes=True).then_inc(consts, 1)
            pool.iota(tile_id[:, :, :], pattern=[[1, RTILES], [0, NE]], base=0, channel_multiplier=0,
                      allow_small_or_imprecise_dtypes=True).then_inc(consts, 1)
            pool.iota(token[:, :], pattern=[[TT, NT]], base=0, channel_multiplier=1,
                      allow_small_or_imprecise_dtypes=True).then_inc(consts, 1)
            pool.wait_ge(consts, 7)
            pool.affine_select(out=before[:, :], in_=before[:, :], compare_op=ALU.is_gt, fill=0.0,
                               base=0, pattern=[[1, TT]], channel_multiplier=-1).then_inc(consts, 1)
            pool.wait_ge(vare_ready, 1)
            pool.tensor_tensor(rstd[:, :], vare[:, :], mhalf[:, :], ALU.pow).then_inc(rstd_ready, 1)
            pool.wait_ge(slots_ready, 1)
            for t in range(NT):
                for c in range(top):
                    pool.indirect_dma_start(out=g["xs"][:, :], out_offset=bass.IndirectOffsetOnAxis(ap=g["slot"][:, c, t:t + 1], axis=0),
                                            in_=xn[:, t, :], in_offset=None).then_inc(sent, 16)
            pool.wait_ge(sent, 16 * NT * top)

        @block.tensor
        def _(pe):
            pe.wait_ge(wr_loaded, 16)
            def score(t):
                pe.wait_ge(xT_ready, t + 1)
                for k in range(2):
                    mm = nc.tensor.matmul(lgp[:, t * NE:(t + 1) * NE], xT[:, t % 2, k * TT:(k + 1) * TT], wr[:, k, :],
                                          start=(k == 0), stop=(k == 1), skip_group_check=True)
                mm.then_inc(scored, 1)
            for t in range(NT):
                pe.wait_ge(xn_ready, t + 1)
                if t >= 2:
                    pe.wait_ge(xT_ready, t - 1)
                for k in range(2):
                    mm = nc.tensor.transpose(tp[:, t % 2, k * TT:(k + 1) * TT], xn[:, t, k * P:(k + 1) * P], ident[0:TT, 0:TT])
                mm.then_inc(turned, 1)
                if t >= 1:
                    score(t - 1)
            score(NT - 1)
            pe.wait_ge(one_ready, 1)
            pe.wait_ge(consts, 8)
            flat = both[:, :, :].rearrange("p e t -> p (e t)")
            nc.tensor.matmul(rank_ps[:, 0:NE * NT], before[:, :], flat, start=True, stop=True).then_inc(counted, 1)
            nc.tensor.matmul(tot_ps[:, 0:NE * NT], ones[:, :], flat, start=True, stop=True).then_inc(counted, 1)

        @block.scalar
        def _(act):
            for t in range(NT):
                act.wait_ge(turned, t + 1)
                if t >= 2:
                    act.wait_ge(scored, t - 1)
                nc.scalar.activation(xT[:, t % 2, :], tp[:, t % 2, 0:2 * TT], ACT.Copy).then_inc(xT_ready, 1)
            act.wait_ge(exp_asked, 1)
            if l == 0:
                nc.scalar.activation(ee[:, :, 0], dif[:, :, 0], ACT.Exp).then_inc(exp_ready, 1)
            else:
                nc.scalar.activation(ee[:, :, :], dif[:, :, :], ACT.Exp).then_inc(exp_ready, 1)

        @block.vector
        def _(dve):
            done = [0]

            def then(ins):
                done[0] += 1
                ins.then_inc(steps, 1)
                dve.wait_ge(steps, done[0])

            def over_tiles(x):
                return x.unsqueeze(1).broadcast_to([TT, NE, NT])

            layernorm_stats(nc, dve, T, stats, mv, stat_steps)
            dve.wait_ge(stat_steps, 2 * NT)
            nc.vector.tensor_scalar(vare[:, :], mv[:, :, 1], 1e-5, None, ALU.add).then_inc(vare_ready, 1)
            dve.wait_ge(rstd_ready, 1)
            for t in range(NT):
                nc.vector.tensor_scalar(xn[:, t, :], T[:, t, :], mv[:, t, 0:1], rstd[:, t:t + 1],
                                        ALU.subtract, ALU.mult).then_inc(xn_ready, 1)
            dve.wait_ge(scored, NT)
            then(nc.vector.tensor_copy(lg[:, :, :], lgp[:, 0:NT * NE].rearrange("p (t e) -> p t e", t=NT)))
            for t in range(NT):
                last = nc.vector.max(best[:, t, :], lg[:, t, :])
                if t < NT - 1:
                    last.then_inc(stat_steps, 1)
            then(last)
            dve.wait_ge(stat_steps, 3 * NT - 1)
            for t in range(NT):
                last = nc.vector.max_index(which[:, t, :], best[:, t, :], lg[:, t, :])
                if t < NT - 1:
                    last.then_inc(stat_steps, 1)
            then(last)
            dve.wait_ge(stat_steps, 4 * NT - 2)
            if l == 0:
                then(nc.vector.tensor_tensor(dif[:, :, 0], best[:, :, 1], best[:, :, 0], ALU.subtract))
            else:
                then(nc.vector.tensor_tensor(dif[:, :, :], lg[:, :, :], best[:, :, 0:1].broadcast_to([TT, NT, NE]), ALU.subtract))
            dve.sem_inc(exp_asked, 1)
            dve.wait_ge(consts, 8)
            for c in range(top):
                then(nc.vector.tensor_copy(whichf[:, c, :], which[:, :, c]))
                then(nc.vector.tensor_tensor(one[:, c, :, :], over_tiles(whichf[:, c, :]), eid[:, :, :], ALU.is_equal))
            if top == 2:
                nc.vector.tensor_tensor(both[:, :, :], one[:, 0, :, :], one[:, 1, :, :], ALU.add).then_inc(one_ready, 1)
            else:
                nc.vector.tensor_copy(both[:, :, :], one[:, 0, :, :]).then_inc(one_ready, 1)
            dve.wait_ge(exp_ready, 1)
            if l == 0:
                then(nc.vector.tensor_scalar(den[:, :], ee[:, :, 0], 1.0, None, ALU.add))
                then(nc.vector.reciprocal(g["share"][:, 0, :], den[:, :]))
                then(nc.vector.tensor_tensor(g["share"][:, 1, :], g["share"][:, 0, :], ee[:, :, 0], ALU.mult))
            else:
                then(nc.vector.tensor_reduce(den[:, :], ee[:, :, :], AX_X, ALU.add))
                then(nc.vector.reciprocal(prob[:, :], den[:, :]))
            dve.wait_ge(counted, 2)
            then(nc.vector.tensor_copy(tot[:, :, :].rearrange("p e t -> p (e t)"), tot_ps[:, 0:NE * NT]))
            flat = tot[:, :, :].rearrange("p e t -> p (e t)")
            then(nc.vector.memset(cum[:, :], 0.0))
            then(nc.vector.tensor_tensor_scan(prev[:, :, :].rearrange("p e t -> p (e t)"), flat, cum[:, :], 0.0, ALU.add, ALU.add))
            then(nc.vector.tensor_tensor(prev[:, :, :], prev[:, :, :], tot[:, :, :], ALU.subtract))
            then(nc.vector.tensor_copy(first[:, :], prev[:, :, 0]))
            then(nc.vector.tensor_tensor(prev[:, :, :], prev[:, :, :], first[:, :].unsqueeze(2).broadcast_to([TT, NE, NT]), ALU.subtract))
            then(nc.vector.tensor_tensor(count[:, :], prev[:, :, NT - 1], tot[:, :, NT - 1], ALU.add))
            then(nc.vector.tensor_tensor(pos[:, :, :], prev[:, :, :], rank_ps[:, 0:NE * NT].rearrange("p (e t) -> p e t", e=NE), ALU.add))
            if l == 0:
                then(nc.vector.tensor_tensor(over[:, :, :], count[:, :].unsqueeze(2).broadcast_to([TT, NE, MAXT]), steps128[:, :, :], ALU.is_gt))
                then(nc.vector.tensor_reduce(tiles[:, :], over[:, :, :], AX_X, ALU.add))
                then(nc.vector.tensor_tensor_scan(ends[:, :], tiles[:, :], cum[:, 0:NE], 0.0, ALU.add, ALU.add))
                then(nc.vector.tensor_tensor(first[:, :], ends[:, :], tiles[:, :], ALU.subtract))
                then(nc.vector.tensor_scalar(first[:, :], first[:, :], float(P), float(B * HW), ALU.mult, ALU.add))
                then(nc.vector.tensor_tensor(pos[:, :, :], pos[:, :, :], first[:, :].unsqueeze(2).broadcast_to([TT, NE, NT]), ALU.add))
                then(nc.vector.tensor_tensor(passed[:, :, :], ends[0:1, :].unsqueeze(1).broadcast_to([1, RTILES, NE]), tile_id[:, :, :], ALU.is_le))
                then(nc.vector.tensor_reduce(owner[:, :], passed[:, :, :], AX_X, ALU.add))
                then(nc.vector.tensor_scalar(owner[:, :], owner[:, :], float(NE - 1), None, ALU.min))
                then(nc.vector.tensor_copy(g["owner"][:, STILES:STILES + RTILES], owner[:, :]))
                then(nc.vector.memset(owner[:, 0:STILES], float(NE)))
                then(nc.vector.tensor_copy(g["owner"][:, 0:STILES], owner[:, 0:STILES]))
            for c in range(top):
                then(nc.vector.tensor_tensor(picked[:, :, :], one[:, c, :, :], pos[:, :, :], ALU.mult))
                then(nc.vector.tensor_reduce(slotf[:, c, :], picked[:, :, :].rearrange("p e t -> p t e"), AX_X, ALU.add))
            if l == 0:
                nc.vector.tensor_copy(g["slot"][:, :, :], slotf[:, :, :]).then_inc(slots_ready, 1)
            else:
                then(nc.vector.tensor_scalar(kept[:, :], slotf[:, 0, :], float(CAP), None, ALU.is_lt))
                then(nc.vector.tensor_tensor(g["share"][:, 0, :], prob[:, :], kept[:, :], ALU.mult))
                then(nc.vector.tensor_scalar(base[:, :], whichf[:, 0, :], float(CAP), None, ALU.mult))
                then(nc.vector.tensor_tensor(slotf[:, 0, :], slotf[:, 0, :], base[:, :], ALU.add))
                then(nc.vector.tensor_scalar(token[:, :], token[:, :], float(NE * CAP), None, ALU.add))
                then(nc.vector.tensor_tensor(slotf[:, 0, :], slotf[:, 0, :], token[:, :], ALU.subtract))
                then(nc.vector.tensor_tensor(slotf[:, 0, :], slotf[:, 0, :], kept[:, :], ALU.mult))
                then(nc.vector.tensor_tensor(slotf[:, 0, :], slotf[:, 0, :], token[:, :], ALU.add))
                then(nc.vector.tensor_scalar(slotf[:, 1, :], slotf[:, 0, :], float(NE * CAP - 1), None, ALU.min))
                nc.vector.tensor_copy(g["slot"][:, :, :], slotf[:, :, :]).then_inc(slots_ready, 1)


def phase_experts0(nc, a, g):
    with ExitStack() as ctx:
        sb, ps, sem = memory(nc, ctx, "experts0", g["used"])
        ident = g["ident"]
        wgu = sb("wgu", [P, NE + 1, 2, 2, F0])
        wd = sb("wd", [P, NE + 1, FC0, C])
        xs, xT = sb("xs", [P, 2, C]), sb("xT", [P, 2, C])
        sg, h, hT, eo = sb("sg", [P, 2, F0]), sb("h", [P, 2, F0]), sb("hT", [P, 2, F0]), sb("eo", [P, 2, C])
        tp, gate, up = ps("tp", [P, BANK]), ps("gate", [P, 2, BANK]), ps("up", [P, 2, BANK])
        htp, down = ps("htp", [P, BANK]), ps("down", [P, 2, BANK])
        shared_loaded, routed_loaded = sem("shared_loaded"), sem("routed_loaded")
        x_loaded, stored = [sem("x_loaded0"), sem("x_loaded1")], [sem("stored0"), sem("stored1")]
        turned, xT_ready, gate_done, up_done = sem("turned"), sem("xT_ready"), sem("gate_done"), sem("up_done")
        sg_ready, h_ready, h_turned, hT_ready = sem("sg_ready"), sem("h_ready"), sem("h_turned"), sem("hT_ready")
        down_done, eo_ready = sem("down_done"), sem("eo_ready")
        block = ctx.enter_context(nc.Block())
        TILES, LOADS = STILES + RTILES, 5

        def tile(i, off):
            return 2 * i + off, off % 2, i + off // 2

        @block.sync
        def _(sp):
            def load(e, w_g, w_u, w_d, done):
                for k in range(2):
                    sp.dma_start(wgu[:, e, 0, k, :], w_g[k * P:(k + 1) * P, :]).then_inc(done, 16)
                    sp.dma_start(wgu[:, e, 1, k, :], w_u[k * P:(k + 1) * P, :]).then_inc(done, 16)
                sp.dma_start(wd[:, e, :, :], w_d.rearrange("(f p) c -> p f c", p=P)).then_inc(done, 16)

            def load_x(t, first=False):
                n, par, _ = t
                if not first:
                    sp.wait_ge(turned, START + n - 1)
                sp.dma_start(xs[:, par, :], g["xs"][bass.ds(n * P, P), :]).then_inc(x_loaded[par], 16)

            load(NE, a["L0_sg"], a["L0_su"], a["L0_sd"], shared_loaded)
            load_x(tile(0, 0), True)
            load_x(tile(0, 1), True)
            for e in range(NE):
                load(e, a["L0_wg"][e], a["L0_wu"][e], a["L0_wd"][e], routed_loaded)
            with sp.Fori(1, TILES // 2) as i:
                load_x(tile(i, 0))
                load_x(tile(i, 1))

        @block.tensor
        def _(pe):
            for s in (turned, h_turned, down_done):
                pe.sem_inc(s, START)

            def owner(t):
                return pe.value_load(g["owner"][0:1, bass.ds(t[0], 1)], min_val=0, max_val=NE)

            def turn(t):
                n, par, m = t
                pe.wait_ge(x_loaded[par], 16 * (m + 1))
                pe.wait_ge(xT_ready, START + n)
                for k in range(2):
                    mm = nc.tensor.transpose(tp[:, k * P:(k + 1) * P], xs[:, par, k * P:(k + 1) * P], ident[:, :])
                mm.then_inc(turned, 1)

            def widen(t):
                n, par, _ = t
                e = owner(t)
                pe.wait_ge(xT_ready, START + n + 1)
                pe.wait_ge(h_ready, START + n - 1)
                for which, bank, done in ((0, gate, gate_done), (1, up, up_done)):
                    for k in range(2):
                        mm = nc.tensor.matmul(bank[:, par, :], xT[:, par, k * P:(k + 1) * P],
                                              wgu[:, bass.ds(e, 1), which, k, :], start=(k == 0), stop=(k == 1))
                    mm.then_inc(done, 1)

            def turn_h(t):
                n, par, _ = t
                pe.wait_ge(h_ready, START + n + 1)
                pe.wait_ge(hT_ready, START + n)
                for f in range(FC0):
                    mm = nc.tensor.transpose(htp[:, f * P:(f + 1) * P], h[:, par, f * P:(f + 1) * P], ident[:, :])
                mm.then_inc(h_turned, 1)

            def narrow(t):
                n, par, _ = t
                e = owner(t)
                pe.wait_ge(hT_ready, START + n + 1)
                pe.wait_ge(eo_ready, START + n - 1)
                for f in range(FC0):
                    mm = nc.tensor.matmul(down[:, par, 0:C], hT[:, par, f * P:(f + 1) * P],
                                          wd[:, bass.ds(e, 1), f, :], start=(f == 0), stop=(f == FC0 - 1))
                mm.then_inc(down_done, 1)

            def two_tiles(i):
                for off in (1, 2):
                    widen(tile(i, off))
                    turn_h(tile(i, off - 1))
                    turn(tile(i, off + 1))
                    narrow(tile(i, off - 1))

            pe.wait_ge(shared_loaded, 16 * LOADS)
            turn(tile(0, 0))
            widen(tile(0, 0))
            turn(tile(0, 1))
            with pe.Fori(0, STILES // 2 - 1) as i:
                two_tiles(i)
            pe.wait_ge(routed_loaded, 16 * LOADS * NE)
            with pe.Fori(STILES // 2 - 1, TILES // 2 - 1) as i:
                two_tiles(i)
            last = TILES // 2 - 1
            widen(tile(last, 1))
            turn_h(tile(last, 0))
            narrow(tile(last, 0))
            turn_h(tile(last, 1))
            narrow(tile(last, 1))

        @block.scalar
        def _(act):
            for s in (xT_ready, hT_ready, eo_ready):
                act.sem_inc(s, START)

            def copy_x(t):
                n, par, _ = t
                act.wait_ge(turned, START + n + 1)
                if not (isinstance(n, int) and n < 2):
                    act.wait_ge(up_done, n - 1)
                nc.scalar.activation(xT[:, par, :], tp[:, 0:C], ACT.Copy).then_inc(xT_ready, 1)

            def silu(t):
                n, par, _ = t
                act.wait_ge(h_ready, START + n - 1)
                act.wait_ge(gate_done, n + 1)
                nc.scalar.activation(sg[:, par, :], gate[:, par, :], ACT.Silu).then_inc(sg_ready, 1)

            def copy_h(t):
                n, par, _ = t
                act.wait_ge(down_done, START + n - 1)
                act.wait_ge(h_turned, START + n + 1)
                nc.scalar.activation(hT[:, par, :], htp[:, :], ACT.Copy).then_inc(hT_ready, 1)

            def copy_out(t):
                n, par, m = t
                if not (isinstance(m, int) and m == 0):
                    act.wait_ge(stored[par], 16 * m)
                act.wait_ge(down_done, START + n + 1)
                nc.scalar.activation(eo[:, par, :], down[:, par, 0:C], ACT.Copy).then_inc(eo_ready, 1)

            def two_tiles(i):
                for off in (1, 2):
                    silu(tile(i, off))
                    copy_h(tile(i, off - 1))
                    copy_x(tile(i, off + 1))
                    copy_out(tile(i, off - 1))

            copy_x(tile(0, 0))
            silu(tile(0, 0))
            copy_x(tile(0, 1))
            two_tiles(0)
            with act.Fori(1, TILES // 2 - 1) as i:
                two_tiles(i)
            last = TILES // 2 - 1
            silu(tile(last, 1))
            for off in (0, 1):
                copy_h(tile(last, off))
                copy_out(tile(last, off))

        @block.vector
        def _(dve):
            dve.sem_inc(h_ready, START)
            with dve.Fori(0, TILES // 2) as i:
                for off in range(2):
                    n, par, _ = tile(i, off)
                    dve.wait_ge(sg_ready, n + 1)
                    dve.wait_ge(up_done, n + 1)
                    dve.wait_ge(h_turned, START + n - 1)
                    nc.vector.tensor_tensor(h[:, par, :], sg[:, par, :], up[:, par, :], ALU.mult).then_inc(h_ready, 1)

        @block.gpsimd
        def _(pool):
            with pool.Fori(0, TILES // 2) as i:
                for off in range(2):
                    n, par, _ = tile(i, off)
                    rows = pool.snap(n * P)
                    pool.wait_ge(eo_ready, START + n + 1)
                    pool.dma_start(g["eo"][bass.ds(rows, P), :], eo[:, par, :]).then_inc(stored[par], 16)
            for par in range(2):
                pool.wait_ge(stored[par], 16 * (TILES // 2))


def phase_experts1(nc, a, g):
    with ExitStack() as ctx:
        sb, ps, sem = memory(nc, ctx, "experts1", g["used"])
        ident = g["ident"]
        w1, w2 = sb("w1", [P, 2, 2, F1]), sb("w2", [P, 2, FC1, C])
        b1, b2 = sb("b1", [P, NE, FC1]), sb("b2", [CT, NE, C])
        xs, xT = sb("xs", [CT, 2, CTILES, C]), sb("xT", [P, 2, 2, CAP])
        hT, eo = sb("hT", [P, FC1, CAP]), sb("eo", [CT, 2, CTILES, C])
        tp, hid, down = ps("tp", [P, 2, BANK]), ps("hid", [P, 2, BANK]), ps("down", [P, 2, BANK])
        bias_loaded = sem("bias_loaded")
        w_loaded, x_loaded, stored = ([sem(f"{n}{i}") for i in range(2)] for n in ("w_loaded", "x_loaded", "stored"))
        turned, xT_ready, hid_done, hT_ready = sem("turned"), sem("xT_ready"), sem("hid_done"), sem("hT_ready")
        down_done, eo_ready = sem("down_done"), sem("eo_ready")
        block = ctx.enter_context(nc.Block())

        def every(eng, body):
            for par in range(2):
                body(par, par, 0, False)
            with eng.Fori(1, NE // 2 - 1) as i:
                for par in range(2):
                    body(i * 2 + par, par, i, False)
            for par in range(2):
                body(NE - 2 + par, par, NE // 2 - 1, par == 1)

        @block.sync
        def _(sp):
            sp.dma_start(b1[:, :, :], a["L1_b1"]).then_inc(bias_loaded, 16)
            sp.dma_start(b2[:, :, :], a["L1_b2"].unsqueeze(0).broadcast_to([CT, NE, C])).then_inc(bias_loaded, 16)

            def load(e, par):
                rows = g["xs"][bass.ds(e * CAP, CAP), :].rearrange("(i p) c -> p i c", p=CT)
                sp.dma_start(xs[:, par, :, :], rows).then_inc(x_loaded[par], 16)
                one = a["L1_w1"][bass.ds(e, 1), :, :].rearrange("o (k p) f -> p (o k) f", p=P)
                sp.dma_start(w1[:, par, :, :], one).then_inc(w_loaded[par], 16)
                two = a["L1_w2"][bass.ds(e, 1), :, :].rearrange("o (f p) c -> p (o f) c", p=P)
                sp.dma_start(w2[:, par, :, :], two).then_inc(w_loaded[par], 16)

            load(0, 0)
            load(1, 1)
            with sp.Fori(0, NE // 2 - 1) as i:
                for par in range(2):
                    e = i * 2 + par
                    sp.wait_ge(down_done, START + CTILES * (e + 1))
                    load(e + 2, par)

        @block.tensor
        def _(pe):
            for s in (turned, down_done):
                pe.sem_inc(s, START)

            def turn(e, par, m):
                pe.wait_ge(x_loaded[par], 16 * (m + 1))
                pe.wait_ge(xT_ready, START + 2 * e)
                for k in range(2):
                    for i in range(CTILES):
                        mm = nc.tensor.transpose(tp[:, k, i * CT:(i + 1) * CT], xs[:, par, i, k * P:(k + 1) * P],
                                                 ident[0:CT, 0:CT])
                    mm.then_inc(turned, 1)

            def body(e, par, m, last):
                pe.wait_ge(w_loaded[par], 32 * (m + 1))
                pe.wait_ge(xT_ready, START + 2 * (e + 1))
                for f in range(FC1):
                    pe.wait_ge(hT_ready, START + FC1 * e + f - 1)
                    for k in range(2):
                        mm = nc.tensor.matmul(hid[:, f % 2, 0:CAP], w1[:, par, k, f * P:(f + 1) * P], xT[:, par, k, :],
                                              start=(k == 0), stop=(k == 1))
                    mm.then_inc(hid_done, 1)
                if not last:
                    turn(e + 1, 1 - par, m + par)
                pe.wait_ge(hT_ready, START + FC1 * (e + 1))
                for i in range(CTILES):
                    pe.wait_ge(eo_ready, START + CTILES * e + i - 1)
                    for f in range(FC1):
                        mm = nc.tensor.matmul(down[0:CT, i % 2, 0:C], hT[:, f, i * CT:(i + 1) * CT], w2[:, par, f, :],
                                              start=(f == 0), stop=(f == FC1 - 1))
                    mm.then_inc(down_done, 1)

            turn(0, 0, 0)
            every(pe, body)

        @block.scalar
        def _(act):
            act.sem_inc(hT_ready, START)
            act.wait_ge(bias_loaded, 32)

            def body(e, par, m, last):
                act.wait_ge(down_done, START + CTILES * e)
                for f in range(FC1):
                    bias = b1[:, e, f:f + 1] if isinstance(e, int) else b1[:, bass.ds(e, 1), f:f + 1]
                    act.wait_ge(hid_done, FC1 * e + f + 1)
                    nc.scalar.activation(hT[:, f, :], hid[:, f % 2, 0:CAP], ACT.Gelu,
                                         bias=bias).then_inc(hT_ready, 1)

            every(act, body)

        @block.vector
        def _(dve):
            for s in (xT_ready, eo_ready):
                dve.sem_inc(s, START)
            dve.wait_ge(bias_loaded, 32)

            def copy_x(e, par):
                for k in range(2):
                    dve.wait_ge(turned, START + 2 * e + k + 1)
                    nc.vector.tensor_copy(xT[:, par, k, :], tp[:, k, 0:CAP]).then_inc(xT_ready, 1)

            def body(e, par, m, last):
                if not last:
                    copy_x(e + 1, 1 - par)
                if not (isinstance(m, int) and m == 0):
                    dve.wait_ge(stored[par], 16 * m)
                for i in range(CTILES):
                    bias = b2[:, e, :] if isinstance(e, int) else b2[:, bass.ds(e, 1), :].rearrange("p o c -> p (o c)")
                    dve.wait_ge(down_done, START + CTILES * e + i + 1)
                    nc.vector.tensor_tensor(eo[:, par, i, :], down[0:CT, i % 2, 0:C], bias, ALU.add).then_inc(eo_ready, 1)

            copy_x(0, 0)
            every(dve, body)

        @block.gpsimd
        def _(pool):
            def body(e, par, m, last):
                rows = e * CAP if isinstance(e, int) else pool.snap(e * CAP)
                pool.wait_ge(eo_ready, START + CTILES * (e + 1))
                pool.dma_start(g["eo"][bass.ds(rows, CAP), :].rearrange("(i p) c -> p i c", p=CT),
                               eo[:, par, :, :]).then_inc(stored[par], 16)

            every(pool, body)
            for par in range(2):
                pool.wait_ge(stored[par], 16 * (NE // 2))


def phase_combine(nc, a, g, l):
    top, shared = TOPK[l], l == 0
    NB = 4
    with ExitStack() as ctx:
        sb, ps, sem = memory(nc, ctx, f"combine{l}", g["used"])
        T = g["T"]
        rows, srow = sb("rows", [TT, NB, top, C]), sb("srow", [TT, NB, C])
        part = sb("part", [TT, NB, C])
        fetched = [[sem(f"fetched{c}_{i}") for i in range(NB)] for c in range(top)]
        s_fetched = [sem(f"s_fetched{i}") for i in range(NB)]
        added, part_ready, summed = sem("added"), sem("part_ready"), sem("summed")
        block = ctx.enter_context(nc.Block())

        @block.gpsimd
        def _(pool):
            for t in range(NT):
                if t >= NB:
                    pool.wait_ge(added, t - NB + 1)
                for c in range(top):
                    if t >= NB:
                        pool.wait_ge(fetched[c][t % NB], 16 * (t // NB))
                    at = g["slot"][:, c if shared else 1, t:t + 1]
                    pool.indirect_dma_start(out=rows[:, t % NB, c, :], out_offset=None, in_=g["eo"][:, :],
                                            in_offset=bass.IndirectOffsetOnAxis(ap=at, axis=0)).then_inc(fetched[c][t % NB], 16)

        @block.sync
        def _(sp):
            if shared:
                for t in range(NT):
                    if t >= NB:
                        sp.wait_ge(added, t - NB + 1)
                    sp.dma_start(srow[:, t % NB, :], g["eo"][t * TT:(t + 1) * TT, :]).then_inc(s_fetched[t % NB], 16)

        @block.vector
        def _(dve):
            for t in range(NT):
                times = 16 * (t // NB + 1)
                src = T[:, t, :]
                for c in range(top):
                    last = c == top - 1
                    dve.wait_ge(fetched[c][t % NB], times)
                    if c:
                        dve.wait_ge(part_ready, t + 1)
                    dst = T[:, t, :] if last else part[:, t % NB, :]
                    ins = nc.vector.scalar_tensor_tensor(out=dst, in0=rows[:, t % NB, c, :], scalar=g["share"][:, c, t:t + 1],
                                                         in1=src, op0=ALU.mult, op1=ALU.add)
                    if not last:
                        ins.then_inc(part_ready, 1)
                        src = part[:, t % NB, :]
                    elif not shared:
                        ins.then_inc(added, 1)
                if shared:
                    ins.then_inc(summed, 1)
                    dve.wait_ge(summed, t + 1)
                    dve.wait_ge(s_fetched[t % NB], times)
                    nc.vector.tensor_tensor(T[:, t, :], T[:, t, :], srow[:, t % NB, :], ALU.add).then_inc(added, 1)


def phase_output(nc, a, g):
    with ExitStack() as ctx:
        sb, ps, sem = memory(nc, ctx, "output", g["used"])
        yc = sb("yc", [P, B * 2, HW])
        tp = ps("tp", [P, 4, BANK])
        turned, copied, stored = sem("turned"), sem("copied"), sem("stored")
        block = ctx.enter_context(nc.Block())

        @block.tensor
        def _(pe):
            for t in range(NT):
                if t >= 4:
                    pe.wait_ge(copied, t - 3)
                for k in range(2):
                    mm = nc.tensor.transpose(tp[:, t % 4, k * TT:(k + 1) * TT], g["T"][:, t, k * P:(k + 1) * P],
                                             g["ident"][0:TT, 0:TT])
                mm.then_inc(turned, 1)

        @block.vector
        def _(dve):
            for t in range(NT):
                b, j = divmod(t, TPB)
                dve.wait_ge(turned, t + 1)
                nc.vector.tensor_copy(yc[:, 2 * b:2 * b + 2, j * TT:(j + 1) * TT], tp[:, t % 4, 0:2 * TT].rearrange("p (k n) -> p k n", k=2)).then_inc(copied, 1)

        @block.sync
        def _(sp):
            for b in range(B):
                sp.wait_ge(copied, TPB * (b + 1))
                sp.dma_start(a["out"][b].rearrange("(k p) h w -> p k (h w)", p=P),
                             yc[:, 2 * b:2 * b + 2, :]).then_inc(stored, 16)
            sp.wait_ge(stored, 16 * B)


def build(nc, a):
    with ExitStack() as ctx:
        sb, ps, sem = memory(nc, ctx, "all", [])
        g = {"used": [], "T": sb("T", [TT, NT, C]), "ident": sb("ident", [P, P]), "fold": sb("fold", [P, DG]),
             "sel": sb("sel", [P, NG, P]), "mamba": []}
        for l in range(2):
            g["mamba"].append({n: sb(f"m{l}_{n}", s) for n, s in (
                ("wu", [P, 2, DI]), ("wz", [P, DI]), ("wdt", [P, DI]), ("wbc", [P, 2 * DS]),
                ("wout", [P, DM]), ("vec", [P, 3]), ("diag", [P, DI]), ("acol", [P, ITEMS]))})
        g["seq"] = nc.dram_tensor("seq_scratch", (NCH + 3, DM, CW), F32, kind="Internal").ap()
        g["scr"] = nc.dram_tensor("rep_scratch", (2, 2 * P + 2 * DS, TC), F32, kind="Internal").ap()
        g["xs"] = nc.dram_tensor("slot_rows", (SLOTS0, C), F32, kind="Internal").ap()
        g["eo"] = nc.dram_tensor("expert_rows", (SLOTS0, C), F32, kind="Internal").ap()
        g["slot"] = sb("slot", [TT, 2, NT], I32)
        g["share"] = sb("share", [TT, 2, NT])
        g["owner"] = sb("owner", [1, STILES + RTILES], I32)
        phase_setup(nc, a, g)
        for l in range(2):
            phase_sequence(nc, a, g, l)
            phase_mamba(nc, a, g, l)
            phase_route(nc, a, g, l)
            if l == 0:
                phase_experts0(nc, a, g)
            else:
                phase_experts1(nc, a, g)
            phase_combine(nc, a, g, l)
            if l == 0:
                nc.clear_and_free_semaphores(g["used"])
                g["used"].clear()
                nc.all_engine_barrier()
        phase_output(nc, a, g)


def layout(inputs):
    import numpy as np
    i = {n: np.asarray(v) for n, v in inputs.items()}
    out = {"x": i["x"]}
    for l in range(2):
        c = lambda n: i[f"L{l}_conv_{n}"]
        out[f"L{l}_winT"] = c("in_proj_w").T
        out[f"L{l}_cwT"] = c("conv_w").T
        out[f"L{l}_alog"] = c("A_log").reshape(NG, DG, NM, NS).transpose(3, 1, 0, 2).reshape(P, ITEMS)
        out[f"L{l}_xpw"] = c("x_proj_w")
        out[f"L{l}_xpT"] = c("x_proj_w").T
        out[f"L{l}_dtwT"] = c("dt_proj_w").T
        out[f"L{l}_woT"] = c("out_proj_w").T
        out[f"L{l}_vec"] = np.stack([c("conv_b"), c("dt_proj_b"), c("D")], axis=1)
        out[f"L{l}_token"] = c("global_token").reshape(DM, 1)
        out[f"L{l}_wrT"] = i[f"L{l}_ffn_router_w"].T
    for short, name in (("wg", "w_gate"), ("wu", "w_up"), ("wd", "w_down"), ("sg", "sg"), ("su", "su"), ("sd", "sd")):
        out[f"L0_{short}"] = i[f"L0_ffn_{name}"]
    out["L1_w1"], out["L1_w2"], out["L1_b2"] = i["L1_ffn_w1"], i["L1_ffn_w2"], i["L1_ffn_b2"]
    out["L1_b1"] = i["L1_ffn_b1"].reshape(NE, FC1, P).transpose(2, 0, 1)
    return {n: np.ascontiguousarray(v) for n, v in out.items()}


def kernel(**inputs):
    import concourse.bacc as bacc
    from concourse.bass_utils import run_bass_kernel_spmd

    nc = bacc.Bacc("TRN2", target_bir_lowering=False, num_devices=1)
    arrays = {f"in_{n}_dram": v for n, v in layout(inputs).items()}
    a = {n[3:-5]: nc.dram_tensor(n, v.shape, mybir.dt.from_np(v.dtype), kind="ExternalInput").ap()
         for n, v in arrays.items()}
    a["out"] = nc.dram_tensor("out_0_dram", (B, C, H, W), F32, kind="ExternalOutput").ap()
    build(nc, a)
    r = run_bass_kernel_spmd(nc, [arrays], core_ids=[0])
    return r.results[0]["out_0_dram"]
```

```python
from contextlib import ExitStack

import concourse.bass as bass
from concourse import mybir

F32 = mybir.dt.float32
I32 = mybir.dt.int32
U32 = mybir.dt.uint32
ALU = mybir.AluOpType
ACT = mybir.ActivationFunctionType
AX_X = mybir.AxisListType.X

P = 128
B, C, H, W = 4, 256, 24, 24
HW = H * W
TT = 96
ROWS = TT // W
TPB = HW // TT
NT = B * TPB
R = 2
DM, DI, DS, DC, DR = C // 4, 128, 16, 4, 4
LSEQ = HW * R * R + 1
BANK = 512
CPB = 5
NCH = B * CPB
TC = 462
PAD = DC - 1
LPAD = PAD + CPB * TC
CW = TC + PAD
NG, DG = 4, 32
NM, NS = 4, 4
ITEMS = NG * NM
REP_ROWS = 2 * NG + 2 * NM
UBUFS = 4
BANKS = 5
STATE_BANK = [i % BANKS for i in range(ITEMS - 1)] + [2]
STATE_GAP = [min(n for n in range(1, ITEMS) if STATE_BANK[i - n] == STATE_BANK[i]) for i in range(ITEMS)]
AT_SILU, AT_EXP, AT_ONE, AT_LN, AT_BC, AT_DT, AT_LR, AT_DT_SUM, AT_DTU = 6, 10, 11, 15, 13, 5, 1, 3, 5
START = 6
NE, TOPK = 8, (2, 1)
F0, F1 = 512, 1024
FC0, FC1 = F0 // P, F1 // P
STILES = B * HW // P
MAXT = B * HW // P
RTILES = TOPK[0] * B * HW // P + NE
SLOTS0 = (STILES + RTILES) * P
CAP = -(-3 * B * HW // (2 * NE))
CT = 108
CTILES = CAP // CT
assert CTILES * CT == CAP and RTILES % 2 == 0 and STILES % 2 == 0 and B * HW % P == 0
assert NE * CAP + B * HW <= SLOTS0
assert NS * DG == P and CPB * TC >= LSEQ and NG * DG == DI and NM * NS == DS and TC <= BANK


def memory(nc, ctx, phase, used):

    def sb(name, shape, dt=F32):
        return ctx.enter_context(nc.sbuf_tensor(f"{phase}_{name}", shape, dt))

    def ps(name, shape, dt=F32):
        return ctx.enter_context(nc.psum_tensor(f"{phase}_{name}", shape, dt))

    def sem(name):
        used.append(nc.alloc_semaphore(f"{phase}_{name}"))
        return used[-1]

    return sb, ps, sem


def phase_setup(nc, a, g):
    with ExitStack() as ctx:
        sb, ps, sem = memory(nc, ctx, "setup", g["used"])
        xc = sb("xc", [P, B * 2, HW])
        raw = [{n: sb(f"raw{l}_{n}", s) for n, s in (
            ("winT", [P, DI]), ("cw", [P, 2, DI]), ("alog", [P, ITEMS]),
            ("wxT", [DR, DI]), ("wdtT", [DR, DI]))} for l in range(2)]
        zero = sb("zero", [P, 4 * C])
        tp = ps("tp", [P, 4, BANK])
        wp = ps("wp", [P, 2, BANK])
        zeroed, zero_stored = sem("zeroed"), sem("zero_stored")
        x_loaded, w_loaded = sem("x_loaded"), sem("w_loaded")
        ident_ready, x_turned, t_copied = sem("ident_ready"), sem("x_turned"), sem("t_copied")
        fold_ready, fold_multiplied = sem("fold_ready"), sem("fold_multiplied")
        pool_steps, exp_ready, act_copied = sem("pool_steps"), sem("exp_ready"), sem("act_copied")
        wz_zeroed, sel_ready, vec_steps = sem("wz_zeroed"), sem("sel_ready"), sem("vec_steps")
        block = ctx.enter_context(nc.Block())
        NW = 13

        @block.sync
        def _(sp):
            for b in range(B):
                sp.dma_start(xc[:, 2 * b:2 * b + 2, :],
                             a["x"][b].rearrange("(k p) h w -> p k (h w)", p=P)).then_inc(x_loaded, 16)
            sp.wait_ge(wz_zeroed, 2)
            for l in range(2):
                w, m = raw[l], g["mamba"][l]
                for s in range(2):
                    sp.dma_start(w["winT"][s * DM:(s + 1) * DM, :], a[f"L{l}_winT"][:, 0:DI]).then_inc(w_loaded, 16)
                    for pair in range(2):
                        tap = a[f"L{l}_cwT"][2 * pair + s:2 * pair + s + 1, :].broadcast_to([DM, DI])
                        sp.dma_start(w["cw"][s * DM:(s + 1) * DM, pair, :], tap).then_inc(w_loaded, 16)
                sp.dma_start(m["wz"][DM:P, :], a[f"L{l}_winT"][:, DI:2 * DI]).then_inc(w_loaded, 16)
                sp.dma_start(w["alog"][:, :], a[f"L{l}_alog"]).then_inc(w_loaded, 16)
                sp.dma_start(w["wxT"][:, :], a[f"L{l}_xpw"][0:DR, :]).then_inc(w_loaded, 16)
                sp.dma_start(w["wdtT"][:, :], a[f"L{l}_dtwT"]).then_inc(w_loaded, 16)
                sp.dma_start(m["wbc"][:, :], a[f"L{l}_xpT"][:, DR:DR + 2 * DS]).then_inc(w_loaded, 16)
                sp.dma_start(m["wout"][:, :], a[f"L{l}_woT"]).then_inc(w_loaded, 16)
                sp.dma_start(m["vec"][:, :], a[f"L{l}_vec"]).then_inc(w_loaded, 16)

            sp.wait_ge(zeroed, 1)
            routed = g["xs"][B * HW:SLOTS0, :].rearrange("(n p r) c -> n p (r c)", p=P, r=4)
            for n in range(routed.shape[0]):
                sp.dma_start(routed[n], zero[:, :]).then_inc(zero_stored, 16)
            sp.wait_ge(zero_stored, 16 * routed.shape[0])

        @block.gpsimd
        def _(pool):
            pool.memset(zero[:, :], 0.0).then_inc(zeroed, 1)
            for l in range(2):
                pool.memset(g["mamba"][l]["wz"][0:DM, :], 0.0).then_inc(wz_zeroed, 1)
            pool.memset(g["ident"][:, :], 0.0).then_inc(pool_steps, 1)
            pool.memset(g["fold"][:, :], 0.0).then_inc(pool_steps, 1)
            pool.memset(g["sel"][:, :, :], 0.0).then_inc(pool_steps, 1)
            pool.wait_ge(pool_steps, 3)
            pool.affine_select(out=g["ident"][:, :], in_=g["ident"][:, :], compare_op=ALU.not_equal, fill=1.0,
                               base=0, pattern=[[-1, P]], channel_multiplier=1).then_inc(ident_ready, 1)
            for s in range(NS):
                pool.affine_select(out=g["fold"][:, :], in_=g["fold"][:, :], compare_op=ALU.not_equal, fill=1.0,
                                   base=-DG * s, pattern=[[-1, DG]], channel_multiplier=1).then_inc(pool_steps, 1)
                pool.wait_ge(pool_steps, 4 + s)
            for k in range(NG):
                pool.tensor_copy(g["sel"][:, k, DG * k:DG * k + DG], g["fold"][:, :]).then_inc(sel_ready, 1)

        @block.tensor
        def _(pe):
            pe.wait_ge(ident_ready, 1)
            pe.wait_ge(x_loaded, 16 * B)
            for t in range(NT):
                if t >= 4:
                    pe.wait_ge(t_copied, t - 3)
                b, j = divmod(t, TPB)
                for k in range(2):
                    mm = nc.tensor.transpose(tp[0:TT, t % 4, k * P:(k + 1) * P],
                                             xc[:, 2 * b + k, j * TT:(j + 1) * TT], g["ident"][:, :])
                mm.then_inc(x_turned, 1)
            pe.wait_ge(w_loaded, 16 * 2 * NW)
            for l in range(2):
                nc.tensor.matmul(wp[:, l, 0:DI], raw[l]["wxT"][:, :], raw[l]["wdtT"][:, :],
                                 start=True, stop=True).then_inc(fold_multiplied, 1)

        @block.scalar
        def _(act):
            act.wait_ge(w_loaded, 16 * 2 * NW)
            for l in range(2):
                nc.scalar.activation(g["mamba"][l]["acol"][:, :], raw[l]["alog"][:, :], ACT.Exp).then_inc(exp_ready, 1)
                act.wait_ge(fold_multiplied, l + 1)
                nc.scalar.activation(g["mamba"][l]["wdt"][:, :], wp[:, l, 0:DI], ACT.Copy).then_inc(act_copied, 1)

        @block.vector
        def _(dve):
            for t in range(NT):
                dve.wait_ge(x_turned, t + 1)
                nc.vector.tensor_copy(g["T"][:, t, :], tp[0:TT, t % 4, 0:C]).then_inc(t_copied, 1)
            dve.wait_ge(w_loaded, 16 * 2 * NW)
            for l in range(2):
                dve.wait_ge(exp_ready, l + 1)
                m = g["mamba"][l]
                nc.vector.tensor_scalar(m["acol"][:, :], m["acol"][:, :], -1.0, None, ALU.mult).then_inc(vec_steps, 1)
                nc.vector.tensor_scalar(m["diag"][:, :], g["ident"][:, :], m["vec"][:, 2:3], None, ALU.mult).then_inc(vec_steps, 1)
                for pair in range(2):
                    nc.vector.tensor_tensor(m["wu"][:, pair, :], raw[l]["winT"][:, :], raw[l]["cw"][:, pair, :],
                                            ALU.mult).then_inc(vec_steps, 1)


def layernorm_stats(nc, dve, T, stats, mv, steps):
    for t in range(NT):
        nc.vector.bn_stats(stats[:, t, :], T[:, t, :]).then_inc(steps, 1)
    dve.wait_ge(steps, NT)
    for t in range(NT):
        nc.vector.bn_aggr(mv[:, t, :], stats[:, t, :]).then_inc(steps, 1)


def phase_sequence(nc, a, g, l):
    with ExitStack() as ctx:
        sb, ps, sem = memory(nc, ctx, f"seq{l}", g["used"])
        T = g["T"]
        stats, mv = sb("stats", [TT, NT, 6]), sb("mv", [TT, NT, 2])
        vare, rstd, mhalf = sb("vare", [TT, NT]), sb("rstd", [TT, NT]), sb("mhalf", [TT, NT])
        tn = sb("tn", [TT, 2, C])
        sq = sb("sq", [DM, B + 1, LPAD])
        token = sb("token", [DM, 1])
        tp = ps("tp", [DM, 2, 512])
        stat_steps, vare_ready, half_ready, rstd_ready = sem("stat_steps"), sem("vare_ready"), sem("half_ready"), sem("rstd_ready")
        tn_ready, turned, placed = sem("tn_ready"), sem("turned"), sem("placed")
        padded, token_loaded, stored = sem("padded"), sem("token_loaded"), sem("stored")
        block = ctx.enter_context(nc.Block())

        @block.gpsimd
        def _(pool):
            pool.memset(mhalf[:, :], -0.5).then_inc(half_ready, 1)
            pool.memset(sq[:, 0:B, 0:PAD], 0.0).then_inc(padded, 1)
            pool.memset(sq[:, 0:B, PAD + LSEQ:LPAD], 0.0).then_inc(padded, 1)
            pool.memset(sq[:, B, 0:CW], 0.0).then_inc(padded, 1)
            pool.wait_ge(token_loaded, 16)
            pool.tensor_copy(sq[:, 0:B, PAD:PAD + 1], token[:, :].unsqueeze(1).broadcast_to([DM, B, 1])).then_inc(padded, 1)
            pool.wait_ge(half_ready, 1)
            pool.wait_ge(vare_ready, 1)
            pool.tensor_tensor(rstd[:, :], vare[:, :], mhalf[:, :], ALU.pow).then_inc(rstd_ready, 1)

        @block.vector
        def _(dve):
            layernorm_stats(nc, dve, T, stats, mv, stat_steps)
            dve.wait_ge(stat_steps, 2 * NT)
            nc.vector.tensor_scalar(vare[:, :], mv[:, :, 1], 1e-6, None, ALU.add).then_inc(vare_ready, 1)
            dve.wait_ge(rstd_ready, 1)
            for t in range(NT):
                if t >= 2:
                    dve.wait_ge(turned, t - 1)
                nc.vector.tensor_scalar(tn[:, t % 2, :], T[:, t, :], mv[:, t, 0:1], rstd[:, t:t + 1],
                                        ALU.subtract, ALU.mult).then_inc(tn_ready, 1)

        @block.tensor
        def _(pe):
            for t in range(NT):
                pe.wait_ge(tn_ready, t + 1)
                if t >= 2:
                    pe.wait_ge(placed, 2 * (t - 1))
                planes = tn[:, t % 2, :].rearrange("p (c q) -> p q c", q=R * R)
                for q in range(R * R):
                    mm = nc.tensor.transpose(tp[:, t % 2, q * TT:(q + 1) * TT], planes[:, q, :], g["ident"][0:TT, 0:TT])
                mm.then_inc(turned, 1)

        @block.scalar
        def _(act):
            for t in range(NT):
                b, j = divmod(t, TPB)
                act.wait_ge(turned, t + 1)
                at = PAD + 1 + j * TT * R * R
                dst = sq[:, b, at:at + TT * R * R].rearrange("c (h i w q) -> c i h w q", h=ROWS, i=R, w=W, q=R)
                src = tp[:, t % 2, 0:TT * R * R].rearrange("c (i q h w) -> c i h w q", i=R, q=R, h=ROWS, w=W)
                for i in range(R):
                    nc.scalar.activation(dst[:, i], src[:, i], ACT.Copy).then_inc(placed, 1)

        @block.sync
        def _(sp):
            sp.dma_start(token[:, :], a[f"L{l}_token"]).then_inc(token_loaded, 16)
            sp.wait_ge(padded, 4)
            for k in range(NCH, NCH + 3):
                sp.dma_start(g["seq"][k], sq[:, B, 0:CW]).then_inc(stored, 16)
            for b in range(B):
                sp.wait_ge(placed, 2 * TPB * (b + 1))
                for c in range(CPB):
                    sp.dma_start(g["seq"][CPB * b + c], sq[:, b, c * TC:c * TC + CW]).then_inc(stored, 16)
            sp.wait_ge(stored, 16 * (NCH + 3))


def phase_mamba(nc, a, g, l):
    with ExitStack() as ctx:
        sb, ps, sem = memory(nc, ctx, f"mamba{l}", g["used"])
        T, m, sel = g["T"], g["mamba"][l], g["sel"]
        xs = sb("xs", [P, CW - 1])
        u, sz = sb("u", [P, UBUFS, TC]), sb("sz", [P, UBUFS, TC])
        ab, ex, w1, ln, rx = sb("ab", [P, TC]), sb("ex", [P, TC]), sb("w1", [P, TC]), sb("ln", [P, TC]), sb("rx", [P, TC])
        rr, lr = sb("rr", [P, TC]), sb("lr", [P, TC])
        dd = sb("dd", [P, 2, TC])
        bc = sb("bc", [2 * DS, TC])
        rep = sb("rep", [P, 2 * REP_ROWS, TC])
        dbu, hc = sb("dbu", [P, 4, TC]), sb("hc", [P, 4, TC])
        carry = sb("carry", [P, ITEMS])
        y = sb("y", [P, NCH * TC])
        yp = sb("yp", [P, 2, R * R, HW])
        stats = sb("stats", [TT, NT, 6])
        state = ps("state", [P, BANKS, BANK])
        ysum, front = ps("ysum", [P, BANK]), ps("front", [P, 2, BANK])

        xs_loaded, rep_loaded, bc_stored, dt_stored = sem("xs_loaded"), sem("rep_loaded"), sem("bc_stored"), sem("dt_stored")
        front_mm, front_act, front_dve, front_pool = sem("front_mm"), sem("front_act"), sem("front_dve"), sem("front_pool")
        decay_ready, dbu_ready, scan_done, carry_done = sem("decay_ready"), sem("dbu_ready"), sem("scan_done"), sem("carry_done")
        hc_ready, hc_summed, carry_zeroed = sem("hc_ready"), sem("hc_summed"), sem("carry_zeroed")
        y_ready, projected, added = sem("y_ready"), sem("projected"), sem("added")
        unshuffled, stat_steps = sem("unshuffled"), sem("stat_steps")
        MM_U, MM_Z, MM_DT, MM_BC, MMS = 1, 2, 3, 4, 4
        A_U, A_Z, A_ABS, A_RELU, A_EXP, A_ONE, A_BC, A_LN, ACTS = 1, 2, 3, 4, 5, 6, 7, 8, 8
        G_LR, G_DT, G_DTU, POOLS = 1, 2, 3, 3
        REPS = 2 * NS
        block = ctx.enter_context(nc.Block())

        def chunk_of(eng, tile, k):
            if isinstance(k, int):
                return tile[:, k % UBUFS, :]
            return tile[:, bass.ds(eng.snap(k % UBUFS), 1), :]

        @block.sync
        def _(sp):
            def load_xs(k):
                for s in range(2):
                    src = g["seq"][bass.ds(k, 1), :, s:s + CW - 1].rearrange("o c n -> (o c) n")
                    sp.dma_start(xs[s * DM:(s + 1) * DM, :], src).then_inc(xs_loaded, 16)

            def half(k):
                return k % 2 if isinstance(k, int) else sp.snap(k % 2)

            def bc_scratch(k):
                return g["bc_rows"][bass.ds(half(k), 1), :, :]

            def rep_row(k):
                return k % 2 * REP_ROWS if isinstance(k, int) else sp.snap(k % 2 * REP_ROWS)

            def store_bc(k):
                rows = bc_scratch(k).rearrange("o w n -> (o w) n")
                sp.wait_ge(front_act, START + ACTS * k + A_BC)
                sp.dma_start(rows, bc[:, :]).then_inc(bc_stored, 16)

            def store_dt(k):
                rows = g["dt_rows"].rearrange("(w p) n -> p w n", p=P)
                sp.wait_ge(front_pool, START + POOLS * k + G_DTU)
                sp.dma_start(rows, dd[:, :, :]).then_inc(dt_stored, 16)

            def replicate_bc(k):
                rows, row = bc_scratch(k), rep_row(k)
                sp.wait_ge(bc_stored, 16 * (k + 1))
                for s in range(NS):
                    src = rows.rearrange("o (w s) n -> s (o w) n", s=NS)[s:s + 1]
                    sp.dma_start(rep[s * DG:(s + 1) * DG, bass.ds(row + 2 * NG, 2 * NM), :],
                                 src.broadcast_to([DG, 2 * NM, TC])).then_inc(rep_loaded, 16)

            def replicate_dt(k):
                row = rep_row(k)
                src = g["dt_rows"].rearrange("(w d) n -> d w n", d=DG)
                sp.wait_ge(dt_stored, 16 * (k + 1))
                for s in range(NS):
                    sp.dma_start(rep[s * DG:(s + 1) * DG, bass.ds(row, 2 * NG), :], src).then_inc(rep_loaded, 16)

            replicas = sp.alloc_register(f"replicas{l}")
            load_xs(0)
            sp.wait_ge(front_mm, START + MM_Z)
            load_xs(1)
            store_bc(0)
            replicate_bc(0)
            store_dt(0)
            replicate_dt(0)
            sp.wait_ge(front_mm, START + MMS + MM_Z)
            load_xs(2)
            store_bc(1)
            with sp.Fori(0, NCH) as k:
                sp.reg_mul(replicas, k, 16 * REPS)
                sp.reg_add(replicas, replicas, 16 * REPS)
                replicas_before = sp.snap(replicas)
                items_before = START + ITEMS * k
                sp.wait_ge(decay_ready, items_before)
                sp.wait_ge(dbu_ready, items_before)
                sp.wait_ge(hc_ready, items_before)
                sp.wait_ge(rep_loaded, replicas_before)
                replicate_bc(k + 1)
                store_dt(k + 1)
                replicate_dt(k + 1)
                sp.wait_ge(front_mm, START + MMS * (k + 2) + MM_Z)
                load_xs(k + 3)
                store_bc(k + 2)
            sp.wait_ge(rep_loaded, 16 * REPS * (NCH + 1))
            sp.wait_ge(bc_stored, 16 * (NCH + 2))
            sp.wait_ge(xs_loaded, 32 * (NCH + 3))

        @block.tensor
        def _(pe):
            for s in (front_mm, hc_summed, projected):
                pe.sem_inc(s, START)

            def prep_u(k):
                pe.wait_ge(xs_loaded, 32 * (k + 1))
                pe.wait_ge(front_act, START + ACTS * k)
                nc.tensor.matmul(front[:, 0, 0:TC], m["wu"][:, 0, :], xs[:, 0:TC], start=True, stop=False)
                nc.tensor.matmul(front[:, 0, 0:TC], m["wu"][:, 1, :], xs[:, 2:2 + TC],
                                 start=False, stop=True).then_inc(front_mm, 1)

            def prep_z(k):
                nc.tensor.matmul(front[:, 1, 0:TC], m["wz"][:, :], xs[:, 2:2 + TC],
                                 start=True, stop=True).then_inc(front_mm, 1)

            def prep_dt(k):
                pe.wait_ge(front_act, START + ACTS * k + A_Z)
                nc.tensor.matmul(front[:, 0, 0:TC], m["wdt"][:, :], chunk_of(pe, u, k),
                                 start=True, stop=True).then_inc(front_mm, 1)

            def prep_bc(k):
                nc.tensor.matmul(front[0:2 * DS, 1, 0:TC], m["wbc"][:, :], chunk_of(pe, u, k),
                                 start=True, stop=True).then_inc(front_mm, 1)

            for k in range(2):
                prep_u(k)
                prep_z(k)
                prep_dt(k)
                prep_bc(k)
            with pe.Fori(0, NCH) as k:
                prep_u(k + 2)
                prep_z(k + 2)
                pe.wait_ge(y_ready, START + k)
                nc.tensor.matmul(ysum[:, 0:TC], m["diag"][:, :], chunk_of(pe, u, k), start=True, stop=False)
                for i in range(ITEMS):
                    pe.wait_ge(hc_ready, START + ITEMS * k + i + 1)
                    nc.tensor.matmul(ysum[:, 0:TC], sel[:, i // NM, :], hc[:, i % 4, :],
                                     start=False, stop=(i == ITEMS - 1)).then_inc(hc_summed, 1)
                    if i == AT_DT:
                        prep_dt(k + 2)
                    if i == AT_DT + 1:
                        prep_bc(k + 2)
            pe.wait_ge(front_act, START + ACTS * (NCH + 2))
            for t in range(NT):
                b, j = divmod(t, TPB)
                pe.wait_ge(unshuffled, R * (b + 1))
                pe.wait_ge(added, START + t - 1)
                out = front[0:TT, t % 2, 0:C].rearrange("p (c q) -> p q c", q=R * R)
                for q in range(R * R):
                    mm = nc.tensor.matmul(out[:, q, :], yp[:, b % 2, q, j * TT:(j + 1) * TT], m["wout"][:, :],
                                          start=True, stop=True, skip_group_check=True)
                mm.then_inc(projected, 1)

        def planes(b, i):
            at = b * CPB * TC + 1
            src = y[:, at:at + HW * R * R].rearrange("d (h i w q) -> d i q h w", h=H, i=R, w=W, q=R)[:, i]
            return src, yp[:, b % 2, R * i:R * i + R, :].rearrange("d q (h w) -> d q h w", h=H)

        @block.scalar
        def _(act):
            act.sem_inc(front_act, START)
            act.sem_inc(decay_ready, START)
            at = act.alloc_register(f"act_row{l}")
            conv_b, dt_b = m["vec"][:, 0:1], m["vec"][:, 1:2]

            def out_of(tile, k):
                if isinstance(k, int):
                    return tile[:, k % UBUFS, :]
                act.reg_add(at, act.snap(k % UBUFS), 0)
                return tile[:, bass.ds(act.snap(at), 1), :]

            def prep_silu(k):
                act.wait_ge(front_mm, START + MMS * k + MM_Z)
                act.wait_ge(y_ready, START + k - UBUFS + 1)
                nc.scalar.activation(out_of(u, k), front[:, 0, 0:TC], ACT.Silu, bias=conv_b).then_inc(front_act, 1)
                nc.scalar.activation(out_of(sz, k), front[:, 1, 0:TC], ACT.Silu).then_inc(front_act, 1)

            def prep_exp(k):
                act.wait_ge(front_mm, START + MMS * k + MM_DT)
                act.wait_ge(front_pool, START + POOLS * k)
                nc.scalar.activation(ab[:, :], front[:, 0, 0:TC], ACT.Abs, bias=dt_b).then_inc(front_act, 1)
                nc.scalar.activation(rx[:, :], front[:, 0, 0:TC], ACT.Relu, bias=dt_b).then_inc(front_act, 1)
                act.wait_ge(front_act, START + ACTS * k + A_ABS)
                nc.scalar.activation(ex[:, :], ab[:, :], ACT.Exp, scale=-1.0).then_inc(front_act, 1)

            def prep_one(k):
                act.wait_ge(front_act, START + ACTS * k + A_EXP)
                nc.scalar.activation(w1[:, :], ex[:, :], ACT.Copy, bias=1.0).then_inc(front_act, 1)

            def prep_ln(k):
                nc.scalar.activation(ln[:, :], ex[:, :], ACT.Ln, bias=1.0).then_inc(front_act, 1)

            def prep_bc(k):
                act.wait_ge(front_mm, START + MMS * k + MM_BC)
                if not (isinstance(k, int) and k == 0):
                    act.wait_ge(bc_stored, 16 * k)
                nc.scalar.activation(bc[:, :], front[0:2 * DS, 1, 0:TC], ACT.Copy).then_inc(front_act, 1)

            for k in range(2):
                prep_silu(k)
                prep_exp(k)
                prep_one(k)
                prep_bc(k)
                prep_ln(k)
            with act.Fori(0, NCH // 2) as pair:
                for par in range(2):
                    k = pair * 2 + par
                    act.wait_ge(rep_loaded, 16 * REPS * (k + 1))
                    for i in range(ITEMS):
                        act.wait_ge(carry_done, START + ITEMS * k + i - STATE_GAP[i] + 1)
                        nc.scalar.activation(state[:, STATE_BANK[i], 0:TC], rep[:, par * REP_ROWS + i // NM, :], ACT.Exp,
                                             scale=m["acol"][:, i:i + 1]).then_inc(decay_ready, 1)
                        if i == AT_SILU:
                            prep_silu(k + 2)
                        if i == AT_EXP:
                            prep_exp(k + 2)
                        if i == AT_ONE:
                            prep_one(k + 2)
                        if i == AT_BC:
                            prep_bc(k + 2)
                        if i == AT_LN:
                            prep_ln(k + 2)
            for b in range(B):
                act.wait_ge(y_ready, START + NCH)
                if b >= 2:
                    act.wait_ge(projected, START + TPB * (b - 1))
                for i in range(R):
                    src, dst = planes(b, i)
                    nc.scalar.activation(dst, src, ACT.Copy).then_inc(unshuffled, 1)

        @block.gpsimd
        def _(pool):
            pool.sem_inc(dbu_ready, START)
            pool.sem_inc(front_pool, START)
            at = pool.alloc_register(f"pool_row{l}")

            def prep(k, step):
                done = START + POOLS * k
                if step == G_LR:
                    pool.wait_ge(front_act, START + ACTS * k + A_LN)
                    pool.wait_ge(front_dve, START + k + 1)
                    pool.tensor_tensor(lr[:, :], ln[:, :], rr[:, :], ALU.subtract).then_inc(front_pool, 1)
                if step == G_DT:
                    if not (isinstance(k, int) and k == 0):
                        pool.wait_ge(dt_stored, 16 * k)
                    pool.wait_ge(front_pool, done + G_LR)
                    pool.tensor_tensor(dd[:, 0, :], lr[:, :], rx[:, :], ALU.add).then_inc(front_pool, 1)
                if step == G_DTU:
                    pool.wait_ge(front_pool, done + G_DT)
                    if isinstance(k, int):
                        u_k = u[:, k % UBUFS, :]
                    else:
                        pool.reg_add(at, pool.snap(k % UBUFS), 0)
                        u_k = u[:, bass.ds(pool.snap(at), 1), :]
                    pool.tensor_tensor(dd[:, 1, :], dd[:, 0, :], u_k, ALU.mult).then_inc(front_pool, 1)

            for step in (G_LR, G_DT, G_DTU):
                prep(0, step)
            with pool.Fori(0, NCH // 2) as pair:
                for par in range(2):
                    k = pair * 2 + par
                    first = par * REP_ROWS
                    pool.wait_ge(rep_loaded, 16 * REPS * (k + 1))
                    for i in range(ITEMS):
                        pool.wait_ge(scan_done, START + ITEMS * k + i - 3)
                        pool.tensor_tensor(dbu[:, i % 4, :], rep[:, first + NG + i // NM, :], rep[:, first + 2 * NG + i % NM, :],
                                           ALU.mult).then_inc(dbu_ready, 1)
                        for step, after in ((G_LR, AT_LR), (G_DT, AT_DT_SUM), (G_DTU, AT_DTU)):
                            if i == after:
                                prep(k + 1, step)

        @block.vector
        def _(dve):
            for s in (scan_done, carry_done, hc_ready, front_dve, y_ready, added):
                dve.sem_inc(s, START)

            def prep(k):
                dve.wait_ge(front_act, START + ACTS * k + A_ONE)
                dve.wait_ge(front_pool, START + POOLS * k)
                nc.vector.scalar_tensor_tensor(out=rr[:, :], in0=w1[:, :], scalar=1.0, in1=ex[:, :],
                                               op0=ALU.subtract, op1=ALU.subtract).then_inc(front_dve, 1)

            for k in range(2):
                prep(k)
            with dve.Fori(0, B) as b:
                dve.wait_ge(carry_done, START + ITEMS * CPB * b)
                nc.vector.memset(carry[:, :], 0.0).then_inc(carry_zeroed, 1)
                with dve.Fori(0, CPB) as c:
                    k = dve.snap(b * CPB + c)
                    dve.wait_ge(carry_zeroed, b + 1)
                    dve.wait_ge(rep_loaded, 16 * REPS * (k + 1))
                    c_rows = dve.snap(k % 2 * REP_ROWS)

                    def read_out(i):
                        dve.wait_ge(scan_done, START + ITEMS * k + i + 1)
                        dve.wait_ge(hc_summed, START + ITEMS * k + i - 3)
                        nc.vector.tensor_tensor(hc[:, i % 4, :], state[:, STATE_BANK[i], 0:TC],
                                                rep[:, bass.ds(c_rows + 3 * NG + i % NM, 1), :],
                                                ALU.mult).then_inc(hc_ready, 1)
                        nc.vector.tensor_copy(carry[:, i:i + 1], state[:, STATE_BANK[i], TC - 1:TC]).then_inc(carry_done, 1)

                    for i in range(ITEMS):
                        n = START + ITEMS * k + i
                        dve.wait_ge(decay_ready, n + 1)
                        dve.wait_ge(dbu_ready, n + 1)
                        bank = state[:, STATE_BANK[i], 0:TC]
                        nc.vector.tensor_tensor_scan(bank, bank, dbu[:, i % 4, :],
                                                     carry[:, i:i + 1], ALU.mult, ALU.add).then_inc(scan_done, 1)
                        if i > 0:
                            read_out(i - 1)
                    read_out(ITEMS - 1)
                    prep(k + 2)
                    dve.wait_ge(hc_summed, START + ITEMS * (k + 1))
                    nc.vector.tensor_tensor(y[:, bass.ds(k * TC, TC)], ysum[:, 0:TC], chunk_of(dve, sz, k),
                                            ALU.mult).then_inc(y_ready, 1)
            for t in range(NT):
                dve.wait_ge(projected, START + t + 1)
                nc.vector.tensor_tensor(T[:, t, :], T[:, t, :], front[0:TT, t % 2, 0:C], ALU.add).then_inc(added, 1)
                if t >= 1:
                    dve.wait_ge(added, START + t)
                    nc.vector.bn_stats(stats[:, t - 1, :], T[:, t - 1, :]).then_inc(stat_steps, 1)
                if t >= 2:
                    dve.wait_ge(stat_steps, 2 * t - 3)
                    nc.vector.bn_aggr(g["mv"][:, t - 2, :], stats[:, t - 2, :]).then_inc(stat_steps, 1)
            dve.wait_ge(added, START + NT)
            nc.vector.bn_stats(stats[:, NT - 1, :], T[:, NT - 1, :]).then_inc(stat_steps, 1)
            dve.wait_ge(stat_steps, 2 * NT - 2)
            for t in (NT - 2, NT - 1):
                nc.vector.bn_aggr(g["mv"][:, t, :], stats[:, t, :]).then_inc(stat_steps, 1)


def phase_route(nc, a, g, l, prefetch):
    top = TOPK[l]
    with ExitStack() as ctx:
        sb, ps, sem = memory(nc, ctx, f"route{l}", g["used"])
        T, ident = g["T"], g["ident"]
        mv = g["mv"]
        vare, rstd, mhalf = sb("vare", [TT, NT]), sb("rstd", [TT, NT]), sb("mhalf", [TT, NT])
        xn = g["xn"]
        xT = sb("xT", [P, 2, 2 * TT])
        wr = sb("wr", [P, 2, NE])
        lg, best, which = sb("lg", [TT, NT, NE]), sb("best", [TT, NT, NE]), sb("which", [TT, NT, NE], U32)
        whichf = sb("whichf", [TT, 2, NT])
        eid = sb("eid", [TT, NE, NT])
        one = sb("one", [TT, 2, NE, NT])
        both, picked = sb("both", [TT, NE, NT]), sb("picked", [TT, NE, NT])
        before, ones = sb("before", [TT, TT]), sb("ones", [TT, TT])
        tot, cum, prev = sb("tot", [TT, NE, NT]), sb("cum", [TT, NE * NT]), sb("prev", [TT, NE, NT])
        pos, count = sb("pos", [TT, NE, NT]), sb("count", [TT, NE])
        steps128, over = sb("steps128", [TT, NE, MAXT]), sb("over", [TT, NE, MAXT])
        tiles, ends, first = sb("tiles", [TT, NE]), sb("ends", [TT, NE]), sb("first", [TT, NE])
        slotf, kept = sb("slotf", [TT, 2, NT]), sb("kept", [TT, NT])
        token, base = sb("token", [TT, NT]), sb("base", [TT, NT])
        tile_id, passed, owner = sb("tile_id", [1, RTILES, NE]), sb("passed", [1, RTILES, NE]), sb("owner", [1, RTILES])
        dif, ee, den, prob = sb("dif", [TT, NT, NE]), sb("ee", [TT, NT, NE]), sb("den", [TT, NT]), sb("prob", [TT, NT])
        tp, lgp = ps("tp", [P, 2, BANK]), ps("lgp", [TT, BANK])
        rank_ps, tot_ps = ps("rank", [TT, BANK]), ps("tot_ps", [TT, BANK])
        top_steps, vare_ready, rstd_ready = sem("top_steps"), sem("vare_ready"), sem("rstd_ready")
        xn_ready, turned, xT_ready, scored = sem("xn_ready"), sem("turned"), sem("xT_ready"), sem("scored")
        consts, wr_loaded, one_ready, counted = sem("consts"), sem("wr_loaded"), sem("one_ready"), sem("counted")
        steps, exp_asked, exp_ready, slots_ready = sem("steps"), sem("exp_asked"), sem("exp_ready"), sem("slots_ready")
        straight = sem("straight")
        block = ctx.enter_context(nc.Block())

        @block.sync
        def _(sp):
            sp.dma_start(wr[:, :, :], a[f"L{l}_wrT"].rearrange("(k p) e -> p k e", p=P)).then_inc(wr_loaded, 16)
            prefetch(sp)
            if l == 0:
                for t in range(NT):
                    sp.wait_ge(xn_ready, t + 1)
                    sp.dma_start(g["xs"][t * TT:(t + 1) * TT, :], xn[:, t, :]).then_inc(straight, 16)
                sp.wait_ge(straight, 16 * NT)

        @block.gpsimd
        def _(pool):
            pool.memset(mhalf[:, :], -0.5).then_inc(consts, 1)
            pool.memset(before[:, :], 1.0).then_inc(consts, 1)
            pool.memset(ones[:, :], 1.0).then_inc(consts, 1)
            pool.iota(eid[:, :, :], pattern=[[1, NE], [0, NT]], base=0, channel_multiplier=0,
                      allow_small_or_imprecise_dtypes=True).then_inc(consts, 1)
            pool.iota(steps128[:, :, :], pattern=[[0, NE], [P, MAXT]], base=0, channel_multiplier=0,
                      allow_small_or_imprecise_dtypes=True).then_inc(consts, 1)
            pool.iota(tile_id[:, :, :], pattern=[[1, RTILES], [0, NE]], base=0, channel_multiplier=0,
                      allow_small_or_imprecise_dtypes=True).then_inc(consts, 1)
            pool.iota(token[:, :], pattern=[[TT, NT]], base=0, channel_multiplier=1,
                      allow_small_or_imprecise_dtypes=True).then_inc(consts, 1)
            pool.wait_ge(consts, 7)
            pool.affine_select(out=before[:, :], in_=before[:, :], compare_op=ALU.is_gt, fill=0.0,
                               base=0, pattern=[[1, TT]], channel_multiplier=-1).then_inc(consts, 1)
            pool.wait_ge(vare_ready, 1)
            pool.tensor_tensor(rstd[:, :], vare[:, :], mhalf[:, :], ALU.pow).then_inc(rstd_ready, 1)

        @block.tensor
        def _(pe):
            pe.wait_ge(wr_loaded, 16)
            def score(t):
                pe.wait_ge(xT_ready, t + 1)
                for k in range(2):
                    mm = nc.tensor.matmul(lgp[:, t * NE:(t + 1) * NE], xT[:, t % 2, k * TT:(k + 1) * TT], wr[:, k, :],
                                          start=(k == 0), stop=(k == 1), skip_group_check=True)
                mm.then_inc(scored, 1)
            for t in range(NT):
                pe.wait_ge(xn_ready, t + 1)
                if t >= 2:
                    pe.wait_ge(xT_ready, t - 1)
                for k in range(2):
                    mm = nc.tensor.transpose(tp[:, t % 2, k * TT:(k + 1) * TT], xn[:, t, k * P:(k + 1) * P], ident[0:TT, 0:TT])
                mm.then_inc(turned, 1)
                if t >= 1:
                    score(t - 1)
            score(NT - 1)
            pe.wait_ge(one_ready, 1)
            pe.wait_ge(consts, 8)
            flat = both[:, :, :].rearrange("p e t -> p (e t)")
            nc.tensor.matmul(rank_ps[:, 0:NE * NT], before[:, :], flat, start=True, stop=True).then_inc(counted, 1)
            nc.tensor.matmul(tot_ps[:, 0:NE * NT], ones[:, :], flat, start=True, stop=True).then_inc(counted, 1)

        @block.scalar
        def _(act):
            for t in range(NT):
                act.wait_ge(turned, t + 1)
                if t >= 2:
                    act.wait_ge(scored, t - 1)
                nc.scalar.activation(xT[:, t % 2, :], tp[:, t % 2, 0:2 * TT], ACT.Copy).then_inc(xT_ready, 1)
            act.wait_ge(exp_asked, 1)
            if l == 0:
                nc.scalar.activation(ee[:, :, 0], dif[:, :, 0], ACT.Exp).then_inc(exp_ready, 1)
            else:
                nc.scalar.activation(ee[:, :, :], dif[:, :, :], ACT.Exp).then_inc(exp_ready, 1)

        @block.vector
        def _(dve):
            done = [0]

            def then(ins):
                done[0] += 1
                ins.then_inc(steps, 1)
                dve.wait_ge(steps, done[0])

            def over_tiles(x):
                return x.unsqueeze(1).broadcast_to([TT, NE, NT])

            nc.vector.tensor_scalar(vare[:, :], mv[:, :, 1], 1e-5, None, ALU.add).then_inc(vare_ready, 1)
            dve.wait_ge(rstd_ready, 1)
            for t in range(NT):
                nc.vector.tensor_scalar(xn[:, t, :], T[:, t, :], mv[:, t, 0:1], rstd[:, t:t + 1],
                                        ALU.subtract, ALU.mult).then_inc(xn_ready, 1)
            dve.wait_ge(scored, NT)
            then(nc.vector.tensor_copy(lg[:, :, :], lgp[:, 0:NT * NE].rearrange("p (t e) -> p t e", t=NT)))
            for t in range(NT):
                last = nc.vector.max(best[:, t, :], lg[:, t, :])
                if t < NT - 1:
                    last.then_inc(top_steps, 1)
            then(last)
            dve.wait_ge(top_steps, NT - 1)
            for t in range(NT):
                last = nc.vector.max_index(which[:, t, :], best[:, t, :], lg[:, t, :])
                if t < NT - 1:
                    last.then_inc(top_steps, 1)
            then(last)
            dve.wait_ge(top_steps, 2 * NT - 2)
            if l == 0:
                then(nc.vector.tensor_tensor(dif[:, :, 0], best[:, :, 1], best[:, :, 0], ALU.subtract))
            else:
                then(nc.vector.tensor_tensor(dif[:, :, :], lg[:, :, :], best[:, :, 0:1].broadcast_to([TT, NT, NE]), ALU.subtract))
            dve.sem_inc(exp_asked, 1)
            dve.wait_ge(consts, 8)
            for c in range(top):
                then(nc.vector.tensor_copy(whichf[:, c, :], which[:, :, c]))
                then(nc.vector.tensor_tensor(one[:, c, :, :], over_tiles(whichf[:, c, :]), eid[:, :, :], ALU.is_equal))
            if top == 2:
                nc.vector.tensor_tensor(both[:, :, :], one[:, 0, :, :], one[:, 1, :, :], ALU.add).then_inc(one_ready, 1)
            else:
                nc.vector.tensor_copy(both[:, :, :], one[:, 0, :, :]).then_inc(one_ready, 1)
            dve.wait_ge(exp_ready, 1)
            if l == 0:
                then(nc.vector.tensor_scalar(den[:, :], ee[:, :, 0], 1.0, None, ALU.add))
                then(nc.vector.reciprocal(g["share"][:, 0, :], den[:, :]))
                then(nc.vector.tensor_tensor(g["share"][:, 1, :], g["share"][:, 0, :], ee[:, :, 0], ALU.mult))
            else:
                then(nc.vector.tensor_reduce(den[:, :], ee[:, :, :], AX_X, ALU.add))
                then(nc.vector.reciprocal(prob[:, :], den[:, :]))
            dve.wait_ge(counted, 2)
            then(nc.vector.tensor_copy(tot[:, :, :].rearrange("p e t -> p (e t)"), tot_ps[:, 0:NE * NT]))
            flat = tot[:, :, :].rearrange("p e t -> p (e t)")
            then(nc.vector.memset(cum[:, :], 0.0))
            then(nc.vector.tensor_tensor_scan(prev[:, :, :].rearrange("p e t -> p (e t)"), flat, cum[:, :], 0.0, ALU.add, ALU.add))
            then(nc.vector.tensor_tensor(prev[:, :, :], prev[:, :, :], tot[:, :, :], ALU.subtract))
            then(nc.vector.tensor_copy(first[:, :], prev[:, :, 0]))
            then(nc.vector.tensor_tensor(prev[:, :, :], prev[:, :, :], first[:, :].unsqueeze(2).broadcast_to([TT, NE, NT]), ALU.subtract))
            then(nc.vector.tensor_tensor(count[:, :], prev[:, :, NT - 1], tot[:, :, NT - 1], ALU.add))
            then(nc.vector.tensor_tensor(pos[:, :, :], prev[:, :, :], rank_ps[:, 0:NE * NT].rearrange("p (e t) -> p e t", e=NE), ALU.add))
            if l == 0:
                then(nc.vector.tensor_tensor(over[:, :, :], count[:, :].unsqueeze(2).broadcast_to([TT, NE, MAXT]), steps128[:, :, :], ALU.is_gt))
                then(nc.vector.tensor_reduce(tiles[:, :], over[:, :, :], AX_X, ALU.add))
                then(nc.vector.tensor_tensor_scan(ends[:, :], tiles[:, :], cum[:, 0:NE], 0.0, ALU.add, ALU.add))
                then(nc.vector.tensor_tensor(first[:, :], ends[:, :], tiles[:, :], ALU.subtract))
                then(nc.vector.tensor_scalar(first[:, :], first[:, :], float(P), float(B * HW), ALU.mult, ALU.add))
                then(nc.vector.tensor_tensor(pos[:, :, :], pos[:, :, :], first[:, :].unsqueeze(2).broadcast_to([TT, NE, NT]), ALU.add))
                then(nc.vector.tensor_tensor(passed[:, :, :], ends[0:1, :].unsqueeze(1).broadcast_to([1, RTILES, NE]), tile_id[:, :, :], ALU.is_le))
                then(nc.vector.tensor_reduce(owner[:, :], passed[:, :, :], AX_X, ALU.add))
                then(nc.vector.tensor_scalar(owner[:, :], owner[:, :], float(NE - 1), None, ALU.min))
                then(nc.vector.tensor_copy(g["owner"][:, STILES:STILES + RTILES], owner[:, :]))
                then(nc.vector.memset(owner[:, 0:STILES], float(NE)))
                then(nc.vector.tensor_copy(g["owner"][:, 0:STILES], owner[:, 0:STILES]))
            for c in range(top):
                then(nc.vector.tensor_tensor(picked[:, :, :], one[:, c, :, :], pos[:, :, :], ALU.mult))
                then(nc.vector.tensor_reduce(slotf[:, c, :], picked[:, :, :].rearrange("p e t -> p t e"), AX_X, ALU.add))
            if l == 0:
                nc.vector.tensor_copy(g["slot"][:, :, :], slotf[:, :, :]).then_inc(slots_ready, 1)
            else:
                then(nc.vector.tensor_scalar(kept[:, :], slotf[:, 0, :], float(CAP), None, ALU.is_lt))
                then(nc.vector.tensor_tensor(g["share"][:, 0, :], prob[:, :], kept[:, :], ALU.mult))
                then(nc.vector.tensor_scalar(base[:, :], whichf[:, 0, :], float(CAP), None, ALU.mult))
                then(nc.vector.tensor_tensor(slotf[:, 0, :], slotf[:, 0, :], base[:, :], ALU.add))
                then(nc.vector.tensor_scalar(token[:, :], token[:, :], float(NE * CAP), None, ALU.add))
                then(nc.vector.tensor_tensor(slotf[:, 0, :], slotf[:, 0, :], token[:, :], ALU.subtract))
                then(nc.vector.tensor_tensor(slotf[:, 0, :], slotf[:, 0, :], kept[:, :], ALU.mult))
                then(nc.vector.tensor_tensor(slotf[:, 0, :], slotf[:, 0, :], token[:, :], ALU.add))
                then(nc.vector.tensor_scalar(slotf[:, 1, :], slotf[:, 0, :], float(NE * CAP - 1), None, ALU.min))
                nc.vector.tensor_copy(g["slot"][:, :, :], slotf[:, :, :]).then_inc(slots_ready, 1)


def scatter(nc, pool, g, top, sent):
    for t in range(NT):
        for c in range(top):
            pool.indirect_dma_start(out=g["xs"][:, :], out_offset=bass.IndirectOffsetOnAxis(ap=g["slot"][:, c, t:t + 1], axis=0),
                                    in_=g["xn"][:, t, :], in_offset=None).then_inc(sent, 16)


def weights0(nc, a, g, ctx):
    sb, ps, sem = memory(nc, ctx, "weights0", g["used"])
    w = {"gu": sb("wgu", [P, NE + 1, 2, 2, F0]),
         "d": sb("wd", [P, NE + 1, FC0, C]),
         "shared_loaded": sem("shared_loaded"), "routed_loaded": sem("routed_loaded")}

    def load(sp, e, w_g, w_u, w_d, done):
        for which, src in ((0, w_g), (1, w_u)):
            sp.dma_start(w["gu"][:, e, which, :, :], src.rearrange("(k p) f -> p k f", p=P)).then_inc(done, 16)
        sp.dma_start(w["d"][:, e, :, :], w_d.rearrange("(f p) c -> p f c", p=P)).then_inc(done, 16)

    def prefetch(sp):
        load(sp, NE, a["L0_sg"], a["L0_su"], a["L0_sd"], w["shared_loaded"])
        for e in range(NE):
            load(sp, e, a["L0_wg"][e], a["L0_wu"][e], a["L0_wd"][e], w["routed_loaded"])

    return w, prefetch


def phase_experts0(nc, a, g, w):
    with ExitStack() as ctx:
        sb, ps, sem = memory(nc, ctx, "experts0", g["used"])
        ident, wgu, wd = g["ident"], w["gu"], w["d"]
        xs, xT = sb("xs", [P, 2, C]), sb("xT", [P, 2, C])
        sg, h, hT, eo = sb("sg", [P, 2, F0]), sb("h", [P, 2, F0]), sb("hT", [P, 2, F0]), sb("eo", [P, 2, C])
        tp, gate, up = ps("tp", [P, BANK]), ps("gate", [P, 2, BANK]), ps("up", [P, 2, BANK])
        htp, down = ps("htp", [P, BANK]), ps("down", [P, 2, BANK])
        sent = sem("sent")
        x_loaded, stored = [sem("x_loaded0"), sem("x_loaded1")], [sem("stored0"), sem("stored1")]
        turned, xT_ready, gate_done, up_done = sem("turned"), sem("xT_ready"), sem("gate_done"), sem("up_done")
        sg_ready, h_ready, h_turned, hT_ready = sem("sg_ready"), sem("h_ready"), sem("h_turned"), sem("hT_ready")
        down_done, eo_ready = sem("down_done"), sem("eo_ready")
        block = ctx.enter_context(nc.Block())
        TILES, LOADS = STILES + RTILES, 3

        def tile(i, off):
            return 2 * i + off, off % 2, i + off // 2

        @block.gpsimd
        def _(pool):
            scatter(nc, pool, g, TOPK[0], sent)

        @block.sync
        def _(sp):
            def load_x(t):
                n, par, _ = t
                if not isinstance(n, int) or n > 1:
                    sp.wait_ge(turned, START + n - 1)
                sp.dma_start(xs[:, par, :], g["xs"][bass.ds(n * P, P), :]).then_inc(x_loaded[par], 16)

            def store(t):
                n, par, _ = t
                sp.wait_ge(eo_ready, START + n + 1)
                sp.dma_start(g["eo"][bass.ds(n * P, P), :], eo[:, par, :]).then_inc(stored[par], 16)

            def two_tiles(i):
                load_x(tile(i, 1))
                store(tile(i - 1, 0))
                load_x(tile(i, 2))
                store(tile(i - 1, 1))

            for off in range(3):
                load_x(tile(0, off))
            with sp.Fori(1, STILES // 2 - 1) as i:
                two_tiles(i)
            load_x(tile(STILES // 2 - 1, 1))
            store(tile(STILES // 2 - 2, 0))
            sp.wait_ge(sent, 16 * NT * TOPK[0])
            load_x(tile(STILES // 2, 0))
            store(tile(STILES // 2 - 2, 1))
            with sp.Fori(STILES // 2, TILES // 2 - 1) as i:
                two_tiles(i)
            load_x(tile(TILES // 2 - 1, 1))
            for off in range(-2, 2):
                store(tile(TILES // 2 - 1, off))
            for par in range(2):
                sp.wait_ge(stored[par], 16 * (TILES // 2))

        @block.tensor
        def _(pe):
            for s in (turned, h_turned, down_done):
                pe.sem_inc(s, START)

            def owner(t):
                return pe.value_load(g["owner"][0:1, bass.ds(t[0], 1)], min_val=0, max_val=NE)

            def turn(t):
                n, par, m = t
                pe.wait_ge(x_loaded[par], 16 * (m + 1))
                pe.wait_ge(xT_ready, START + n)
                for k in range(2):
                    mm = nc.tensor.transpose(tp[:, k * P:(k + 1) * P], xs[:, par, k * P:(k + 1) * P], ident[:, :])
                mm.then_inc(turned, 1)

            def widen(t, between):
                n, par, _ = t
                e = owner(t)
                pe.wait_ge(xT_ready, START + n + 1)
                pe.wait_ge(h_ready, START + n - 1)
                for which, bank, done in ((0, gate, gate_done), (1, up, up_done)):
                    for k in range(2):
                        mm = nc.tensor.matmul(bank[:, par, :], xT[:, par, k * P:(k + 1) * P],
                                              wgu[:, bass.ds(e, 1), which, k, :], start=(k == 0), stop=(k == 1))
                    mm.then_inc(done, 1)
                    if which == 0:
                        between()

            def turn_h(t):
                n, par, _ = t
                pe.wait_ge(h_ready, START + n + 1)
                pe.wait_ge(hT_ready, START + n)
                for f in range(FC0):
                    mm = nc.tensor.transpose(htp[:, f * P:(f + 1) * P], h[:, par, f * P:(f + 1) * P], ident[:, :])
                mm.then_inc(h_turned, 1)

            def narrow(t):
                n, par, _ = t
                e = owner(t)
                pe.wait_ge(hT_ready, START + n + 1)
                pe.wait_ge(eo_ready, START + n - 1)
                for f in range(FC0):
                    mm = nc.tensor.matmul(down[:, par, 0:C], hT[:, par, f * P:(f + 1) * P],
                                          wd[:, bass.ds(e, 1), f, :], start=(f == 0), stop=(f == FC0 - 1))
                mm.then_inc(down_done, 1)

            def two_tiles(i):
                for off in (1, 2):
                    def turns():
                        turn_h(tile(i, off - 1))
                        turn(tile(i, off + 1))
                    widen(tile(i, off), turns)
                    narrow(tile(i, off - 1))

            pe.wait_ge(w["shared_loaded"], 16 * LOADS)
            turn(tile(0, 0))
            widen(tile(0, 0), lambda: turn(tile(0, 1)))
            with pe.Fori(0, STILES // 2 - 1) as i:
                two_tiles(i)
            pe.wait_ge(w["routed_loaded"], 16 * LOADS * NE)
            with pe.Fori(STILES // 2 - 1, TILES // 2 - 1) as i:
                two_tiles(i)
            last = TILES // 2 - 1
            widen(tile(last, 1), lambda: turn_h(tile(last, 0)))
            narrow(tile(last, 0))
            turn_h(tile(last, 1))
            narrow(tile(last, 1))

        @block.scalar
        def _(act):
            for s in (xT_ready, hT_ready, eo_ready):
                act.sem_inc(s, START)

            def copy_x(t):
                n, par, _ = t
                act.wait_ge(turned, START + n + 1)
                if not (isinstance(n, int) and n < 2):
                    act.wait_ge(up_done, n - 1)
                nc.scalar.activation(xT[:, par, :], tp[:, 0:C], ACT.Copy).then_inc(xT_ready, 1)

            def silu(t):
                n, par, _ = t
                act.wait_ge(h_ready, START + n - 1)
                act.wait_ge(gate_done, n + 1)
                nc.scalar.activation(sg[:, par, :], gate[:, par, :], ACT.Silu).then_inc(sg_ready, 1)

            def copy_h(t):
                n, par, _ = t
                act.wait_ge(down_done, START + n - 1)
                act.wait_ge(h_turned, START + n + 1)
                nc.scalar.activation(hT[:, par, :], htp[:, :], ACT.Copy).then_inc(hT_ready, 1)

            def copy_out(t):
                n, par, m = t
                if not (isinstance(m, int) and m == 0):
                    act.wait_ge(stored[par], 16 * m)
                act.wait_ge(down_done, START + n + 1)
                nc.scalar.activation(eo[:, par, :], down[:, par, 0:C], ACT.Copy).then_inc(eo_ready, 1)

            def two_tiles(i):
                for off in (1, 2):
                    silu(tile(i, off))
                    copy_h(tile(i, off - 1))
                    copy_x(tile(i, off + 1))
                    copy_out(tile(i, off - 1))

            copy_x(tile(0, 0))
            silu(tile(0, 0))
            copy_x(tile(0, 1))
            two_tiles(0)
            with act.Fori(1, TILES // 2 - 1) as i:
                two_tiles(i)
            last = TILES // 2 - 1
            silu(tile(last, 1))
            for off in (0, 1):
                copy_h(tile(last, off))
                copy_out(tile(last, off))

        @block.vector
        def _(dve):
            dve.sem_inc(h_ready, START)
            with dve.Fori(0, TILES // 2) as i:
                for off in range(2):
                    n, par, _ = tile(i, off)
                    dve.wait_ge(sg_ready, n + 1)
                    dve.wait_ge(up_done, n + 1)
                    dve.wait_ge(h_turned, START + n - 1)
                    nc.vector.tensor_tensor(h[:, par, :], sg[:, par, :], up[:, par, :], ALU.mult).then_inc(h_ready, 1)


def weights1(nc, a, g, ctx):
    sb, ps, sem = memory(nc, ctx, "weights1", g["used"])
    w = {"1": sb("w1", [P, 2, 2, F1]), "2": sb("w2", [P, 2, FC1, C]),
         "b1": sb("b1", [P, NE, FC1]), "b2": sb("b2", [CT, NE, C]),
         "bias_loaded": sem("bias_loaded"), "loaded": [sem("w_loaded0"), sem("w_loaded1")]}

    def load(sp, e, par):
        one = a["L1_w1"][bass.ds(e, 1), :, :].rearrange("o (k p) f -> p (o k) f", p=P)
        sp.dma_start(w["1"][:, par, :, :], one).then_inc(w["loaded"][par], 16)
        two = a["L1_w2"][bass.ds(e, 1), :, :].rearrange("o (f p) c -> p (o f) c", p=P)
        sp.dma_start(w["2"][:, par, :, :], two).then_inc(w["loaded"][par], 16)

    def prefetch(sp):
        load(sp, 0, 0)
        load(sp, 1, 1)
        sp.dma_start(w["b1"][:, :, :], a["L1_b1"]).then_inc(w["bias_loaded"], 16)
        sp.dma_start(w["b2"][:, :, :], a["L1_b2"].unsqueeze(0).broadcast_to([CT, NE, C])).then_inc(w["bias_loaded"], 16)

    w["load"] = load
    return w, prefetch


def phase_experts1(nc, a, g, w):
    with ExitStack() as ctx:
        sb, ps, sem = memory(nc, ctx, "experts1", g["used"])
        ident = g["ident"]
        w1, w2, b1, b2, w_loaded, bias_loaded = (w[n] for n in ("1", "2", "b1", "b2", "loaded", "bias_loaded"))
        xs, xT = sb("xs", [CT, 2, CTILES, C]), sb("xT", [P, 2, 2, CAP])
        hT, eo = sb("hT", [P, FC1, CAP]), sb("eo", [CT, 2, CTILES, C])
        tp, hid, down = ps("tp", [P, 2, BANK]), ps("hid", [P, 2, BANK]), ps("down", [P, 2, BANK])
        sent = sem("sent")
        x_loaded, stored = ([sem(f"{n}{i}") for i in range(2)] for n in ("x_loaded", "stored"))
        turned, xT_ready, hid_done, hT_ready = sem("turned"), sem("xT_ready"), sem("hid_done"), sem("hT_ready")
        down_done, eo_ready = sem("down_done"), sem("eo_ready")
        block = ctx.enter_context(nc.Block())

        def every(eng, body):
            for par in range(2):
                body(par, par, 0, False)
            with eng.Fori(1, NE // 2 - 1) as i:
                for par in range(2):
                    body(i * 2 + par, par, i, False)
            for par in range(2):
                body(NE - 2 + par, par, NE // 2 - 1, par == 1)

        @block.sync
        def _(sp):
            def load_x(e, par):
                rows = g["xs"][bass.ds(e * CAP, CAP), :].rearrange("(i p) c -> p i c", p=CT)
                sp.dma_start(xs[:, par, :, :], rows).then_inc(x_loaded[par], 16)

            sp.wait_ge(sent, 16 * NT)
            load_x(0, 0)
            load_x(1, 1)
            with sp.Fori(0, NE // 2 - 1) as i:
                for par in range(2):
                    e = i * 2 + par
                    sp.wait_ge(down_done, START + CTILES * (e + 1))
                    load_x(e + 2, par)
                    w["load"](sp, e + 2, par)

        @block.tensor
        def _(pe):
            for s in (turned, down_done):
                pe.sem_inc(s, START)

            def turn(e, par, m):
                pe.wait_ge(x_loaded[par], 16 * (m + 1))
                pe.wait_ge(xT_ready, START + 2 * e)
                for k in range(2):
                    for i in range(CTILES):
                        mm = nc.tensor.transpose(tp[:, k, i * CT:(i + 1) * CT], xs[:, par, i, k * P:(k + 1) * P],
                                                 ident[0:CT, 0:CT])
                    mm.then_inc(turned, 1)

            def body(e, par, m, last):
                pe.wait_ge(w_loaded[par], 32 * (m + 1))
                pe.wait_ge(xT_ready, START + 2 * (e + 1))
                for f in range(FC1):
                    pe.wait_ge(hT_ready, START + FC1 * e + f - 1)
                    for k in range(2):
                        mm = nc.tensor.matmul(hid[:, f % 2, 0:CAP], w1[:, par, k, f * P:(f + 1) * P], xT[:, par, k, :],
                                              start=(k == 0), stop=(k == 1))
                    mm.then_inc(hid_done, 1)
                if not last:
                    turn(e + 1, 1 - par, m + par)
                pe.wait_ge(hT_ready, START + FC1 * (e + 1))
                for i in range(CTILES):
                    pe.wait_ge(eo_ready, START + CTILES * e + i - 1)
                    for f in range(FC1):
                        mm = nc.tensor.matmul(down[0:CT, i % 2, 0:C], hT[:, f, i * CT:(i + 1) * CT], w2[:, par, f, :],
                                              start=(f == 0), stop=(f == FC1 - 1))
                    mm.then_inc(down_done, 1)

            turn(0, 0, 0)
            every(pe, body)

        @block.scalar
        def _(act):
            act.sem_inc(hT_ready, START)
            act.wait_ge(bias_loaded, 32)

            def body(e, par, m, last):
                act.wait_ge(down_done, START + CTILES * e)
                for f in range(FC1):
                    bias = b1[:, e, f:f + 1] if isinstance(e, int) else b1[:, bass.ds(e, 1), f:f + 1]
                    act.wait_ge(hid_done, FC1 * e + f + 1)
                    nc.scalar.activation(hT[:, f, :], hid[:, f % 2, 0:CAP], ACT.Gelu,
                                         bias=bias).then_inc(hT_ready, 1)

            every(act, body)

        @block.vector
        def _(dve):
            for s in (xT_ready, eo_ready):
                dve.sem_inc(s, START)
            dve.wait_ge(bias_loaded, 32)

            def copy_x(e, par):
                for k in range(2):
                    dve.wait_ge(turned, START + 2 * e + k + 1)
                    nc.vector.tensor_copy(xT[:, par, k, :], tp[:, k, 0:CAP]).then_inc(xT_ready, 1)

            def body(e, par, m, last):
                if not last:
                    copy_x(e + 1, 1 - par)
                if not (isinstance(m, int) and m == 0):
                    dve.wait_ge(stored[par], 16 * m)
                for i in range(CTILES):
                    bias = b2[:, e, :] if isinstance(e, int) else b2[:, bass.ds(e, 1), :].rearrange("p o c -> p (o c)")
                    dve.wait_ge(down_done, START + CTILES * e + i + 1)
                    nc.vector.tensor_tensor(eo[:, par, i, :], down[0:CT, i % 2, 0:C], bias, ALU.add).then_inc(eo_ready, 1)

            copy_x(0, 0)
            every(dve, body)

        @block.gpsimd
        def _(pool):
            def body(e, par, m, last):
                rows = e * CAP if isinstance(e, int) else pool.snap(e * CAP)
                pool.wait_ge(eo_ready, START + CTILES * (e + 1))
                pool.dma_start(g["eo"][bass.ds(rows, CAP), :].rearrange("(i p) c -> p i c", p=CT),
                               eo[:, par, :, :]).then_inc(stored[par], 16)

            scatter(nc, pool, g, TOPK[1], sent)
            every(pool, body)
            for par in range(2):
                pool.wait_ge(stored[par], 16 * (NE // 2))


def phase_combine(nc, a, g, l):
    top, shared = TOPK[l], l == 0
    NB = 4
    with ExitStack() as ctx:
        sb, ps, sem = memory(nc, ctx, f"combine{l}", g["used"])
        T = g["T"]
        rows, srow = sb("rows", [TT, NB, top, C]), sb("srow", [TT, NB, C])
        part = sb("part", [TT, NB, C])
        fetched = [[sem(f"fetched{c}_{i}") for i in range(NB)] for c in range(top)]
        s_fetched = [sem(f"s_fetched{i}") for i in range(NB)]
        added, part_ready, summed = sem("added"), sem("part_ready"), sem("summed")
        block = ctx.enter_context(nc.Block())

        @block.gpsimd
        def _(pool):
            for t in range(NT):
                if t >= NB:
                    pool.wait_ge(added, t - NB + 1)
                for c in range(top):
                    if t >= NB:
                        pool.wait_ge(fetched[c][t % NB], 16 * (t // NB))
                    at = g["slot"][:, c if shared else 1, t:t + 1]
                    pool.indirect_dma_start(out=rows[:, t % NB, c, :], out_offset=None, in_=g["eo"][:, :],
                                            in_offset=bass.IndirectOffsetOnAxis(ap=at, axis=0)).then_inc(fetched[c][t % NB], 16)

        @block.sync
        def _(sp):
            if shared:
                for t in range(NT):
                    if t >= NB:
                        sp.wait_ge(added, t - NB + 1)
                    sp.dma_start(srow[:, t % NB, :], g["eo"][t * TT:(t + 1) * TT, :]).then_inc(s_fetched[t % NB], 16)

        @block.vector
        def _(dve):
            for t in range(NT):
                times = 16 * (t // NB + 1)
                src = T[:, t, :]
                for c in range(top):
                    last = c == top - 1
                    dve.wait_ge(fetched[c][t % NB], times)
                    if c:
                        dve.wait_ge(part_ready, t + 1)
                    dst = T[:, t, :] if last else part[:, t % NB, :]
                    ins = nc.vector.scalar_tensor_tensor(out=dst, in0=rows[:, t % NB, c, :], scalar=g["share"][:, c, t:t + 1],
                                                         in1=src, op0=ALU.mult, op1=ALU.add)
                    if not last:
                        ins.then_inc(part_ready, 1)
                        src = part[:, t % NB, :]
                    elif not shared:
                        ins.then_inc(added, 1)
                if shared:
                    ins.then_inc(summed, 1)
                    dve.wait_ge(summed, t + 1)
                    dve.wait_ge(s_fetched[t % NB], times)
                    nc.vector.tensor_tensor(T[:, t, :], T[:, t, :], srow[:, t % NB, :], ALU.add).then_inc(added, 1)


def phase_output(nc, a, g):
    with ExitStack() as ctx:
        sb, ps, sem = memory(nc, ctx, "output", g["used"])
        yc = sb("yc", [P, B * 2, HW])
        tp = ps("tp", [P, 4, BANK])
        turned, copied, stored = sem("turned"), sem("copied"), sem("stored")
        block = ctx.enter_context(nc.Block())

        @block.tensor
        def _(pe):
            for t in range(NT):
                if t >= 4:
                    pe.wait_ge(copied, t - 3)
                for k in range(2):
                    mm = nc.tensor.transpose(tp[:, t % 4, k * TT:(k + 1) * TT], g["T"][:, t, k * P:(k + 1) * P],
                                             g["ident"][0:TT, 0:TT])
                mm.then_inc(turned, 1)

        @block.vector
        def _(dve):
            for t in range(NT):
                b, j = divmod(t, TPB)
                dve.wait_ge(turned, t + 1)
                nc.vector.tensor_copy(yc[:, 2 * b:2 * b + 2, j * TT:(j + 1) * TT], tp[:, t % 4, 0:2 * TT].rearrange("p (k n) -> p k n", k=2)).then_inc(copied, 1)

        @block.sync
        def _(sp):
            for b in range(B):
                sp.wait_ge(copied, TPB * (b + 1))
                sp.dma_start(a["out"][b].rearrange("(k p) h w -> p k (h w)", p=P),
                             yc[:, 2 * b:2 * b + 2, :]).then_inc(stored, 16)
            sp.wait_ge(stored, 16 * B)


def build(nc, a):
    with ExitStack() as ctx:
        sb, ps, sem = memory(nc, ctx, "all", [])
        g = {"used": [], "T": sb("T", [TT, NT, C]), "ident": sb("ident", [P, P]), "fold": sb("fold", [P, DG]),
             "sel": sb("sel", [P, NG, P]), "mamba": []}
        for l in range(2):
            g["mamba"].append({n: sb(f"m{l}_{n}", s) for n, s in (
                ("wu", [P, 2, DI]), ("wz", [P, DI]), ("wdt", [P, DI]), ("wbc", [P, 2 * DS]),
                ("wout", [P, DM]), ("vec", [P, 3]), ("diag", [P, DI]), ("acol", [P, ITEMS]))})
        g["seq"] = nc.dram_tensor("seq_scratch", (NCH + 3, DM, CW), F32, kind="Internal").ap()
        g["dt_rows"] = nc.dram_tensor("dt_rows", (2 * P, TC), F32, kind="Internal").ap()
        g["bc_rows"] = nc.dram_tensor("bc_rows", (2, 2 * DS, TC), F32, kind="Internal").ap()
        g["xs"] = nc.dram_tensor("slot_rows", (SLOTS0, C), F32, kind="Internal").ap()
        g["eo"] = nc.dram_tensor("expert_rows", (SLOTS0, C), F32, kind="Internal").ap()
        g["slot"] = sb("slot", [TT, 2, NT], I32)
        g["share"] = sb("share", [TT, 2, NT])
        g["mv"] = sb("mv", [TT, NT, 2])
        g["owner"] = sb("owner", [1, STILES + RTILES], I32)
        phase_setup(nc, a, g)
        for l in range(2):
            phase_sequence(nc, a, g, l)
            phase_mamba(nc, a, g, l)
            with ExitStack() as ffn:
                weights, phase_experts = ((weights0, phase_experts0), (weights1, phase_experts1))[l]
                g["xn"] = ffn.enter_context(nc.sbuf_tensor(f"xn{l}", [TT, NT, C], F32))
                w, prefetch = weights(nc, a, g, ffn)
                phase_route(nc, a, g, l, prefetch)
                phase_experts(nc, a, g, w)
            phase_combine(nc, a, g, l)
            if l == 0:
                nc.clear_and_free_semaphores(g["used"])
                g["used"].clear()
                nc.all_engine_barrier()
        phase_output(nc, a, g)


def layout(inputs):
    import numpy as np
    i = {n: np.asarray(v) for n, v in inputs.items()}
    out = {"x": i["x"]}
    for l in range(2):
        c = lambda n: i[f"L{l}_conv_{n}"]
        out[f"L{l}_winT"] = c("in_proj_w").T
        out[f"L{l}_cwT"] = c("conv_w").T
        out[f"L{l}_alog"] = c("A_log").reshape(NG, DG, NM, NS).transpose(3, 1, 0, 2).reshape(P, ITEMS)
        out[f"L{l}_xpw"] = c("x_proj_w")
        out[f"L{l}_xpT"] = c("x_proj_w").T
        out[f"L{l}_dtwT"] = c("dt_proj_w").T
        out[f"L{l}_woT"] = c("out_proj_w").T
        out[f"L{l}_vec"] = np.stack([c("conv_b"), c("dt_proj_b"), c("D")], axis=1)
        out[f"L{l}_token"] = c("global_token").reshape(DM, 1)
        out[f"L{l}_wrT"] = i[f"L{l}_ffn_router_w"].T
    for short, name in (("wg", "w_gate"), ("wu", "w_up"), ("wd", "w_down"), ("sg", "sg"), ("su", "su"), ("sd", "sd")):
        out[f"L0_{short}"] = i[f"L0_ffn_{name}"]
    out["L1_w1"], out["L1_w2"], out["L1_b2"] = i["L1_ffn_w1"], i["L1_ffn_w2"], i["L1_ffn_b2"]
    out["L1_b1"] = i["L1_ffn_b1"].reshape(NE, FC1, P).transpose(2, 0, 1)
    return {n: np.ascontiguousarray(v) for n, v in out.items()}


def kernel(**inputs):
    import concourse.bacc as bacc
    from concourse.bass_utils import run_bass_kernel_spmd

    nc = bacc.Bacc("TRN2", target_bir_lowering=False, num_devices=1)
    arrays = {f"in_{n}_dram": v for n, v in layout(inputs).items()}
    a = {n[3:-5]: nc.dram_tensor(n, v.shape, mybir.dt.from_np(v.dtype), kind="ExternalInput").ap()
         for n, v in arrays.items()}
    a["out"] = nc.dram_tensor("out_0_dram", (B, C, H, W), F32, kind="ExternalOutput").ap()
    build(nc, a)
    r = run_bass_kernel_spmd(nc, [arrays], core_ids=[0])
    return r.results[0]["out_0_dram"]
```

```python
from contextlib import ExitStack

import concourse.bass as bass
from concourse import mybir

F32 = mybir.dt.float32
I32 = mybir.dt.int32
U32 = mybir.dt.uint32
ALU = mybir.AluOpType
ACT = mybir.ActivationFunctionType
AX_X = mybir.AxisListType.X

P = 128
B, C, H, W = 4, 256, 24, 24
HW = H * W
TT = 96
ROWS = TT // W
TPB = HW // TT
NT = B * TPB
GT = 3
R = 2
DM, DI, DS, DC, DR = C // 4, 128, 16, 4, 4
LSEQ = HW * R * R + 1
BANK = 512
CPB = 5
NCH = B * CPB
TC = 462
PAD = DC - 1
LPAD = PAD + CPB * TC
CW = TC + PAD
NG, DG = 4, 32
NM, NS = 4, 4
ITEMS = NG * NM
REP_ROWS = 2 * NG + 2 * NM
UBUFS = 4
BANKS = 5
STATE_BANK = [i % BANKS for i in range(ITEMS - 1)] + [2]
PAIRED = [i % BANKS in (0, 2) and STATE_BANK[(i + 1) % ITEMS] == STATE_BANK[i] + 1 for i in range(ITEMS)]
SECOND = [PAIRED[i - 1] for i in range(ITEMS)]
COPIES = [i + 1 - sum(SECOND[:i + 1]) for i in range(ITEMS)]
STATE_GAP = [min(n for n in range(1, ITEMS) if STATE_BANK[i - n] == STATE_BANK[i]) for i in range(ITEMS)]
AT_SILU, AT_EXP, AT_ONE, AT_LN, AT_BC, AT_DT, AT_DTU = 6, 10, 11, 15, 13, 5, 4
START = 6
NE, TOPK = 8, (2, 1)
F0, F1 = 512, 1024
FC0, FC1 = F0 // P, F1 // P
STILES = B * HW // P
AHEAD = NE // 2
MAXT = B * HW // P
RTILES = TOPK[0] * B * HW // P + NE
SLOTS0 = (STILES + RTILES) * P
CAP = -(-3 * B * HW // (2 * NE))
CT = 108
CTILES = CAP // CT
assert CTILES * CT == CAP and RTILES % 2 == 0 and STILES % 2 == 0 and B * HW % P == 0
assert NE * CAP + B * HW <= SLOTS0
assert R * DM == P and NS * DG == P and CPB * TC >= LSEQ and NG * DG == DI and NM * NS == DS and TC <= BANK


def memory(nc, ctx, phase, used):

    def sb(name, shape, dt=F32):
        return ctx.enter_context(nc.sbuf_tensor(f"{phase}_{name}", shape, dt))

    def ps(name, shape, dt=F32):
        return ctx.enter_context(nc.psum_tensor(f"{phase}_{name}", shape, dt))

    def sem(name):
        used.append(nc.alloc_semaphore(f"{phase}_{name}"))
        return used[-1]

    return sb, ps, sem


def x_tiles(nc, a, g, ctx):
    sb, ps, sem = memory(nc, ctx, "setup", g["used"])
    xc = sb("xc", [P, B * 2, HW])
    raw = [{n: sb(f"raw{l}_{n}", s) for n, s in (
        ("winT", [P, DI]), ("cw", [P, 2, DI]), ("alog", [P, ITEMS]),
        ("wxT", [DR, DI]), ("wdtT", [DR, DI]))} for l in range(2)]
    zero = sb("zero", [P, 4 * C])
    tp = ps("tp", [P, 4, BANK])
    wp = ps("wp", [P, BANK])
    ready, zeroed, zero_stored = sem("t_copied"), sem("zeroed"), sem("zero_stored")
    x_loaded, w_loaded = [sem(f"x_loaded{b}") for b in range(B)], sem("w_loaded")
    ident_ready, x_turned = sem("ident_ready"), sem("x_turned")
    fold_multiplied, pool_steps, exp_ready, act_copied = sem("fold_multiplied"), sem("pool_steps"), sem("exp_ready"), sem("act_copied")
    wz_zeroed, sel_ready, vec_steps = sem("wz_zeroed"), sem("sel_ready"), sem("vec_steps")
    NW = 13
    routed = g["xs"][B * HW:SLOTS0, :].rearrange("(n p r) c -> n p (r c)", p=P, r=4)

    def sync(sp):
        for b in range(B):
            sp.dma_start(xc[:, 2 * b:2 * b + 2, :],
                         a["x"][b].rearrange("(k p) h w -> p k (h w)", p=P)).then_inc(x_loaded[b], 16)
        sp.wait_ge(wz_zeroed, 2)
        for l in range(2):
            w, m = raw[l], g["mamba"][l]
            for s in range(2):
                sp.dma_start(w["winT"][s * DM:(s + 1) * DM, :], a[f"L{l}_winT"][:, 0:DI]).then_inc(w_loaded, 16)
                for pair in range(2):
                    tap = a[f"L{l}_cwT"][2 * pair + s:2 * pair + s + 1, :].broadcast_to([DM, DI])
                    sp.dma_start(w["cw"][s * DM:(s + 1) * DM, pair, :], tap).then_inc(w_loaded, 16)
            sp.dma_start(m["wz"][DM:P, :], a[f"L{l}_winT"][:, DI:2 * DI]).then_inc(w_loaded, 16)
            sp.dma_start(w["alog"][:, :], a[f"L{l}_alog"]).then_inc(w_loaded, 16)
            sp.dma_start(w["wxT"][:, :], a[f"L{l}_xpw"][0:DR, :]).then_inc(w_loaded, 16)
            sp.dma_start(w["wdtT"][:, :], a[f"L{l}_dtwT"]).then_inc(w_loaded, 16)
            sp.dma_start(m["wbc"][:, :], a[f"L{l}_xpT"][:, DR:DR + 2 * DS]).then_inc(w_loaded, 16)
            sp.dma_start(m["wout"][:, :], a[f"L{l}_woT"]).then_inc(w_loaded, 16)
            sp.dma_start(m["vec"][:, :], a[f"L{l}_vec"]).then_inc(w_loaded, 16)
        sp.wait_ge(zeroed, 1)
        for n in range(routed.shape[0]):
            sp.dma_start(routed[n], zero[:, :]).then_inc(zero_stored, 16)

    def sync_end(sp):
        sp.wait_ge(zero_stored, 16 * routed.shape[0])

    def gpsimd(pool):
        pool.memset(g["ident"][:, :], 0.0).then_inc(pool_steps, 1)
        pool.memset(g["fold"][:, :], 0.0).then_inc(pool_steps, 1)
        pool.memset(g["sel"][:, :, :], 0.0).then_inc(pool_steps, 1)
        pool.wait_ge(pool_steps, 3)
        pool.affine_select(out=g["ident"][:, :], in_=g["ident"][:, :], compare_op=ALU.not_equal, fill=1.0,
                           base=0, pattern=[[-1, P]], channel_multiplier=1).then_inc(ident_ready, 1)
        for l in range(2):
            pool.memset(g["mamba"][l]["wz"][0:DM, :], 0.0).then_inc(wz_zeroed, 1)
        pool.memset(zero[:, :], 0.0).then_inc(zeroed, 1)
        for s in range(NS):
            pool.affine_select(out=g["fold"][:, :], in_=g["fold"][:, :], compare_op=ALU.not_equal, fill=1.0,
                               base=-DG * s, pattern=[[-1, DG]], channel_multiplier=1).then_inc(pool_steps, 1)
            pool.wait_ge(pool_steps, 4 + s)
        for k in range(NG):
            pool.tensor_copy(g["sel"][:, k, DG * k:DG * k + DG], g["fold"][:, :]).then_inc(sel_ready, 1)

    def tensor(pe, t):
        b, j = divmod(t, TPB)
        if t == 0:
            pe.wait_ge(ident_ready, 1)
        if j == 0:
            pe.wait_ge(x_loaded[b], 16)
        if t >= 4:
            pe.wait_ge(ready, t - 3)
        for k in range(2):
            mm = nc.tensor.transpose(tp[0:TT, t % 4, k * P:(k + 1) * P],
                                     xc[:, 2 * b + k, j * TT:(j + 1) * TT], g["ident"][:, :])
        mm.then_inc(x_turned, 1)

    def tensor_end(pe):
        pe.wait_ge(w_loaded, 16 * 2 * NW)
        for l in range(2):
            if l == 1:
                pe.wait_ge(act_copied, 1)
            nc.tensor.matmul(wp[:, 0:DI], raw[l]["wxT"][:, :], raw[l]["wdtT"][:, :],
                             start=True, stop=True).then_inc(fold_multiplied, 1)

    def scalar_end(act):
        act.wait_ge(w_loaded, 16 * 2 * NW)
        for l in range(2):
            nc.scalar.activation(g["mamba"][l]["acol"][:, :], raw[l]["alog"][:, :], ACT.Exp).then_inc(exp_ready, 1)
            act.wait_ge(fold_multiplied, l + 1)
            nc.scalar.activation(g["mamba"][l]["wdt"][:, :], wp[:, 0:DI], ACT.Copy).then_inc(act_copied, 1)

    def scalar(act, t):
        act.wait_ge(x_turned, t + 1)
        nc.scalar.activation(g["T"][:, t, :], tp[0:TT, t % 4, 0:C], ACT.Copy).then_inc(ready, 1)

    def vector_end(dve):
        dve.wait_ge(w_loaded, 16 * 2 * NW)
        for l in range(2):
            m = g["mamba"][l]
            nc.vector.tensor_scalar(m["diag"][:, :], g["ident"][:, :], m["vec"][:, 2:3], None, ALU.mult).then_inc(vec_steps, 1)
            for pair in range(2):
                nc.vector.tensor_tensor(m["wu"][:, pair, :], raw[l]["winT"][:, :], raw[l]["cw"][:, pair, :],
                                        ALU.mult).then_inc(vec_steps, 1)
            dve.wait_ge(exp_ready, l + 1)
            nc.vector.tensor_scalar(m["acol"][:, :], m["acol"][:, :], -1.0, None, ALU.mult).then_inc(vec_steps, 1)

    def nothing(*_):
        pass

    return {"ready": ready, "sync": sync, "sync_end": sync_end, "gpsimd": gpsimd, "gpsimd_tile": nothing, "tensor": tensor,
            "tensor_end": tensor_end, "scalar": scalar, "scalar_end": scalar_end, "vector": nothing, "vector_end": vector_end}


def combined_tiles(nc, a, g, ctx, l):
    top, shared = TOPK[l], l == 0
    NB = 4
    sb, ps, sem = memory(nc, ctx, f"combine{l}", g["used"])
    T = g["T"]
    rows, srow = sb("rows", [TT, NB, top, C]), sb("srow", [TT, NB, C])
    part = sb("part", [TT, NB, C])
    fetched = [[sem(f"fetched{c}_{i}") for i in range(NB)] for c in range(top)]
    s_fetched = [sem(f"s_fetched{i}") for i in range(NB)]
    ready, part_ready, summed = sem("ready"), sem("part_ready"), sem("summed")

    def gpsimd_tile(pool, t):
        if t >= NB:
            pool.wait_ge(ready, t - NB + 1)
        for c in range(top):
            if t >= NB:
                pool.wait_ge(fetched[c][t % NB], 16 * (t // NB))
            at = g["slot"][:, c if shared else 1, t:t + 1]
            pool.indirect_dma_start(out=rows[:, t % NB, c, :], out_offset=None, in_=g["eo"][:, :],
                                    in_offset=bass.IndirectOffsetOnAxis(ap=at, axis=0)).then_inc(fetched[c][t % NB], 16)

    def sync(sp):
        if shared:
            for t in range(NT):
                if t >= NB:
                    sp.wait_ge(ready, t - NB + 1)
                sp.dma_start(srow[:, t % NB, :], g["eo"][t * TT:(t + 1) * TT, :]).then_inc(s_fetched[t % NB], 16)

    def vector(dve, t):
        times = 16 * (t // NB + 1)
        src = T[:, t, :]
        for c in range(top):
            last = c == top - 1
            dve.wait_ge(fetched[c][t % NB], times)
            if c:
                dve.wait_ge(part_ready, t + 1)
            dst = T[:, t, :] if last else part[:, t % NB, :]
            ins = nc.vector.scalar_tensor_tensor(out=dst, in0=rows[:, t % NB, c, :], scalar=g["share"][:, c, t:t + 1],
                                                 in1=src, op0=ALU.mult, op1=ALU.add)
            if not last:
                ins.then_inc(part_ready, 1)
                src = part[:, t % NB, :]
            elif not shared:
                ins.then_inc(ready, 1)
        if shared:
            ins.then_inc(summed, 1)
            dve.wait_ge(summed, t + 1)
            dve.wait_ge(s_fetched[t % NB], times)
            nc.vector.tensor_tensor(T[:, t, :], T[:, t, :], srow[:, t % NB, :], ALU.add).then_inc(ready, 1)

    def nothing(*_):
        pass

    return {"ready": ready, "sync": sync, "sync_end": nothing, "gpsimd": nothing, "gpsimd_tile": gpsimd_tile, "tensor": nothing,
            "tensor_end": nothing, "scalar": nothing, "scalar_end": nothing, "vector": vector, "vector_end": nothing}


def phase_sequence(nc, a, g, l):
    with ExitStack() as ctx:
        sb, ps, sem = memory(nc, ctx, f"seq{l}", g["used"])
        T = g["T"]
        tiles = x_tiles(nc, a, g, ctx) if l == 0 else combined_tiles(nc, a, g, ctx, 0)
        ready = tiles["ready"]
        stats, mv = sb("stats", [TT, NT, 6]), sb("mv", [TT, NT, 2])
        vare, rstd, mhalf = sb("vare", [TT, NT]), sb("rstd", [TT, NT]), sb("mhalf", [TT, GT])
        tn = sb("tn", [TT, 2 * GT, R * R, DM])
        sq = sb("sq", [DM, B + 1, LPAD])
        token = sb("token", [DM, 1])
        tp = ps("tp", [P, 2, BANK])
        stat_steps, vare_ready, half_ready, rstd_ready = sem("stat_steps"), sem("vare_ready"), sem("half_ready"), sem("rstd_ready")
        tn_ready, turned, placed = sem("tn_ready"), sem("turned"), sem("placed")
        padded, token_loaded, stored = sem("padded"), sem("token_loaded"), sem("stored")
        LAG = 2 * GT - 1
        block = ctx.enter_context(nc.Block())

        @block.gpsimd
        def _(pool):
            tiles["gpsimd"](pool)
            pool.memset(mhalf[:, :], -0.5).then_inc(half_ready, 1)
            pool.memset(sq[:, 0:B, 0:PAD], 0.0).then_inc(padded, 1)
            pool.memset(sq[:, 0:B, PAD + LSEQ:LPAD], 0.0).then_inc(padded, 1)
            pool.memset(sq[:, B, 0:CW], 0.0).then_inc(padded, 1)
            pool.wait_ge(token_loaded, 16)
            pool.tensor_copy(sq[:, 0:B, PAD:PAD + 1], token[:, :].unsqueeze(1).broadcast_to([DM, B, 1])).then_inc(padded, 1)
            pool.wait_ge(half_ready, 1)

            def power(k):
                own = slice(k * GT, (k + 1) * GT)
                pool.wait_ge(vare_ready, k + 1)
                pool.tensor_tensor(rstd[:, own], vare[:, own], mhalf[:, :], ALU.pow).then_inc(rstd_ready, 1)

            for t in range(NT):
                tiles["gpsimd_tile"](pool, t)
                if t > GT and t % GT == 1:
                    power(t // GT - 1)
            power(NT // GT - 1)

        @block.vector
        def _(dve):
            def statistics(t):
                dve.wait_ge(ready, t + 1)
                nc.vector.bn_stats(stats[:, t, :], T[:, t, :]).then_inc(stat_steps, 1)

            def normalise(k):
                dve.wait_ge(rstd_ready, k + 1)
                for t in range(k * GT, (k + 1) * GT):
                    if t >= 2 * GT:
                        dve.wait_ge(turned, t - 2 * GT + 1)
                    nc.vector.tensor_scalar(tn[:, t % (2 * GT), :, :], T[:, t, :].rearrange("p (c q) -> p q c", q=R * R), mv[:, t, 0:1], rstd[:, t:t + 1],
                                            ALU.subtract, ALU.mult).then_inc(tn_ready, 1)

            for k in range(NT // GT):
                first, end = k * GT, (k + 1) * GT
                for t in range(first, end):
                    tiles["vector"](dve, t)
                    if t > first:
                        statistics(t - 1)
                statistics(end - 1)
                dve.wait_ge(stat_steps, end + first)
                for t in range(first, end):
                    nc.vector.bn_aggr(mv[:, t, :], stats[:, t, :]).then_inc(stat_steps, 1)
                dve.wait_ge(stat_steps, 2 * end)
                nc.vector.tensor_scalar(vare[:, first:end], mv[:, first:end, 1], 1e-6, None, ALU.add).then_inc(vare_ready, 1)
                if k >= 1:
                    normalise(k - 1)
            normalise(NT // GT - 1)
            tiles["vector_end"](dve)

        @block.tensor
        def _(pe):
            for s in range(NT + LAG):
                if s < NT:
                    tiles["tensor"](pe, s)
                t = s - LAG
                if t >= 0:
                    pe.wait_ge(tn_ready, t + 1)
                    if t >= 2:
                        pe.wait_ge(placed, 2 * (t - 1))
                    for i in range(R):
                        both = tn[:, t % (2 * GT), R * i:R * i + R, :].rearrange("p q c -> p (q c)")
                        mm = nc.tensor.transpose(tp[:, t % 2, i * TT:(i + 1) * TT], both, g["ident"][0:TT, 0:TT])
                    mm.then_inc(turned, 1)
            tiles["tensor_end"](pe)

        @block.scalar
        def _(act):
            for s in range(NT + LAG):
                if s < NT:
                    tiles["scalar"](act, s)
                t = s - LAG
                if t < 0:
                    continue
                b, j = divmod(t, TPB)
                act.wait_ge(turned, t + 1)
                at = PAD + 1 + j * TT * R * R
                dst = sq[:, b, at:at + TT * R * R].rearrange("c (h i w q) -> c q i h w", h=ROWS, i=R, w=W, q=R)
                for q in range(R):
                    src = tp[q * DM:(q + 1) * DM, t % 2, 0:TT * R].rearrange("c (i h w) -> c i h w", i=R, h=ROWS)
                    nc.scalar.activation(dst[:, q], src, ACT.Copy).then_inc(placed, 1)
            tiles["scalar_end"](act)

        @block.sync
        def _(sp):
            sp.dma_start(token[:, :], a[f"L{l}_token"]).then_inc(token_loaded, 16)
            tiles["sync"](sp)
            sp.wait_ge(padded, 4)
            for k in range(NCH, NCH + 3):
                sp.dma_start(g["seq"][k], sq[:, B, 0:CW]).then_inc(stored, 16)
            for b in range(B):
                sp.wait_ge(placed, 2 * TPB * (b + 1))
                for c in range(CPB):
                    sp.dma_start(g["seq"][CPB * b + c], sq[:, b, c * TC:c * TC + CW]).then_inc(stored, 16)
            sp.wait_ge(stored, 16 * (NCH + 3))
            tiles["sync_end"](sp)


def phase_mamba(nc, a, g, l):
    with ExitStack() as ctx:
        sb, ps, sem = memory(nc, ctx, f"mamba{l}", g["used"])
        T, m, sel = g["T"], g["mamba"][l], g["sel"]
        xs = sb("xs", [P, CW - 1])
        u, sz = sb("u", [P, UBUFS, TC]), sb("sz", [P, UBUFS, TC])
        ab, ex, w1, ln, rx = sb("ab", [P, TC]), sb("ex", [P, TC]), sb("w1", [P, TC]), sb("ln", [P, TC]), sb("rx", [P, TC])
        rr, lr = sb("rr", [P, TC]), sb("lr", [P, TC])
        dd = sb("dd", [P, 2, TC])
        bc = sb("bc", [2 * DS, TC])
        rep = sb("rep", [P, 2 * REP_ROWS, TC])
        dbu, hc = sb("dbu", [P, 4, TC]), sb("hc", [P, 4, TC])
        carry = sb("carry", [P, ITEMS])
        y = sb("y", [P, NCH * TC])
        yp = sb("yp", [P, 2, R * R, HW])
        stats, vare, mhalf = sb("stats", [TT, NT, 6]), sb("vare", [TT, NT]), sb("mhalf", [TT, GT])
        state = ps("state", [P, BANKS, BANK])
        ysum, front = ps("ysum", [P, BANK]), ps("front", [P, 2, BANK])

        xs_loaded, rep_loaded, bc_stored, dt_stored = sem("xs_loaded"), sem("rep_loaded"), sem("bc_stored"), sem("dt_stored")
        front_mm, front_act, front_dve, front_pool = sem("front_mm"), sem("front_act"), sem("front_dve"), sem("front_pool")
        decay_ready, dbu_ready, scan_done, carry_done = sem("decay_ready"), sem("dbu_ready"), sem("scan_done"), sem("carry_done")
        hc_ready, hc_summed, carry_zeroed = sem("hc_ready"), sem("hc_summed"), sem("carry_zeroed")
        y_ready, projected, added = sem("y_ready"), sem("projected"), sem("added")
        unshuffled, stats_ready, mv_ready = sem("unshuffled"), sem("stats_ready"), sem("mv_ready")
        half_ready, vare_ready, rstd_ready = sem("half_ready"), sem("vare_ready"), sem("rstd_ready")
        MM_U, MM_Z, MM_DT, MM_BC, MMS = 1, 2, 3, 4, 4
        A_U, A_Z, A_ABS, A_RELU, A_EXP, A_ONE, A_BC, A_LN, ACTS = 1, 2, 3, 4, 5, 6, 7, 8, 8
        D_R, D_LR, D_DT, DVES = 1, 2, 3, 3
        REPS = 2 * NS
        block = ctx.enter_context(nc.Block())

        def chunk_of(eng, tile, k):
            if isinstance(k, int):
                return tile[:, k % UBUFS, :]
            return tile[:, bass.ds(eng.snap(k % UBUFS), 1), :]

        @block.sync
        def _(sp):
            def load_xs(k):
                for s in range(2):
                    src = g["seq"][bass.ds(k, 1), :, s:s + CW - 1].rearrange("o c n -> (o c) n")
                    sp.dma_start(xs[s * DM:(s + 1) * DM, :], src).then_inc(xs_loaded, 16)

            def half(k):
                return k % 2 if isinstance(k, int) else sp.snap(k % 2)

            def bc_scratch(k):
                return g["bc_rows"][bass.ds(half(k), 1), :, :]

            def rep_row(k):
                return k % 2 * REP_ROWS if isinstance(k, int) else sp.snap(k % 2 * REP_ROWS)

            def store_bc(k):
                rows = bc_scratch(k).rearrange("o w n -> (o w) n")
                sp.wait_ge(front_act, START + ACTS * k + A_BC)
                sp.dma_start(rows, bc[:, :]).then_inc(bc_stored, 16)

            def store_dt(k):
                rows = g["dt_rows"].rearrange("(w p) n -> p w n", p=P)
                sp.wait_ge(front_pool, START + k + 1)
                sp.dma_start(rows, dd[:, :, :]).then_inc(dt_stored, 16)

            def replicate_bc(k):
                rows, row = bc_scratch(k), rep_row(k)
                sp.wait_ge(bc_stored, 16 * (k + 1))
                for s in range(NS):
                    src = rows.rearrange("o (w s) n -> s (o w) n", s=NS)[s:s + 1]
                    sp.dma_start(rep[s * DG:(s + 1) * DG, bass.ds(row + 2 * NG, 2 * NM), :],
                                 src.broadcast_to([DG, 2 * NM, TC])).then_inc(rep_loaded, 16)

            def replicate_dt(k):
                row = rep_row(k)
                src = g["dt_rows"].rearrange("(w d) n -> d w n", d=DG)
                sp.wait_ge(dt_stored, 16 * (k + 1))
                for s in range(NS):
                    sp.dma_start(rep[s * DG:(s + 1) * DG, bass.ds(row, 2 * NG), :], src).then_inc(rep_loaded, 16)

            replicas = sp.alloc_register(f"replicas{l}")
            load_xs(0)
            sp.wait_ge(front_mm, START + MM_Z)
            load_xs(1)
            store_bc(0)
            replicate_bc(0)
            store_dt(0)
            replicate_dt(0)
            sp.wait_ge(front_mm, START + MMS + MM_Z)
            load_xs(2)
            store_bc(1)
            with sp.Fori(0, NCH) as k:
                sp.reg_mul(replicas, k, 16 * REPS)
                sp.reg_add(replicas, replicas, 16 * REPS)
                replicas_before = sp.snap(replicas)
                items_before = START + ITEMS * k
                sp.wait_ge(decay_ready, items_before)
                sp.wait_ge(dbu_ready, items_before)
                sp.wait_ge(hc_ready, items_before)
                sp.wait_ge(rep_loaded, replicas_before)
                replicate_bc(k + 1)
                store_dt(k + 1)
                replicate_dt(k + 1)
                sp.wait_ge(front_mm, START + MMS * (k + 2) + MM_Z)
                load_xs(k + 3)
                store_bc(k + 2)
            sp.wait_ge(rep_loaded, 16 * REPS * (NCH + 1))
            sp.wait_ge(bc_stored, 16 * (NCH + 2))
            sp.wait_ge(xs_loaded, 32 * (NCH + 3))

        @block.tensor
        def _(pe):
            for s in (front_mm, hc_summed, projected):
                pe.sem_inc(s, START)

            def prep_u(k):
                pe.wait_ge(xs_loaded, 32 * (k + 1))
                pe.wait_ge(front_act, START + ACTS * k)
                nc.tensor.matmul(front[:, 0, 0:TC], m["wu"][:, 0, :], xs[:, 0:TC], start=True, stop=False)
                nc.tensor.matmul(front[:, 0, 0:TC], m["wu"][:, 1, :], xs[:, 2:2 + TC],
                                 start=False, stop=True).then_inc(front_mm, 1)

            def prep_z(k):
                nc.tensor.matmul(front[:, 1, 0:TC], m["wz"][:, :], xs[:, 2:2 + TC],
                                 start=True, stop=True).then_inc(front_mm, 1)

            def prep_dt(k):
                pe.wait_ge(front_act, START + ACTS * k + A_Z)
                nc.tensor.matmul(front[:, 0, 0:TC], m["wdt"][:, :], chunk_of(pe, u, k),
                                 start=True, stop=True).then_inc(front_mm, 1)

            def prep_bc(k):
                nc.tensor.matmul(front[0:2 * DS, 1, 0:TC], m["wbc"][:, :], chunk_of(pe, u, k),
                                 start=True, stop=True).then_inc(front_mm, 1)

            for k in range(2):
                prep_u(k)
                prep_z(k)
                prep_dt(k)
                prep_bc(k)
            with pe.Fori(0, NCH) as k:
                prep_u(k + 2)
                prep_z(k + 2)
                pe.wait_ge(y_ready, START + k)
                nc.tensor.matmul(ysum[:, 0:TC], m["diag"][:, :], chunk_of(pe, u, k), start=True, stop=False)
                for i in range(ITEMS):
                    pe.wait_ge(hc_ready, START + ITEMS * k + i + 1)
                    nc.tensor.matmul(ysum[:, 0:TC], sel[:, i // NM, :], hc[:, i % 4, :],
                                     start=False, stop=(i == ITEMS - 1)).then_inc(hc_summed, 1)
                    if i == AT_DT:
                        prep_dt(k + 2)
                    if i == AT_DT + 1:
                        prep_bc(k + 2)
            pe.wait_ge(front_act, START + ACTS * (NCH + 2))
            for t in range(NT):
                b, j = divmod(t, TPB)
                pe.wait_ge(unshuffled, R * (b + 1))
                pe.wait_ge(added, START + t - 1)
                out = front[0:TT, t % 2, 0:C].rearrange("p (c q) -> p q c", q=R * R)
                for q in range(R * R):
                    mm = nc.tensor.matmul(out[:, q, :], yp[:, b % 2, q, j * TT:(j + 1) * TT], m["wout"][:, :],
                                          start=True, stop=True, skip_group_check=True)
                mm.then_inc(projected, 1)

        def planes(b, i):
            at = b * CPB * TC + 1
            src = y[:, at:at + HW * R * R].rearrange("d (h i w q) -> d i q h w", h=H, i=R, w=W, q=R)[:, i]
            return src, yp[:, b % 2, R * i:R * i + R, :].rearrange("d q (h w) -> d q h w", h=H)

        @block.scalar
        def _(act):
            act.sem_inc(front_act, START)
            act.sem_inc(decay_ready, START)
            at = act.alloc_register(f"act_row{l}")
            conv_b, dt_b = m["vec"][:, 0:1], m["vec"][:, 1:2]

            def out_of(tile, k):
                if isinstance(k, int):
                    return tile[:, k % UBUFS, :]
                act.reg_add(at, act.snap(k % UBUFS), 0)
                return tile[:, bass.ds(act.snap(at), 1), :]

            def prep_silu(k):
                act.wait_ge(front_mm, START + MMS * k + MM_Z)
                act.wait_ge(y_ready, START + k - UBUFS + 1)
                nc.scalar.activation(out_of(u, k), front[:, 0, 0:TC], ACT.Silu, bias=conv_b).then_inc(front_act, 1)
                nc.scalar.activation(out_of(sz, k), front[:, 1, 0:TC], ACT.Silu).then_inc(front_act, 1)

            def prep_exp(k):
                act.wait_ge(front_mm, START + MMS * k + MM_DT)
                act.wait_ge(front_dve, START + DVES * k)
                nc.scalar.activation(ab[:, :], front[:, 0, 0:TC], ACT.Abs, bias=dt_b).then_inc(front_act, 1)
                nc.scalar.activation(rx[:, :], front[:, 0, 0:TC], ACT.Relu, bias=dt_b).then_inc(front_act, 1)
                act.wait_ge(front_act, START + ACTS * k + A_ABS)
                nc.scalar.activation(ex[:, :], ab[:, :], ACT.Exp, scale=-1.0).then_inc(front_act, 1)

            def prep_one(k):
                act.wait_ge(front_act, START + ACTS * k + A_EXP)
                nc.scalar.activation(w1[:, :], ex[:, :], ACT.Copy, bias=1.0).then_inc(front_act, 1)

            def prep_ln(k):
                nc.scalar.activation(ln[:, :], ex[:, :], ACT.Ln, bias=1.0).then_inc(front_act, 1)

            def prep_bc(k):
                act.wait_ge(front_mm, START + MMS * k + MM_BC)
                if not (isinstance(k, int) and k == 0):
                    act.wait_ge(bc_stored, 16 * k)
                nc.scalar.activation(bc[:, :], front[0:2 * DS, 1, 0:TC], ACT.Copy).then_inc(front_act, 1)

            for k in range(2):
                prep_silu(k)
                prep_exp(k)
                prep_one(k)
                prep_bc(k)
                prep_ln(k)
            nc.scalar.preload_act_table_set("exp_and_others")
            with act.Fori(0, NCH // 2) as pair:
                for par in range(2):
                    k = pair * 2 + par
                    act.wait_ge(rep_loaded, 16 * REPS * (k + 1))
                    for i in range(ITEMS):
                        last = i - STATE_GAP[i]
                        if SECOND[last]:
                            act.wait_ge(hc_ready, START + ITEMS * k + last + 1)
                        else:
                            before = 0 if last >= 0 else COPIES[-1]
                            act.wait_ge(carry_done, START + COPIES[-1] * k + COPIES[last] - before)
                        nc.scalar.activation(state[:, STATE_BANK[i], 0:TC], rep[:, par * REP_ROWS + i // NM, :], ACT.Exp,
                                             scale=m["acol"][:, i:i + 1]).then_inc(decay_ready, 1)
                        if i == AT_SILU:
                            prep_silu(k + 2)
                        if i == AT_EXP:
                            prep_exp(k + 2)
                        if i == AT_ONE:
                            prep_one(k + 2)
                        if i == AT_BC:
                            prep_bc(k + 2)
                        if i == AT_LN:
                            prep_ln(k + 2)
            for b in range(B):
                act.wait_ge(y_ready, START + NCH)
                if b >= 2:
                    act.wait_ge(projected, START + TPB * (b - 1))
                for i in range(R):
                    src, dst = planes(b, i)
                    nc.scalar.activation(dst, src, ACT.Copy).then_inc(unshuffled, 1)

        @block.gpsimd
        def _(pool):
            pool.sem_inc(dbu_ready, START)
            pool.sem_inc(front_pool, START)
            at = pool.alloc_register(f"pool_row{l}")

            def prep(k):
                pool.wait_ge(front_dve, START + DVES * k + D_DT)
                if isinstance(k, int):
                    u_k = u[:, k % UBUFS, :]
                else:
                    pool.reg_add(at, pool.snap(k % UBUFS), 0)
                    u_k = u[:, bass.ds(pool.snap(at), 1), :]
                pool.tensor_tensor(dd[:, 1, :], dd[:, 0, :], u_k, ALU.mult).then_inc(front_pool, 1)

            prep(0)
            with pool.Fori(0, NCH // 2) as pair:
                for par in range(2):
                    k = pair * 2 + par
                    first = par * REP_ROWS
                    pool.wait_ge(rep_loaded, 16 * REPS * (k + 1))
                    for i in range(ITEMS):
                        pool.wait_ge(scan_done, START + ITEMS * k + i - 3)
                        pool.tensor_tensor(dbu[:, i % 4, :], rep[:, first + NG + i // NM, :], rep[:, first + 2 * NG + i % NM, :],
                                           ALU.mult).then_inc(dbu_ready, 1)
                        if i == AT_DTU:
                            prep(k + 1)
            pool.memset(mhalf[:, :], -0.5).then_inc(half_ready, 1)
            pool.wait_ge(half_ready, 1)
            for k in range(NT // GT):
                own = slice(k * GT, (k + 1) * GT)
                pool.wait_ge(vare_ready, k + 1)
                pool.tensor_tensor(g["rstd"][:, own], vare[:, own], mhalf[:, :], ALU.pow).then_inc(rstd_ready, 1)

        @block.vector
        def _(dve):
            for s in (scan_done, carry_done, hc_ready, front_dve, y_ready, added):
                dve.sem_inc(s, START)

            def prep(k):
                done = START + DVES * k
                dve.wait_ge(front_act, START + ACTS * k + A_ONE)
                nc.vector.scalar_tensor_tensor(out=rr[:, :], in0=w1[:, :], scalar=1.0, in1=ex[:, :],
                                               op0=ALU.subtract, op1=ALU.subtract).then_inc(front_dve, 1)
                dve.wait_ge(front_act, START + ACTS * k + A_LN)
                dve.wait_ge(front_dve, done + D_R)
                nc.vector.tensor_tensor(lr[:, :], ln[:, :], rr[:, :], ALU.subtract).then_inc(front_dve, 1)
                if not (isinstance(k, int) and k == 0):
                    dve.wait_ge(dt_stored, 16 * k)
                dve.wait_ge(front_dve, done + D_LR)
                nc.vector.tensor_tensor(dd[:, 0, :], lr[:, :], rx[:, :], ALU.add).then_inc(front_dve, 1)

            for k in range(2):
                prep(k)
            with dve.Fori(0, B) as b:
                dve.wait_ge(carry_done, START + COPIES[-1] * CPB * b)
                nc.vector.memset(carry[:, :], 0.0).then_inc(carry_zeroed, 1)
                with dve.Fori(0, CPB) as c:
                    k = dve.snap(b * CPB + c)
                    dve.wait_ge(carry_zeroed, b + 1)
                    dve.wait_ge(rep_loaded, 16 * REPS * (k + 1))
                    c_rows = dve.snap(k % 2 * REP_ROWS)

                    def read_out(i):
                        dve.wait_ge(scan_done, START + ITEMS * k + i + 1)
                        dve.wait_ge(hc_summed, START + ITEMS * k + i - 3)
                        nc.vector.tensor_tensor(hc[:, i % 4, :], state[:, STATE_BANK[i], 0:TC],
                                                rep[:, bass.ds(c_rows + 3 * NG + i % NM, 1), :],
                                                ALU.mult).then_inc(hc_ready, 1)
                        if not SECOND[i]:
                            n = 2 if PAIRED[i] else 1
                            dve.wait_ge(scan_done, START + ITEMS * k + i + n)
                            nc.vector.tensor_copy(carry[:, i:i + n], state[:, STATE_BANK[i]:STATE_BANK[i] + n, TC - 1]).then_inc(carry_done, 1)

                    for i in range(ITEMS):
                        n = START + ITEMS * k + i
                        dve.wait_ge(decay_ready, n + 1)
                        dve.wait_ge(dbu_ready, n + 1)
                        bank = state[:, STATE_BANK[i], 0:TC]
                        nc.vector.tensor_tensor_scan(bank, bank, dbu[:, i % 4, :],
                                                     carry[:, i:i + 1], ALU.mult, ALU.add).then_inc(scan_done, 1)
                        if i > 0:
                            read_out(i - 1)
                    read_out(ITEMS - 1)
                    prep(k + 2)
                    dve.wait_ge(hc_summed, START + ITEMS * (k + 1))
                    nc.vector.tensor_tensor(y[:, bass.ds(k * TC, TC)], ysum[:, 0:TC], chunk_of(dve, sz, k),
                                            ALU.mult).then_inc(y_ready, 1)
            for s in range(NT + 2):
                if s < NT:
                    dve.wait_ge(projected, START + s + 1)
                    nc.vector.tensor_tensor(T[:, s, :], T[:, s, :], front[0:TT, s % 2, 0:C], ALU.add).then_inc(added, 1)
                t = s - 1
                if 0 <= t < NT:
                    dve.wait_ge(added, START + t + 1)
                    nc.vector.bn_stats(stats[:, t, :], T[:, t, :]).then_inc(stats_ready, 1)
                t = s - 2
                if 0 <= t < NT:
                    dve.wait_ge(stats_ready, t + 1)
                    nc.vector.bn_aggr(g["mv"][:, t, :], stats[:, t, :]).then_inc(mv_ready, 1)
                if t >= 0 and (t + 1) % GT == 0:
                    own = slice(t + 1 - GT, t + 1)
                    dve.wait_ge(mv_ready, t + 1)
                    nc.vector.tensor_scalar(vare[:, own], g["mv"][:, own, 1], 1e-5, None, ALU.add).then_inc(vare_ready, 1)


def phase_route(nc, a, g, l, prefetch):
    top = TOPK[l]
    with ExitStack() as ctx:
        sb, ps, sem = memory(nc, ctx, f"route{l}", g["used"])
        T, ident = g["T"], g["ident"]
        mv, rstd = g["mv"], g["rstd"]
        xn = g["xn"]
        xT = sb("xT", [P, 2, 2 * TT])
        wr = sb("wr", [P, 2, NE])
        lg, best, which = sb("lg", [TT, NT, NE]), sb("best", [TT, NT, NE]), sb("which", [TT, NT, NE], U32)
        whichf = sb("whichf", [TT, 2, NT])
        eid = sb("eid", [TT, NE, NT])
        one = sb("one", [TT, 2, NE, NT])
        both, picked = sb("both", [TT, NE, NT]), sb("picked", [TT, NE, NT])
        before, ones = sb("before", [TT, TT]), sb("ones", [TT, TT])
        tot, cum, prev = sb("tot", [TT, NE, NT]), sb("cum", [TT, NE * NT]), sb("prev", [TT, NE, NT])
        pos, count = sb("pos", [TT, NE, NT]), sb("count", [TT, NE])
        steps128, over = sb("steps128", [TT, NE, MAXT]), sb("over", [TT, NE, MAXT])
        tiles, ends, first = sb("tiles", [TT, NE]), sb("ends", [TT, NE]), sb("first", [TT, NE])
        slotf, kept = sb("slotf", [TT, 2, NT]), sb("kept", [TT, NT])
        token, base = sb("token", [TT, NT]), sb("base", [TT, NT])
        tile_id, passed, owner = sb("tile_id", [1, RTILES, NE]), sb("passed", [1, RTILES, NE]), sb("owner", [1, RTILES])
        dif, ee, den, prob = sb("dif", [TT, NT, NE]), sb("ee", [TT, NT, NE]), sb("den", [TT, NT]), sb("prob", [TT, NT])
        tp, lgp = ps("tp", [P, 2, BANK]), ps("lgp", [TT, B, BANK])
        rank_ps, tot_ps = ps("rank", [TT, BANK]), ps("tot_ps", [TT, BANK])
        top_steps = sem("top_steps")
        xn_ready, turned, xT_ready, scored = sem("xn_ready"), sem("turned"), sem("xT_ready"), sem("scored")
        consts, wr_loaded, one_ready, counted = sem("consts"), sem("wr_loaded"), sem("one_ready"), sem("counted")
        steps, exp_asked, exp_ready, slots_ready = sem("steps"), sem("exp_asked"), sem("exp_ready"), sem("slots_ready")
        straight = sem("straight")
        block = ctx.enter_context(nc.Block())

        @block.sync
        def _(sp):
            sp.dma_start(wr[:, :, :], a[f"L{l}_wrT"].rearrange("(k p) e -> p k e", p=P)).then_inc(wr_loaded, 16)
            prefetch(sp)
            if l == 0:
                for t in range(NT):
                    sp.wait_ge(xn_ready, t + 1)
                    sp.dma_start(g["xs"][t * TT:(t + 1) * TT, :], xn[:, t, :]).then_inc(straight, 16)
                sp.wait_ge(straight, 16 * NT)

        @block.gpsimd
        def _(pool):
            pool.memset(before[:, :], 1.0).then_inc(consts, 1)
            pool.memset(ones[:, :], 1.0).then_inc(consts, 1)
            pool.iota(eid[:, :, :], pattern=[[1, NE], [0, NT]], base=0, channel_multiplier=0,
                      allow_small_or_imprecise_dtypes=True).then_inc(consts, 1)
            pool.iota(steps128[:, :, :], pattern=[[0, NE], [P, MAXT]], base=0, channel_multiplier=0,
                      allow_small_or_imprecise_dtypes=True).then_inc(consts, 1)
            pool.iota(tile_id[:, :, :], pattern=[[1, RTILES], [0, NE]], base=0, channel_multiplier=0,
                      allow_small_or_imprecise_dtypes=True).then_inc(consts, 1)
            pool.iota(token[:, :], pattern=[[TT, NT]], base=0, channel_multiplier=1,
                      allow_small_or_imprecise_dtypes=True).then_inc(consts, 1)
            pool.wait_ge(consts, 6)
            pool.affine_select(out=before[:, :], in_=before[:, :], compare_op=ALU.is_gt, fill=0.0,
                               base=0, pattern=[[1, TT]], channel_multiplier=-1).then_inc(consts, 1)

        @block.tensor
        def _(pe):
            pe.wait_ge(wr_loaded, 16)
            def score(t):
                pe.wait_ge(xT_ready, t + 1)
                for k in range(2):
                    mm = nc.tensor.matmul(lgp[:, t // TPB, t % TPB * NE:(t % TPB + 1) * NE], xT[:, t % 2, k * TT:(k + 1) * TT], wr[:, k, :],
                                          start=(k == 0), stop=(k == 1), skip_group_check=True)
                mm.then_inc(scored, 1)
            for t in range(NT):
                pe.wait_ge(xn_ready, t + 1)
                if t >= 2:
                    pe.wait_ge(xT_ready, t - 1)
                for k in range(2):
                    mm = nc.tensor.transpose(tp[:, t % 2, k * TT:(k + 1) * TT], xn[:, t, k * P:(k + 1) * P], ident[0:TT, 0:TT])
                mm.then_inc(turned, 1)
                if t >= 1:
                    score(t - 1)
            score(NT - 1)
            pe.wait_ge(one_ready, 1)
            pe.wait_ge(consts, 7)
            flat = both[:, :, :].rearrange("p e t -> p (e t)")
            nc.tensor.matmul(rank_ps[:, 0:NE * NT], before[:, :], flat, start=True, stop=True).then_inc(counted, 1)
            nc.tensor.matmul(tot_ps[:, 0:NE * NT], ones[:, :], flat, start=True, stop=True).then_inc(counted, 1)

        @block.scalar
        def _(act):
            for t in range(NT):
                act.wait_ge(turned, t + 1)
                if t >= 2:
                    act.wait_ge(scored, t - 1)
                nc.scalar.activation(xT[:, t % 2, :], tp[:, t % 2, 0:2 * TT], ACT.Copy).then_inc(xT_ready, 1)
            act.wait_ge(exp_asked, 1)
            if l == 0:
                nc.scalar.activation(ee[:, :, 0], dif[:, :, 0], ACT.Exp).then_inc(exp_ready, 1)
            else:
                nc.scalar.activation(ee[:, :, :], dif[:, :, :], ACT.Exp).then_inc(exp_ready, 1)

        @block.vector
        def _(dve):
            done = [0]

            def then(ins):
                done[0] += 1
                ins.then_inc(steps, 1)
                dve.wait_ge(steps, done[0])

            def over_tiles(x):
                return x.unsqueeze(1).broadcast_to([TT, NE, NT])

            for t in range(NT):
                nc.vector.tensor_scalar(xn[:, t, :], T[:, t, :], mv[:, t, 0:1], rstd[:, t:t + 1],
                                        ALU.subtract, ALU.mult).then_inc(xn_ready, 1)
            for b in range(B):
                own = range(b * TPB, (b + 1) * TPB)
                dve.wait_ge(scored, (b + 1) * TPB)
                then(nc.vector.tensor_copy(lg[:, b * TPB:(b + 1) * TPB, :],
                                           lgp[:, b, 0:TPB * NE].rearrange("p (t e) -> p t e", t=TPB)))
                for t in own:
                    nc.vector.max(best[:, t, :], lg[:, t, :]).then_inc(top_steps, 1)
                dve.wait_ge(top_steps, (2 * b + 1) * TPB)
                for t in own:
                    nc.vector.max_index(which[:, t, :], best[:, t, :], lg[:, t, :]).then_inc(top_steps, 1)
            dve.wait_ge(top_steps, 2 * NT)
            if l == 0:
                then(nc.vector.tensor_tensor(dif[:, :, 0], best[:, :, 1], best[:, :, 0], ALU.subtract))
            else:
                then(nc.vector.tensor_tensor(dif[:, :, :], lg[:, :, :], best[:, :, 0:1].broadcast_to([TT, NT, NE]), ALU.subtract))
            dve.sem_inc(exp_asked, 1)
            dve.wait_ge(consts, 7)
            for c in range(top):
                then(nc.vector.tensor_copy(whichf[:, c, :], which[:, :, c]))
                then(nc.vector.tensor_tensor(one[:, c, :, :], over_tiles(whichf[:, c, :]), eid[:, :, :], ALU.is_equal))
            if top == 2:
                nc.vector.tensor_tensor(both[:, :, :], one[:, 0, :, :], one[:, 1, :, :], ALU.add).then_inc(one_ready, 1)
            else:
                nc.vector.tensor_copy(both[:, :, :], one[:, 0, :, :]).then_inc(one_ready, 1)
            dve.wait_ge(exp_ready, 1)
            if l == 0:
                then(nc.vector.tensor_scalar(den[:, :], ee[:, :, 0], 1.0, None, ALU.add))
                then(nc.vector.reciprocal(g["share"][:, 0, :], den[:, :]))
                then(nc.vector.tensor_tensor(g["share"][:, 1, :], g["share"][:, 0, :], ee[:, :, 0], ALU.mult))
            else:
                then(nc.vector.tensor_reduce(den[:, :], ee[:, :, :], AX_X, ALU.add))
                then(nc.vector.reciprocal(prob[:, :], den[:, :]))
            dve.wait_ge(counted, 2)
            then(nc.vector.tensor_copy(tot[:, :, :].rearrange("p e t -> p (e t)"), tot_ps[:, 0:NE * NT]))
            flat = tot[:, :, :].rearrange("p e t -> p (e t)")
            then(nc.vector.memset(cum[:, :], 0.0))
            then(nc.vector.tensor_tensor_scan(prev[:, :, :].rearrange("p e t -> p (e t)"), flat, cum[:, :], 0.0, ALU.add, ALU.add))
            then(nc.vector.tensor_tensor(prev[:, :, :], prev[:, :, :], tot[:, :, :], ALU.subtract))
            then(nc.vector.tensor_copy(first[:, :], prev[:, :, 0]))
            then(nc.vector.tensor_tensor(prev[:, :, :], prev[:, :, :], first[:, :].unsqueeze(2).broadcast_to([TT, NE, NT]), ALU.subtract))
            then(nc.vector.tensor_tensor(count[:, :], prev[:, :, NT - 1], tot[:, :, NT - 1], ALU.add))
            then(nc.vector.tensor_tensor(pos[:, :, :], prev[:, :, :], rank_ps[:, 0:NE * NT].rearrange("p (e t) -> p e t", e=NE), ALU.add))
            if l == 0:
                then(nc.vector.tensor_tensor(over[:, :, :], count[:, :].unsqueeze(2).broadcast_to([TT, NE, MAXT]), steps128[:, :, :], ALU.is_gt))
                then(nc.vector.tensor_reduce(tiles[:, :], over[:, :, :], AX_X, ALU.add))
                then(nc.vector.tensor_tensor_scan(ends[:, :], tiles[:, :], cum[:, 0:NE], 0.0, ALU.add, ALU.add))
                then(nc.vector.tensor_tensor(first[:, :], ends[:, :], tiles[:, :], ALU.subtract))
                then(nc.vector.tensor_scalar(first[:, :], first[:, :], float(P), float(B * HW), ALU.mult, ALU.add))
                then(nc.vector.tensor_tensor(pos[:, :, :], pos[:, :, :], first[:, :].unsqueeze(2).broadcast_to([TT, NE, NT]), ALU.add))
                then(nc.vector.tensor_tensor(passed[:, :, :], ends[0:1, :].unsqueeze(1).broadcast_to([1, RTILES, NE]), tile_id[:, :, :], ALU.is_le))
                then(nc.vector.tensor_reduce(owner[:, :], passed[:, :, :], AX_X, ALU.add))
                then(nc.vector.tensor_scalar(owner[:, :], owner[:, :], float(NE - 1), None, ALU.min))
                then(nc.vector.tensor_copy(g["owner"][:, STILES:STILES + RTILES], owner[:, :]))
                then(nc.vector.memset(owner[:, 0:STILES], float(NE)))
                then(nc.vector.tensor_copy(g["owner"][:, 0:STILES], owner[:, 0:STILES]))
            for c in range(top):
                then(nc.vector.tensor_tensor(picked[:, :, :], one[:, c, :, :], pos[:, :, :], ALU.mult))
                then(nc.vector.tensor_reduce(slotf[:, c, :], picked[:, :, :].rearrange("p e t -> p t e"), AX_X, ALU.add))
            if l == 0:
                nc.vector.tensor_copy(g["slot"][:, :, :], slotf[:, :, :]).then_inc(slots_ready, 1)
            else:
                then(nc.vector.tensor_scalar(kept[:, :], slotf[:, 0, :], float(CAP), None, ALU.is_lt))
                then(nc.vector.tensor_tensor(g["share"][:, 0, :], prob[:, :], kept[:, :], ALU.mult))
                then(nc.vector.tensor_scalar(base[:, :], whichf[:, 0, :], float(CAP), None, ALU.mult))
                then(nc.vector.tensor_tensor(slotf[:, 0, :], slotf[:, 0, :], base[:, :], ALU.add))
                then(nc.vector.tensor_scalar(token[:, :], token[:, :], float(NE * CAP), None, ALU.add))
                then(nc.vector.tensor_tensor(slotf[:, 0, :], slotf[:, 0, :], token[:, :], ALU.subtract))
                then(nc.vector.tensor_tensor(slotf[:, 0, :], slotf[:, 0, :], kept[:, :], ALU.mult))
                then(nc.vector.tensor_tensor(slotf[:, 0, :], slotf[:, 0, :], token[:, :], ALU.add))
                then(nc.vector.tensor_scalar(slotf[:, 1, :], slotf[:, 0, :], float(NE * CAP - 1), None, ALU.min))
                nc.vector.tensor_copy(g["slot"][:, :, :], slotf[:, :, :]).then_inc(slots_ready, 1)


def scatter(nc, pool, g, top, sent):
    for t in range(NT):
        for c in range(top):
            pool.indirect_dma_start(out=g["xs"][:, :], out_offset=bass.IndirectOffsetOnAxis(ap=g["slot"][:, c, t:t + 1], axis=0),
                                    in_=g["xn"][:, t, :], in_offset=None).then_inc(sent, 16)


def weights0(nc, a, g, ctx):
    sb, ps, sem = memory(nc, ctx, "weights0", g["used"])
    w = {"gu": sb("wgu", [P, NE + 1, 2, 2, F0]),
         "d": sb("wd", [P, NE + 1, FC0, C]),
         "shared_loaded": sem("shared_loaded"), "routed_loaded": sem("routed_loaded")}

    def load(sp, e, w_g, w_u, w_d, done):
        for which, src in ((0, w_g), (1, w_u)):
            sp.dma_start(w["gu"][:, e, which, :, :], src.rearrange("(k p) f -> p k f", p=P)).then_inc(done, 16)
        sp.dma_start(w["d"][:, e, :, :], w_d.rearrange("(f p) c -> p f c", p=P)).then_inc(done, 16)

    def load_routed(sp, e):
        load(sp, e, a["L0_wg"][e], a["L0_wu"][e], a["L0_wd"][e], w["routed_loaded"])

    def prefetch(sp):
        load(sp, NE, a["L0_sg"], a["L0_su"], a["L0_sd"], w["shared_loaded"])
        for e in range(AHEAD):
            load_routed(sp, e)

    w["load_routed"] = load_routed
    return w, prefetch


def phase_experts0(nc, a, g, w):
    with ExitStack() as ctx:
        sb, ps, sem = memory(nc, ctx, "experts0", g["used"])
        ident, wgu, wd = g["ident"], w["gu"], w["d"]
        xs, xT = sb("xs", [P, 2, C]), sb("xT", [P, 2, C])
        sg, h, hT, eo = sb("sg", [P, 2, F0]), sb("h", [P, 2, F0]), sb("hT", [P, 2, F0]), sb("eo", [P, 2, C])
        tp, gate, up = ps("tp", [P, BANK]), ps("gate", [P, 2, BANK]), ps("up", [P, 2, BANK])
        htp, down = ps("htp", [P, BANK]), ps("down", [P, 2, BANK])
        sent = sem("sent")
        x_loaded, stored = [sem("x_loaded0"), sem("x_loaded1")], [sem("stored0"), sem("stored1")]
        turned, xT_ready, gate_done, up_done = sem("turned"), sem("xT_ready"), sem("gate_done"), sem("up_done")
        sg_ready, h_ready, h_turned, hT_ready = sem("sg_ready"), sem("h_ready"), sem("h_turned"), sem("hT_ready")
        down_done, eo_ready = sem("down_done"), sem("eo_ready")
        block = ctx.enter_context(nc.Block())
        TILES, LOADS = STILES + RTILES, 3

        def tile(i, off):
            return 2 * i + off, off % 2, i + off // 2

        @block.gpsimd
        def _(pool):
            scatter(nc, pool, g, TOPK[0], sent)

        @block.sync
        def _(sp):
            def load_x(t):
                n, par, _ = t
                if not isinstance(n, int) or n > 1:
                    sp.wait_ge(turned, START + n - 1)
                sp.dma_start(xs[:, par, :], g["xs"][bass.ds(n * P, P), :]).then_inc(x_loaded[par], 16)

            def store(t):
                n, par, _ = t
                sp.wait_ge(eo_ready, START + n + 1)
                sp.dma_start(g["eo"][bass.ds(n * P, P), :], eo[:, par, :]).then_inc(stored[par], 16)

            def two_tiles(i):
                load_x(tile(i, 1))
                store(tile(i - 1, 0))
                load_x(tile(i, 2))
                store(tile(i - 1, 1))

            for off in range(3):
                load_x(tile(0, off))
            for i in range(1, NE - AHEAD + 1):
                two_tiles(i)
                w["load_routed"](sp, AHEAD + i - 1)
            with sp.Fori(NE - AHEAD + 1, STILES // 2 - 1) as i:
                two_tiles(i)
            load_x(tile(STILES // 2 - 1, 1))
            store(tile(STILES // 2 - 2, 0))
            sp.wait_ge(sent, 16 * NT * TOPK[0])
            load_x(tile(STILES // 2, 0))
            store(tile(STILES // 2 - 2, 1))
            with sp.Fori(STILES // 2, TILES // 2 - 1) as i:
                two_tiles(i)
            load_x(tile(TILES // 2 - 1, 1))
            for off in range(-2, 2):
                store(tile(TILES // 2 - 1, off))
            for par in range(2):
                sp.wait_ge(stored[par], 16 * (TILES // 2))

        @block.tensor
        def _(pe):
            for s in (turned, h_turned, down_done):
                pe.sem_inc(s, START)

            def owner(t):
                return pe.value_load(g["owner"][0:1, bass.ds(t[0], 1)], min_val=0, max_val=NE)

            def turn(t):
                n, par, m = t
                pe.wait_ge(x_loaded[par], 16 * (m + 1))
                pe.wait_ge(xT_ready, START + n)
                for k in range(2):
                    mm = nc.tensor.transpose(tp[:, k * P:(k + 1) * P], xs[:, par, k * P:(k + 1) * P], ident[:, :])
                mm.then_inc(turned, 1)

            def widen(t, between):
                n, par, _ = t
                e = owner(t)
                pe.wait_ge(xT_ready, START + n + 1)
                pe.wait_ge(h_ready, START + n - 1)
                for which, bank, done in ((0, gate, gate_done), (1, up, up_done)):
                    for k in range(2):
                        mm = nc.tensor.matmul(bank[:, par, :], xT[:, par, k * P:(k + 1) * P],
                                              wgu[:, bass.ds(e, 1), which, k, :], start=(k == 0), stop=(k == 1))
                    mm.then_inc(done, 1)
                    if which == 0:
                        between()

            def turn_h(t):
                n, par, _ = t
                pe.wait_ge(h_ready, START + n + 1)
                pe.wait_ge(hT_ready, START + n)
                for f in range(FC0):
                    mm = nc.tensor.transpose(htp[:, f * P:(f + 1) * P], h[:, par, f * P:(f + 1) * P], ident[:, :])
                mm.then_inc(h_turned, 1)

            def narrow(t):
                n, par, _ = t
                e = owner(t)
                pe.wait_ge(hT_ready, START + n + 1)
                pe.wait_ge(eo_ready, START + n - 1)
                for f in range(FC0):
                    mm = nc.tensor.matmul(down[:, par, 0:C], hT[:, par, f * P:(f + 1) * P],
                                          wd[:, bass.ds(e, 1), f, :], start=(f == 0), stop=(f == FC0 - 1))
                mm.then_inc(down_done, 1)

            def two_tiles(i):
                for off in (1, 2):
                    def turns():
                        turn_h(tile(i, off - 1))
                        turn(tile(i, off + 1))
                    widen(tile(i, off), turns)
                    narrow(tile(i, off - 1))

            pe.wait_ge(w["shared_loaded"], 16 * LOADS)
            turn(tile(0, 0))
            widen(tile(0, 0), lambda: turn(tile(0, 1)))
            with pe.Fori(0, STILES // 2 - 1) as i:
                two_tiles(i)
            pe.wait_ge(w["routed_loaded"], 16 * LOADS * NE)
            with pe.Fori(STILES // 2 - 1, TILES // 2 - 1) as i:
                two_tiles(i)
            last = TILES // 2 - 1
            widen(tile(last, 1), lambda: turn_h(tile(last, 0)))
            narrow(tile(last, 0))
            turn_h(tile(last, 1))
            narrow(tile(last, 1))

        @block.scalar
        def _(act):
            for s in (xT_ready, hT_ready, eo_ready):
                act.sem_inc(s, START)

            def copy_x(t):
                n, par, _ = t
                act.wait_ge(turned, START + n + 1)
                if not (isinstance(n, int) and n < 2):
                    act.wait_ge(up_done, n - 1)
                nc.scalar.activation(xT[:, par, :], tp[:, 0:C], ACT.Copy).then_inc(xT_ready, 1)

            def silu(t):
                n, par, _ = t
                act.wait_ge(h_ready, START + n - 1)
                act.wait_ge(gate_done, n + 1)
                nc.scalar.activation(sg[:, par, :], gate[:, par, :], ACT.Silu).then_inc(sg_ready, 1)

            def copy_h(t):
                n, par, _ = t
                act.wait_ge(down_done, START + n - 1)
                act.wait_ge(h_turned, START + n + 1)
                nc.scalar.activation(hT[:, par, :], htp[:, :], ACT.Copy).then_inc(hT_ready, 1)

            def copy_out(t):
                n, par, m = t
                if not (isinstance(m, int) and m == 0):
                    act.wait_ge(stored[par], 16 * m)
                act.wait_ge(down_done, START + n + 1)
                nc.scalar.activation(eo[:, par, :], down[:, par, 0:C], ACT.Copy).then_inc(eo_ready, 1)

            def two_tiles(i):
                for off in (1, 2):
                    silu(tile(i, off))
                    copy_h(tile(i, off - 1))
                    copy_x(tile(i, off + 1))
                    copy_out(tile(i, off - 1))

            copy_x(tile(0, 0))
            silu(tile(0, 0))
            copy_x(tile(0, 1))
            two_tiles(0)
            with act.Fori(1, TILES // 2 - 1) as i:
                two_tiles(i)
            last = TILES // 2 - 1
            silu(tile(last, 1))
            for off in (0, 1):
                copy_h(tile(last, off))
                copy_out(tile(last, off))

        @block.vector
        def _(dve):
            dve.sem_inc(h_ready, START)
            with dve.Fori(0, TILES // 2) as i:
                for off in range(2):
                    n, par, _ = tile(i, off)
                    dve.wait_ge(sg_ready, n + 1)
                    dve.wait_ge(up_done, n + 1)
                    dve.wait_ge(h_turned, START + n - 1)
                    nc.vector.tensor_tensor(h[:, par, :], sg[:, par, :], up[:, par, :], ALU.mult).then_inc(h_ready, 1)


def weights1(nc, a, g, ctx):
    sb, ps, sem = memory(nc, ctx, "weights1", g["used"])
    w = {"1": sb("w1", [P, 2, 2, F1]), "2": sb("w2", [P, 2, FC1, C]),
         "b1": sb("b1", [P, NE, FC1]), "b2": sb("b2", [CT, NE, C]),
         "bias_loaded": sem("bias_loaded"), "loaded": [sem("w_loaded0"), sem("w_loaded1")]}

    def load(sp, e, par):
        one = a["L1_w1"][bass.ds(e, 1), :, :].rearrange("o (k p) f -> p (o k) f", p=P)
        sp.dma_start(w["1"][:, par, :, :], one).then_inc(w["loaded"][par], 16)
        two = a["L1_w2"][bass.ds(e, 1), :, :].rearrange("o (f p) c -> p (o f) c", p=P)
        sp.dma_start(w["2"][:, par, :, :], two).then_inc(w["loaded"][par], 16)

    def prefetch(sp):
        load(sp, 0, 0)
        load(sp, 1, 1)
        sp.dma_start(w["b1"][:, :, :], a["L1_b1"]).then_inc(w["bias_loaded"], 16)
        sp.dma_start(w["b2"][:, :, :], a["L1_b2"].unsqueeze(0).broadcast_to([CT, NE, C])).then_inc(w["bias_loaded"], 16)

    w["load"] = load
    return w, prefetch


def phase_experts1(nc, a, g, w):
    with ExitStack() as ctx:
        sb, ps, sem = memory(nc, ctx, "experts1", g["used"])
        ident = g["ident"]
        w1, w2, b1, b2, w_loaded, bias_loaded = (w[n] for n in ("1", "2", "b1", "b2", "loaded", "bias_loaded"))
        xs, xT = sb("xs", [CT, 2, CTILES, C]), sb("xT", [P, 2, 2, CAP])
        hT, eo = sb("hT", [P, FC1, CAP]), sb("eo", [CT, 2, CTILES, C])
        tp, hid, down = ps("tp", [P, 2, BANK]), ps("hid", [P, 2, BANK]), ps("down", [P, 2, BANK])
        sent = sem("sent")
        x_loaded, stored = ([sem(f"{n}{i}") for i in range(2)] for n in ("x_loaded", "stored"))
        turned, xT_ready, hid_done, hT_ready = sem("turned"), sem("xT_ready"), sem("hid_done"), sem("hT_ready")
        down_done, eo_ready = sem("down_done"), sem("eo_ready")
        block = ctx.enter_context(nc.Block())

        def every(eng, body):
            for par in range(2):
                body(par, par, 0, False)
            with eng.Fori(1, NE // 2 - 1) as i:
                for par in range(2):
                    body(i * 2 + par, par, i, False)
            for par in range(2):
                body(NE - 2 + par, par, NE // 2 - 1, par == 1)

        @block.sync
        def _(sp):
            def load_x(e, par):
                rows = g["xs"][bass.ds(e * CAP, CAP), :].rearrange("(i p) c -> p i c", p=CT)
                sp.dma_start(xs[:, par, :, :], rows).then_inc(x_loaded[par], 16)

            sp.wait_ge(sent, 16 * NT)
            load_x(0, 0)
            load_x(1, 1)
            with sp.Fori(0, NE // 2 - 1) as i:
                for par in range(2):
                    e = i * 2 + par
                    sp.wait_ge(down_done, START + CTILES * (e + 1))
                    load_x(e + 2, par)
                    w["load"](sp, e + 2, par)

        @block.tensor
        def _(pe):
            for s in (turned, down_done):
                pe.sem_inc(s, START)

            def turn(e, par, m):
                pe.wait_ge(x_loaded[par], 16 * (m + 1))
                pe.wait_ge(xT_ready, START + 2 * e)
                for k in range(2):
                    for i in range(CTILES):
                        mm = nc.tensor.transpose(tp[:, k, i * CT:(i + 1) * CT], xs[:, par, i, k * P:(k + 1) * P],
                                                 ident[0:CT, 0:CT])
                    mm.then_inc(turned, 1)

            def body(e, par, m, last):
                pe.wait_ge(w_loaded[par], 32 * (m + 1))
                pe.wait_ge(xT_ready, START + 2 * (e + 1))
                for f in range(FC1):
                    pe.wait_ge(hT_ready, START + FC1 * e + f - 1)
                    for k in range(2):
                        mm = nc.tensor.matmul(hid[:, f % 2, 0:CAP], w1[:, par, k, f * P:(f + 1) * P], xT[:, par, k, :],
                                              start=(k == 0), stop=(k == 1))
                    mm.then_inc(hid_done, 1)
                if not last:
                    turn(e + 1, 1 - par, m + par)
                pe.wait_ge(hT_ready, START + FC1 * (e + 1))
                for i in range(CTILES):
                    pe.wait_ge(eo_ready, START + CTILES * e + i - 1)
                    for f in range(FC1):
                        mm = nc.tensor.matmul(down[0:CT, i % 2, 0:C], hT[:, f, i * CT:(i + 1) * CT], w2[:, par, f, :],
                                              start=(f == 0), stop=(f == FC1 - 1))
                    mm.then_inc(down_done, 1)

            turn(0, 0, 0)
            every(pe, body)

        @block.scalar
        def _(act):
            act.sem_inc(hT_ready, START)
            act.wait_ge(bias_loaded, 32)

            def body(e, par, m, last):
                act.wait_ge(down_done, START + CTILES * e)
                for f in range(FC1):
                    bias = b1[:, e, f:f + 1] if isinstance(e, int) else b1[:, bass.ds(e, 1), f:f + 1]
                    act.wait_ge(hid_done, FC1 * e + f + 1)
                    nc.scalar.activation(hT[:, f, :], hid[:, f % 2, 0:CAP], ACT.Gelu,
                                         bias=bias).then_inc(hT_ready, 1)

            every(act, body)

        @block.vector
        def _(dve):
            for s in (xT_ready, eo_ready):
                dve.sem_inc(s, START)
            dve.wait_ge(bias_loaded, 32)

            def copy_x(e, par):
                for k in range(2):
                    dve.wait_ge(turned, START + 2 * e + k + 1)
                    nc.vector.tensor_copy(xT[:, par, k, :], tp[:, k, 0:CAP]).then_inc(xT_ready, 1)

            def body(e, par, m, last):
                if not last:
                    copy_x(e + 1, 1 - par)
                if not (isinstance(m, int) and m == 0):
                    dve.wait_ge(stored[par], 16 * m)
                for i in range(CTILES):
                    bias = b2[:, e, :] if isinstance(e, int) else b2[:, bass.ds(e, 1), :].rearrange("p o c -> p (o c)")
                    dve.wait_ge(down_done, START + CTILES * e + i + 1)
                    nc.vector.tensor_tensor(eo[:, par, i, :], down[0:CT, i % 2, 0:C], bias, ALU.add).then_inc(eo_ready, 1)

            copy_x(0, 0)
            every(dve, body)

        @block.gpsimd
        def _(pool):
            def body(e, par, m, last):
                rows = e * CAP if isinstance(e, int) else pool.snap(e * CAP)
                pool.wait_ge(eo_ready, START + CTILES * (e + 1))
                pool.dma_start(g["eo"][bass.ds(rows, CAP), :].rearrange("(i p) c -> p i c", p=CT),
                               eo[:, par, :, :]).then_inc(stored[par], 16)

            scatter(nc, pool, g, TOPK[1], sent)
            every(pool, body)
            for par in range(2):
                pool.wait_ge(stored[par], 16 * (NE // 2))


def phase_output(nc, a, g):
    with ExitStack() as ctx:
        sb, ps, sem = memory(nc, ctx, "output", g["used"])
        yc = sb("yc", [P, B * 2, HW])
        tp = ps("tp", [P, 4, BANK])
        turned, copied, stored = sem("turned"), sem("copied"), sem("stored")
        tiles = combined_tiles(nc, a, g, ctx, 1)
        block = ctx.enter_context(nc.Block())

        @block.gpsimd
        def _(pool):
            for t in range(NT):
                tiles["gpsimd_tile"](pool, t)

        @block.vector
        def _(dve):
            for t in range(NT):
                tiles["vector"](dve, t)

        @block.tensor
        def _(pe):
            for t in range(NT):
                pe.wait_ge(tiles["ready"], t + 1)
                if t >= 4:
                    pe.wait_ge(copied, t - 3)
                for k in range(2):
                    mm = nc.tensor.transpose(tp[:, t % 4, k * TT:(k + 1) * TT], g["T"][:, t, k * P:(k + 1) * P],
                                             g["ident"][0:TT, 0:TT])
                mm.then_inc(turned, 1)

        @block.scalar
        def _(act):
            for t in range(NT):
                b, j = divmod(t, TPB)
                act.wait_ge(turned, t + 1)
                nc.scalar.activation(yc[:, 2 * b:2 * b + 2, j * TT:(j + 1) * TT],
                                     tp[:, t % 4, 0:2 * TT].rearrange("p (k n) -> p k n", k=2), ACT.Copy).then_inc(copied, 1)

        @block.sync
        def _(sp):
            for b in range(B):
                sp.wait_ge(copied, TPB * (b + 1))
                sp.dma_start(a["out"][b].rearrange("(k p) h w -> p k (h w)", p=P),
                             yc[:, 2 * b:2 * b + 2, :]).then_inc(stored, 16)
            sp.wait_ge(stored, 16 * B)


def build(nc, a):
    with ExitStack() as ctx:
        sb, ps, sem = memory(nc, ctx, "all", [])
        g = {"used": [], "T": sb("T", [TT, NT, C]), "ident": sb("ident", [P, P]), "fold": sb("fold", [P, DG]),
             "sel": sb("sel", [P, NG, P]), "mamba": []}
        for l in range(2):
            g["mamba"].append({n: sb(f"m{l}_{n}", s) for n, s in (
                ("wu", [P, 2, DI]), ("wz", [P, DI]), ("wdt", [P, DI]), ("wbc", [P, 2 * DS]),
                ("wout", [P, DM]), ("vec", [P, 3]), ("diag", [P, DI]), ("acol", [P, ITEMS]))})
        g["seq"] = nc.dram_tensor("seq_scratch", (NCH + 3, DM, CW), F32, kind="Internal").ap()
        g["dt_rows"] = nc.dram_tensor("dt_rows", (2 * P, TC), F32, kind="Internal").ap()
        g["bc_rows"] = nc.dram_tensor("bc_rows", (2, 2 * DS, TC), F32, kind="Internal").ap()
        g["xs"] = nc.dram_tensor("slot_rows", (SLOTS0, C), F32, kind="Internal").ap()
        g["eo"] = nc.dram_tensor("expert_rows", (SLOTS0, C), F32, kind="Internal").ap()
        g["slot"] = sb("slot", [TT, 2, NT], I32)
        g["share"] = sb("share", [TT, 2, NT])
        g["mv"], g["rstd"] = sb("mv", [TT, NT, 2]), sb("rstd", [TT, NT])
        g["owner"] = sb("owner", [1, STILES + RTILES], I32)
        for l in range(2):
            phase_sequence(nc, a, g, l)
            phase_mamba(nc, a, g, l)
            with ExitStack() as ffn:
                weights, phase_experts = ((weights0, phase_experts0), (weights1, phase_experts1))[l]
                g["xn"] = ffn.enter_context(nc.sbuf_tensor(f"xn{l}", [TT, NT, C], F32))
                w, prefetch = weights(nc, a, g, ffn)
                phase_route(nc, a, g, l, prefetch)
                phase_experts(nc, a, g, w)
            if l == 0:
                nc.clear_and_free_semaphores(g["used"])
                g["used"].clear()
                nc.all_engine_barrier()
        phase_output(nc, a, g)


def layout(inputs):
    import numpy as np
    i = {n: np.asarray(v) for n, v in inputs.items()}
    out = {"x": i["x"]}
    for l in range(2):
        c = lambda n: i[f"L{l}_conv_{n}"]
        out[f"L{l}_winT"] = c("in_proj_w").T
        out[f"L{l}_cwT"] = c("conv_w").T
        out[f"L{l}_alog"] = c("A_log").reshape(NG, DG, NM, NS).transpose(3, 1, 0, 2).reshape(P, ITEMS)
        out[f"L{l}_xpw"] = c("x_proj_w")
        out[f"L{l}_xpT"] = c("x_proj_w").T
        out[f"L{l}_dtwT"] = c("dt_proj_w").T
        out[f"L{l}_woT"] = c("out_proj_w").T
        out[f"L{l}_vec"] = np.stack([c("conv_b"), c("dt_proj_b"), c("D")], axis=1)
        out[f"L{l}_token"] = c("global_token").reshape(DM, 1)
        out[f"L{l}_wrT"] = i[f"L{l}_ffn_router_w"].T
    for short, name in (("wg", "w_gate"), ("wu", "w_up"), ("wd", "w_down"), ("sg", "sg"), ("su", "su"), ("sd", "sd")):
        out[f"L0_{short}"] = i[f"L0_ffn_{name}"]
    out["L1_w1"], out["L1_w2"], out["L1_b2"] = i["L1_ffn_w1"], i["L1_ffn_w2"], i["L1_ffn_b2"]
    out["L1_b1"] = i["L1_ffn_b1"].reshape(NE, FC1, P).transpose(2, 0, 1)
    return {n: np.ascontiguousarray(v) for n, v in out.items()}


def kernel(**inputs):
    import concourse.bacc as bacc
    from concourse.bass_utils import run_bass_kernel_spmd

    nc = bacc.Bacc("TRN2", target_bir_lowering=False, num_devices=1)
    arrays = {f"in_{n}_dram": v for n, v in layout(inputs).items()}
    a = {n[3:-5]: nc.dram_tensor(n, v.shape, mybir.dt.from_np(v.dtype), kind="ExternalInput").ap()
         for n, v in arrays.items()}
    a["out"] = nc.dram_tensor("out_0_dram", (B, C, H, W), F32, kind="ExternalOutput").ap()
    build(nc, a)
    r = run_bass_kernel_spmd(nc, [arrays], core_ids=[0])
    return r.results[0]["out_0_dram"]
```
